# Optimizing a Trainium2 kernel written in Bass

```python
import numpy as np
import jax
import jax.numpy as jnp

def _softmax(x, axis=-1):
    return jax.nn.softmax(x, axis=axis)

def _gelu(x):
    return jax.nn.gelu(x, approximate=True)

def _silu(x):
    return jax.nn.silu(x)

def _sigmoid(x):
    return jax.nn.sigmoid(x)

def _layernorm(x, axis=-1, eps=1e-05):
    m = jnp.mean(x, axis=axis, keepdims=True)
    v = jnp.var(x, axis=axis, keepdims=True)
    return (x - m) / jnp.sqrt(v + eps)

def _scatter_add(tgt, idx, src, axis=0):
    return tgt.at[idx].add(src)

def _segment_sum(src, seg, n):
    return jax.ops.segment_sum(src, seg, n)
kernel_name = 'mk_recurrent_d2_jaxref_r8_273d60'

def setup_inputs(seed: int=0):
    np.random.seed(seed)
    _w = jnp.asarray

    def _L0_attn_setup():
        import jax, jax.numpy as jnp
        import numpy as np
        NUM_HEADS = 16
        HEAD_DIM = 64
        D_MODEL = 128
        B, L = (8, 512)

        def _relative_position_encoding(seq_len, dim):
            positions = jnp.arange(seq_len, dtype=jnp.float32)[:, None]
            div_term = jnp.exp(jnp.arange(0, dim, 2, dtype=jnp.float32) * -(np.log(10000.0) / dim))
            ang = positions * div_term
            pe = jnp.zeros((seq_len, dim), dtype=jnp.float32)
            pe = pe.at[:, 0::2].set(jnp.sin(ang))
            pe = pe.at[:, 1::2].set(jnp.cos(ang))
            return pe
        key = jax.random.key(seed)
        k1, k2, k3 = jax.random.split(key, 3)
        x = jax.random.normal(k1, (B, L, D_MODEL), dtype=jnp.float32)
        w_qkv = jax.random.normal(k2, (D_MODEL, 3 * NUM_HEADS * HEAD_DIM), dtype=jnp.float32) * (1.0 / np.sqrt(D_MODEL))
        b_qkv = jnp.zeros((3 * NUM_HEADS * HEAD_DIM,), dtype=jnp.float32)
        w_out = jax.random.normal(k3, (NUM_HEADS * HEAD_DIM, D_MODEL), dtype=jnp.float32) * (1.0 / np.sqrt(NUM_HEADS * HEAD_DIM))
        b_out = jnp.zeros((D_MODEL,), dtype=jnp.float32)
        return {'x': x, 'w_qkv': w_qkv, 'b_qkv': b_qkv, 'w_out': w_out, 'b_out': b_out}
    _L0_attn_in = _L0_attn_setup()

    def _L0_ffn_setup():
        import jax, jax.numpy as jnp
        import numpy as np
        B, S, H, I, E, TOPK, KS = (4, 512, 128, 64, 16, 2, 3)
        key = jax.random.key(seed)
        ks = jax.random.split(key, 9)
        sc = 0.02
        return {'hidden_states': jax.random.normal(ks[0], (B, S, H), dtype=jnp.float32), 'router_w': jax.random.normal(ks[1], (H, E), dtype=jnp.float32) * sc, 'router_bias': jnp.zeros((E,), dtype=jnp.float32), 'expert_gate_w': jax.random.normal(ks[2], (E - 1, H, I), dtype=jnp.float32) * sc, 'expert_up_w': jax.random.normal(ks[3], (E - 1, H, I), dtype=jnp.float32) * sc, 'expert_down_w': jax.random.normal(ks[4], (E - 1, I, H), dtype=jnp.float32) * sc, 'conv_w': jax.random.normal(ks[5], (I, H, KS), dtype=jnp.float32) * sc, 'shared_up_w': jax.random.normal(ks[6], (H, I), dtype=jnp.float32) * sc, 'shared_down_w': jax.random.normal(ks[7], (I, H), dtype=jnp.float32) * sc}
    _L0_ffn_in = _L0_ffn_setup()

    def _L1_attn_setup():
        import jax, jax.numpy as jnp
        import numpy as np
        DIM = 128
        HEADS = 16
        DIM_HEAD = 64
        DIM_INNER = HEADS * DIM_HEAD

        def rms_norm(x, gamma):
            eps = 1e-12
            norm = jnp.maximum(jnp.linalg.norm(x, axis=-1, keepdims=True), eps)
            return x / norm * x.shape[-1] ** 0.5 * (gamma + 1.0)
        key = jax.random.key(seed)
        k1, k2, k3 = jax.random.split(key, 3)
        x = jax.random.normal(k1, (2, 256, DIM), dtype=jnp.float32)
        gamma = jnp.zeros((DIM,), dtype=jnp.float32)
        w_qkv = jax.random.normal(k2, (DIM, DIM_INNER * 3), dtype=jnp.float32) * DIM ** (-0.5)
        w_out = jax.random.normal(k3, (DIM_INNER, DIM), dtype=jnp.float32) * DIM_INNER ** (-0.5)
        return {'x': x, 'gamma': gamma, 'w_qkv': w_qkv, 'w_out': w_out}
    _L1_attn_in = _L1_attn_setup()

    def _L1_ffn_setup():
        import jax, jax.numpy as jnp
        import numpy as np
        D_IN, D_HID = (128, 512)

        def _ternary(key, shape):
            return jax.random.randint(key, shape, -1, 2).astype(jnp.float32)

        def _tlin(x, w, s):
            return jnp.einsum('bsi,oi->bso', x, w) * s
        key = jax.random.key(seed)
        ks = jax.random.split(key, 12)
        inv = lambda fan: 1.0 / np.sqrt(fan).astype(np.float32)
        return {'x': jax.random.normal(ks[0], (4, 256, D_IN), dtype=jnp.float32), 'w1_w': _ternary(ks[1], (D_HID, D_IN)), 'w1_s': jax.random.uniform(ks[2], (D_HID,), dtype=jnp.float32) * inv(D_IN), 'w2_w': _ternary(ks[3], (D_HID, D_IN)), 'w2_s': jax.random.uniform(ks[4], (D_HID,), dtype=jnp.float32) * inv(D_IN), 'h1_w': _ternary(ks[5], (D_HID, D_HID)), 'h1_s': jax.random.uniform(ks[6], (D_HID,), dtype=jnp.float32) * inv(D_HID), 'h2_w': _ternary(ks[7], (D_HID, D_HID)), 'h2_s': jax.random.uniform(ks[8], (D_HID,), dtype=jnp.float32) * inv(D_HID), 'w3_w': _ternary(ks[9], (D_IN, D_HID)), 'w3_s': jax.random.uniform(ks[10], (D_IN,), dtype=jnp.float32) * inv(D_HID)}
    _L1_ffn_in = _L1_ffn_setup()
    _d = {'L0_attn_x': _L0_attn_in['x'], 'L0_attn_w_qkv': _L0_attn_in['w_qkv'], 'L0_attn_b_qkv': _L0_attn_in['b_qkv'], 'L0_attn_w_out': _L0_attn_in['w_out'], 'L0_attn_b_out': _L0_attn_in['b_out'], 'L0_ffn_router_w': _L0_ffn_in['router_w'], 'L0_ffn_router_bias': _L0_ffn_in['router_bias'], 'L0_ffn_expert_gate_w': _L0_ffn_in['expert_gate_w'], 'L0_ffn_expert_up_w': _L0_ffn_in['expert_up_w'], 'L0_ffn_expert_down_w': _L0_ffn_in['expert_down_w'], 'L0_ffn_conv_w': _L0_ffn_in['conv_w'], 'L0_ffn_shared_up_w': _L0_ffn_in['shared_up_w'], 'L0_ffn_shared_down_w': _L0_ffn_in['shared_down_w'], 'L1_attn_gamma': _L1_attn_in['gamma'], 'L1_attn_w_qkv': _L1_attn_in['w_qkv'], 'L1_attn_w_out': _L1_attn_in['w_out'], 'L1_ffn_w1_w': _L1_ffn_in['w1_w'], 'L1_ffn_w1_s': _L1_ffn_in['w1_s'], 'L1_ffn_w2_w': _L1_ffn_in['w2_w'], 'L1_ffn_w2_s': _L1_ffn_in['w2_s'], 'L1_ffn_h1_w': _L1_ffn_in['h1_w'], 'L1_ffn_h1_s': _L1_ffn_in['h1_s'], 'L1_ffn_h2_w': _L1_ffn_in['h2_w'], 'L1_ffn_h2_s': _L1_ffn_in['h2_s'], 'L1_ffn_w3_w': _L1_ffn_in['w3_w'], 'L1_ffn_w3_s': _L1_ffn_in['w3_s']}
    _x0 = _d['L0_attn_x']
    _d['L0_attn_x'] = jax.random.normal(jax.random.fold_in(jax.random.key(seed), 1), (2, 1024, 128), dtype=_x0.dtype)
    del _x0
    return _d

def reference(L0_attn_x, L0_attn_w_qkv, L0_attn_b_qkv, L0_attn_w_out, L0_attn_b_out, L0_ffn_router_w, L0_ffn_router_bias, L0_ffn_expert_gate_w, L0_ffn_expert_up_w, L0_ffn_expert_down_w, L0_ffn_conv_w, L0_ffn_shared_up_w, L0_ffn_shared_down_w, L1_attn_gamma, L1_attn_w_qkv, L1_attn_w_out, L1_ffn_w1_w, L1_ffn_w1_s, L1_ffn_w2_w, L1_ffn_w2_s, L1_ffn_h1_w, L1_ffn_h1_s, L1_ffn_h2_w, L1_ffn_h2_s, L1_ffn_w3_w, L1_ffn_w3_s):

    def _L0_attn_ref(x, w_qkv, b_qkv, w_out, b_out):
        import jax, jax.numpy as jnp
        import numpy as np
        NUM_HEADS = 16
        HEAD_DIM = 64
        D_MODEL = 128
        B, L = (8, 512)

        def _relative_position_encoding(seq_len, dim):
            positions = jnp.arange(seq_len, dtype=jnp.float32)[:, None]
            div_term = jnp.exp(jnp.arange(0, dim, 2, dtype=jnp.float32) * -(np.log(10000.0) / dim))
            ang = positions * div_term
            pe = jnp.zeros((seq_len, dim), dtype=jnp.float32)
            pe = pe.at[:, 0::2].set(jnp.sin(ang))
            pe = pe.at[:, 1::2].set(jnp.cos(ang))
            return pe
        Bq, Lq, _ = x.shape
        qkv = x @ w_qkv + b_qkv
        qkv = qkv.reshape(Bq, Lq, NUM_HEADS, 3 * HEAD_DIM)
        q, k, v = jnp.split(qkv, 3, axis=-1)
        pos_enc = _relative_position_encoding(Lq, HEAD_DIM)
        k = k + pos_enc[None, :, None, :]
        scale = jnp.sqrt(jnp.float32(HEAD_DIM))
        attn = jnp.einsum('blhd,bl gd->blhg'.replace(' ', ''), q, k) / scale
        attn = jax.nn.softmax(attn, axis=-1)
        out = jnp.einsum('blhg,blgd->blhd', attn, v)
        out = out.reshape(Bq, Lq, NUM_HEADS * HEAD_DIM)
        return out @ w_out + b_out

    def _L0_ffn_ref(hidden_states, router_w, router_bias, expert_gate_w, expert_up_w, expert_down_w, conv_w, shared_up_w, shared_down_w):
        import jax, jax.numpy as jnp
        import numpy as np
        B, S, H, I, E, TOPK, KS = (4, 512, 128, 64, 16, 2, 3)
        b, s, h = hidden_states.shape
        flat = hidden_states.reshape(b * s, h)
        logits = (flat @ router_w).astype(jnp.float32) + router_bias
        probs = jax.nn.softmax(logits, axis=-1)
        top_w, top_i = jax.lax.top_k(probs, TOPK)
        norm_w = top_w / (jnp.sum(top_w, axis=-1, keepdims=True) + 1e-06)
        norm_w = norm_w.astype(hidden_states.dtype)
        combine = jnp.sum(jax.nn.one_hot(top_i, E, dtype=norm_w.dtype) * norm_w[..., None], axis=1)
        routed = combine[:, E - 1:E] * flat
        for e in range(E - 1):
            y = jax.nn.silu(flat @ expert_gate_w[e]) * (flat @ expert_up_w[e]) @ expert_down_w[e]
            routed = routed + combine[:, e:e + 1] * y
        routed = routed.reshape(b, s, h)
        x_ncw = jnp.transpose(hidden_states, (0, 2, 1))
        gate = jax.lax.conv_general_dilated(x_ncw, conv_w, window_strides=(1,), padding=[(KS - 1, 0)], dimension_numbers=('NCW', 'OIW', 'NCW'))
        gate = jnp.transpose(gate, (0, 2, 1))
        shared = jax.nn.silu(gate) * (hidden_states @ shared_up_w) @ shared_down_w
        return shared + routed

    def _L1_attn_ref(x, gamma, w_qkv, w_out):
        import jax, jax.numpy as jnp
        import numpy as np
        DIM = 128
        HEADS = 16
        DIM_HEAD = 64
        DIM_INNER = HEADS * DIM_HEAD

        def rms_norm(x, gamma):
            eps = 1e-12
            norm = jnp.maximum(jnp.linalg.norm(x, axis=-1, keepdims=True), eps)
            return x / norm * x.shape[-1] ** 0.5 * (gamma + 1.0)
        b, n, _ = x.shape
        scale = DIM_HEAD ** (-0.5)
        xn = rms_norm(x, gamma)
        qkv = xn @ w_qkv
        qkv = qkv.reshape(b, n, 3, HEADS, DIM_HEAD)
        qkv = jnp.transpose(qkv, (2, 0, 3, 1, 4))
        q, k, v = (qkv[0], qkv[1], qkv[2])
        q = q * scale
        sim = jnp.einsum('bhid,bhjd->bhij', q, k)
        attn = jax.nn.softmax(sim, axis=-1)
        out = jnp.einsum('bhij,bhjd->bhid', attn, v)
        out = jnp.transpose(out, (0, 2, 1, 3)).reshape(b, n, DIM_INNER)
        return out @ w_out

    def _L1_ffn_ref(x, w1_w, w1_s, w2_w, w2_s, h1_w, h1_s, h2_w, h2_s, w3_w, w3_s):
        import jax, jax.numpy as jnp
        import numpy as np
        D_IN, D_HID = (128, 512)

        def _ternary(key, shape):
            return jax.random.randint(key, shape, -1, 2).astype(jnp.float32)

        def _tlin(x, w, s):
            return jnp.einsum('bsi,oi->bso', x, w) * s
        h = jax.nn.silu(_tlin(x, w1_w, w1_s)) * _tlin(x, w2_w, w2_s)
        h = jax.nn.gelu(_tlin(h, h1_w, h1_s), approximate=False)
        h = jax.nn.gelu(_tlin(h, h2_w, h2_s), approximate=False)
        return _tlin(h, w3_w, w3_s)
    x = L0_attn_x
    xn = _layernorm(x, axis=-1)
    s = _L0_attn_ref(xn, L0_attn_w_qkv, L0_attn_b_qkv, L0_attn_w_out, L0_attn_b_out)
    g = _silu(_L0_ffn_ref(xn, L0_ffn_router_w, L0_ffn_router_bias, L0_ffn_expert_gate_w, L0_ffn_expert_up_w, L0_ffn_expert_down_w, L0_ffn_conv_w, L0_ffn_shared_up_w, L0_ffn_shared_down_w))
    x = x + s * g
    xn = _layernorm(x, axis=-1)
    s = _L1_attn_ref(xn, L1_attn_gamma, L1_attn_w_qkv, L1_attn_w_out)
    g = _silu(_L1_ffn_ref(xn, L1_ffn_w1_w, L1_ffn_w1_s, L1_ffn_w2_w, L1_ffn_w2_s, L1_ffn_h1_w, L1_ffn_h1_s, L1_ffn_h2_w, L1_ffn_h2_s, L1_ffn_w3_w, L1_ffn_w3_s))
    x = x + s * g
    return x

_drawn_inputs = setup_inputs


def setup_inputs(seed=0):
    import zlib

    import numpy as np

    out = dict(_drawn_inputs(seed))
    spreads = {'L0_attn_b_qkv': (0.0, 0.1),
     'L0_attn_b_out': (0.0, 0.1),
     'L0_ffn_router_bias': (0.0, 0.1),
     'L1_attn_gamma': (0.0, 0.1)}
    factors = {}
    for name, (base, spread) in spreads.items():
        noise = np.random.default_rng([zlib.crc32(name.encode()), seed]).standard_normal(out[name].shape)
        drawn = base * np.exp(spread * noise) if base else spread * noise
        out[name] = jnp.asarray(drawn.astype(out[name].dtype))
    for name, factor in factors.items():
        out[name] = (out[name] * factor).astype(out[name].dtype)
    return out
```

```python
from contextlib import ExitStack

import concourse.bass as bass
from concourse import mybir

F32 = mybir.dt.float32
F32R = mybir.dt.float32r
ACT = mybir.ActivationFunctionType
ALU = mybir.AluOpType
AX_X = mybir.AxisListType.X

P = 128
SEQS, LEN = 2, 1024
TOKENS = SEQS * LEN
CH = 512
CHUNKS = TOKENS // CH
HALVES = LEN // CH
HEADS, HD = 16, 64
PAIRS = HEADS // 2
STEPS = SEQS * PAIRS
KT = LEN // P
TT = CH // P
EXPERTS = 16
EPAIRS = EXPERTS // 2
HALO = 2
HID = 512
HT = HID // P
LOWEST = -3.0e38
LN_EPS = 1e-5
RMS_EPS = 1e-12
SCALE = HD ** -0.5
CW = 128
LO = 32

W_QK = 4 * P
W_V = W_QK + P


class Counter:

    def __init__(self, sem, per, ahead=0):
        self.sem, self.per, self.ahead = sem, per, ahead

    def wait(self, eng, period, n):
        value = period * self.per + n + self.ahead
        if not isinstance(value, int) or value > self.ahead:
            eng.wait_ge(self.sem, value)


class Steps:

    ENGINES = ("tensor", "vector", "scalar", "gpsimd", "sync")

    def __init__(self, nc, name, ctx, periods=CHUNKS):
        self.nc, self.list, self.at, self.periods = nc, [], {}, periods
        self.count = {e: 0 for e in self.ENGINES}
        self.sem = {e: ctx.enter_context(nc.semaphore(f"{name}_{e}")) for e in self.ENGINES}

    def add(self, name, engine, emit, *after):
        assert name not in self.at
        self.count[engine] += 16 if engine == "sync" else 1
        self.at[name] = (engine, self.count[engine])
        self.list.append((name, engine, emit, after))

    def run(self):
        with self.nc.Block() as block:
            programs = {"tensor": block.tensor, "vector": block.vector, "scalar": block.scalar,
                        "gpsimd": block.gpsimd, "sync": block.sync}
            for engine, program in programs.items():
                if self.count[engine]:
                    program(lambda eng, engine=engine: self._run(eng, engine))

    def _run(self, eng, engine):
        eng.sem_inc(self.sem[engine], self.count[engine])
        if self.periods == 1:
            self._period(eng, engine, 0)
        else:
            with eng.Fori(0, self.periods) as chunk:
                self._period(eng, engine, chunk)
        if engine == "sync":
            eng.wait_ge(self.sem[engine], (self.periods + 1) * self.count[engine])

    def _period(self, eng, engine, chunk):
        for name, mine, emit, after in self.list:
            if mine != engine:
                continue
            latest = {}
            for what in after:
                of, n = self.at[what.lstrip("-")]
                latest[of] = max(latest.get(of, (0, 0)), (0 if what.startswith("-") else 1, n))
            for of, (this, n) in latest.items():
                eng.wait_ge(self.sem[of], (chunk + this) * self.count[of] + n)
            emit(eng, chunk).then_inc(self.sem[engine], 16 if engine == "sync" else 1)


def attention(nc, c, w_pair, w_out):
    with ExitStack() as ctx:
        def sb(name, shape, dt=F32):
            return ctx.enter_context(nc.sbuf_tensor(name, shape, dt))

        def ps(name, shape):
            return ctx.enter_context(nc.psum_tensor(name, shape, F32))

        def counter(name, per, ahead=0):
            return Counter(ctx.enter_context(nc.semaphore(name)), per, ahead)

        x_cur = sb("x_cur", [P, 2, LEN])
        w_cur = sb("w_cur", [P, 2, W_V])
        wo_cur = sb("wo_cur", [P, 2, P])
        q_a = sb("q_a", [P, 2, 2, LEN], F32R)
        k_a = sb("k_a", [P, 2, 2, LEN], F32R)
        q_b = sb("q_b", [P, 2, 2, LEN], F32R)
        k_b = sb("k_b", [P, 2, 2, LEN], F32R)
        v_cur = sb("v_cur", [P, 2, KT, P])
        RING = 8
        prob = sb("prob", [P, RING, CH])
        acc = sb("acc", [P, HALVES, 2, CH])
        mx_part = sb("mx_part", [P, 2, KT, 2])
        mx_row = sb("mx_row", [P, 2, KT])
        rden = sb("rden", [P, HALVES, CH])
        o_n = sb("o_n", [P, HALVES, CH])

        st_ps = ps("st_ps", [P, 2, CH])
        mx_ps = ps("mx_ps", [P, 2, CH])
        o_ps = ps("o_ps", [P, HALVES, CH])
        pj_ps = ps("pj_ps", [P, 2, CH])

        s_init = ctx.enter_context(nc.semaphore("s_init"))
        s_w = [counter(f"s_w{par}", 32) for par in range(2)]
        s_wo = [counter(f"s_wo{par}", 16) for par in range(2)]
        s_prep = counter("s_prep", 12)
        s_hi = counter("s_hi", 12)
        s_lo = counter("s_lo", 10)
        s_v = counter("s_v", 2)
        s_mx = counter("s_mx", 32)
        s_mxr = counter("s_mxr", 32)
        s_row = counter("s_row", 2)
        s_st = counter("s_st", 32)
        s_exp = counter("s_exp", 32)
        s_pv = counter("s_pv", 16)
        s_acc = counter("s_acc", 28)
        s_fin = counter("s_fin", 4, 4)
        s_den = counter("s_den", 2, 2)
        s_out = counter("s_out", 2, 2)
        s_rcp = counter("s_rcp", 8)
        s_on = counter("s_on", 2, 2)

        slots = [[] for _ in range(48)]
        for n, (t, h) in enumerate([(t, h) for t in (0, 2, 1, 3) for h in range(HALVES)]):
            slots[n].append(("qk", t, h))
        for half, at in ((1, 3), (0, 27)):
            slots[at].append(("den", half))
            for n in range(4):
                slots[at + 1 + n].append(("rcp", half, n))
            slots[at + 5].append(("norm", half))
            slots[at + 8].append(("out", half))
        slots[8].append(("v", 0))
        slots[10].append(("v", 1))
        for n in range(32):
            slots[9 + n].append(("tile", n))
        slots[29].append(("tr", 0))
        slots[43].append(("tr", 1))
        UNITS = ("qk", "v", "tr", "den", "out")
        PREPARE = ("qk", "v", "tr", "tile")
        order = [u for slot in slots for u in slot if u[0] in UNITS]
        prepare = [u for u in order if u[0] in PREPARE]
        lows = [u for u in prepare if u[0] in ("qk", "tr")]
        his = {}
        for u in prepare:
            if u[0] == "qk":
                his[u] = (his[max(his, key=his.get)] if his else 0) + (2 if u[1] < 2 else 1)
        assert len(order) % 2 == 0 and len(prepare) == 12 and len(lows) == 10
        def written(u, m):
            if u in prepare:
                return s_prep, m + 1, prepare.index(u) + 1
            return s_fin, m - u[1], 2 * u[1] + (u[0] == "out") + 1

        def read(u, m):
            if u[0] == "v":
                return s_v, m + 1, u[1] + 1
            if u in prepare:
                return s_lo, m + 1, lows.index(u) + 1
            return (s_den if u[0] == "den" else s_out), m - u[1], u[1] + 1

        def exists(u, m):
            if not isinstance(m, int):
                return True
            if u[0] in PREPARE:
                return -1 <= m < STEPS - 1
            return 0 <= m - u[1] < STEPS

        def bank(u):
            return order.index(u) % 2

        def wait(eng, event):
            event[0].wait(eng, event[1], event[2])

        def extras(slot, m):
            return [u for u in slots[slot] if exists(u, m)]

        def bank_free(eng, u, m):
            n, period = order.index(u) - 2, m
            for _ in range(2 * len(order)):
                if n < 0:
                    n, period = n + len(order), period - 1
                if exists(order[n], period):
                    return wait(eng, read(order[n], period))
                n -= 2

        def needed_adds(s):
            return 14 * (s // KT) + 2 * max(1, s % KT)

        def parts(m):
            if not isinstance(m, int):
                return True, True, True
            return 0 <= m < STEPS, m < STEPS - 1, m > 0

        def periods(eng, body):
            body(eng, -1, 1)
            body(eng, 0, 0)
            with eng.Fori(0, STEPS // 2 - 1) as i:
                body(eng, 2 * i + 1, 1)
                body(eng, 2 * i + 2, 0)
            body(eng, STEPS - 1, 1)
            body(eng, STEPS, 0)

        def pe(eng, m, par):
            own, prep, fin = parts(m)
            nxt = 1 - par

            def pv(step, period, par_v):
                half, j = step // KT, step % KT
                s_exp.wait(eng, period, 2 * step + 2)
                if j == 0:
                    s_on.wait(eng, period - 1, half + 1)
                for h in range(2):
                    mm = eng.matmul(o_ps[64 * h:64 * h + 64, half, :], v_cur[:, par_v, j, HD * h:HD * h + HD],
                                    prob[:, (2 * step + h) % RING, :], start=(j == 0), stop=(j == KT - 1),
                                    skip_group_check=True)
                mm.then_inc(s_pv.sem, 1)

            def unit(u):
                if u == prepare[0]:
                    s_w[nxt].wait(eng, (m + 1) // 2, 32)
                bank_free(eng, u, m)
                out = pj_ps[:, bank(u), :]
                if u[0] == "qk":
                    _, t, half = u
                    tok = slice(half * CH, half * CH + CH)
                    mm = eng.matmul(out, w_cur[:, nxt, t * P:t * P + P], x_cur[:, nxt, tok],
                                    start=True, stop=True)
                elif u[0] == "v":
                    for i in range(TT):
                        j = TT * u[1] + i
                        mm = eng.matmul(out[:, i * P:i * P + P], x_cur[:, nxt, j * P:j * P + P],
                                        w_cur[:, nxt, W_QK:W_V], start=True, stop=True)
                elif u[0] == "tr":
                    s_row.wait(eng, m + 1, u[1] + 1)
                    mm = eng.transpose(out[0:KT, 0:P], mx_row[:, u[1], :], c.ident[:, :])
                elif u[0] == "den":
                    s_acc.wait(eng, m - u[1], 14 * (u[1] + 1))
                    for h in range(2):
                        mm = eng.matmul(out[64 * h:64 * h + 64, :], c.ones[:, 0:64], acc[:, u[1], h, :],
                                        start=True, stop=True, skip_group_check=True)
                else:
                    q, par_q = m - u[1], par if u[1] == 0 else nxt
                    s_wo[par_q].wait(eng, q // 2, 16)
                    s_on.wait(eng, q, u[1] + 1)
                    mm = eng.matmul(out, wo_cur[:, par_q, :], o_n[:, u[1], :],
                                    start=True, stop=True)
                mm.then_inc(written(u, m)[0].sem, 1)

            def score_tile(n):
                h, i, keys = n // 16, n % 16 // 2, n % 2
                if n % 16 == 0:
                    wait(eng, read(("qk", 2 + h, 1), m))
                s_mxr.wait(eng, m + 1, n - 1)
                eng.matmul(mx_ps[:, n % 2, :], q_a[:, nxt, h, i * P:i * P + P],
                           k_a[:, nxt, h, keys * CH:keys * CH + CH], start=True, stop=True)\
                   .then_inc(s_mx.sem, 1)

            def beside(slot):
                for u in extras(slot, m):
                    if u[0] in UNITS:
                        unit(u)
                    elif u[0] == "tile":
                        score_tile(u[1])

            for s in range(16):
                half, j = s // KT, s % KT
                if own and s == 0:
                    s_lo.wait(eng, m, 10)
                    s_v.wait(eng, m, 2)
                for h in range(2):
                    if own:
                        s_exp.wait(eng, m, 2 * s + h - 1)
                        keys, tok = slice(j * P, j * P + P), slice(half * CH, half * CH + CH)
                        eng.matmul(st_ps[:, h, :], k_a[:, par, h, keys], q_a[:, par, h, tok],
                                   start=True, stop=False)
                        eng.matmul(st_ps[:, h, :], k_b[:, par, h, keys], q_b[:, par, h, tok],
                                   start=False, stop=True).then_inc(s_st.sem, 1)
                    beside(3 * s + h)
                if s == 0 and fin:
                    pv(15, m - 1, nxt)
                if s > 0 and own:
                    pv(s - 1, m, par)
                beside(3 * s + 2)

        def act(eng, m, par):
            own, prep, fin = parts(m)
            nxt = 1 - par
            for slot in range(48):
                s, h = slot // 3, slot % 3
                if own and h < 2:
                    s_st.wait(eng, m, 2 * s + h + 1)
                    s_pv.wait(eng, m, s - 3)
                    s_acc.wait(eng, *((m, needed_adds(s - 4)) if s >= 4 else (m - 1, needed_adds(s + 12))))
                    eng.activation(prob[:, (2 * s + h) % RING, :], st_ps[:, h, :], ACT.Exp, scale=SCALE)\
                       .then_inc(s_exp.sem, 1)
                for u in extras(slot, m):
                    if u[0] == "qk":
                        _, t, half = u
                        if u == prepare[0]:
                            s_st.wait(eng, m, 0)
                        wait(eng, written(u, m))
                        tok = slice(half * CH, half * CH + CH)
                        outs = [(q_a if t < 2 else k_a)[:, nxt, t % 2, tok]]
                        rows = [P]
                        if t < 2:
                            outs.append(q_b[0:HD, nxt, t % 2, tok])
                            rows.append(HD)
                        for o, r in zip(outs, rows):
                            src = pj_ps[0:r, bank(u), :]
                            eng.activation(o, src, ACT.Copy).then_inc(s_hi.sem, 1)
                    elif u[0] == "den":
                        wait(eng, written(u, m))
                        s_on.wait(eng, m - u[1] - 1, u[1] + 1)
                        eng.activation(rden[:, u[1], :], pj_ps[:, bank(u), :], ACT.Copy).then_inc(s_den.sem, 1)
                    elif u[0] == "v":
                        if u[1] == 0:
                            s_pv.wait(eng, m, 0)
                        wait(eng, written(u, m))
                        eng.activation(v_cur[:, nxt, TT * u[1]:TT * u[1] + TT, :],
                                       pj_ps[:, bank(u), :].rearrange("p (t n) -> p t n", t=TT), ACT.Copy)\
                           .then_inc(s_v.sem, 1)

        def dve(eng, m, par):
            own, prep, fin = parts(m)
            nxt = 1 - par
            for slot in range(48):
                for u in extras(slot, m):
                    if u[0] in UNITS:
                        src = pj_ps[:, bank(u), :]
                    if u[0] == "qk":
                        _, t, half = u
                        tok = slice(half * CH, half * CH + CH)
                        s_hi.wait(eng, m + 1, his[u])
                        r = slice(HD, P) if t < 2 else slice(0, HD)
                        hi = (q_a if t < 2 else k_a)[r, nxt, t % 2, tok]
                        out = (q_a if t < 2 else k_b)[r, nxt, t % 2, tok]
                        eng.tensor_tensor(out, src[r, :], hi.bitcast(F32), ALU.subtract).then_inc(s_lo.sem, 1)
                    elif u[0] == "tr":
                        wait(eng, written(u, m))
                        eng.tensor_tensor(
                            q_b[HD:HD + KT, nxt, u[1], :].rearrange("p (i n) -> p i n", i=KT),
                            src[0:KT, 0:P].unsqueeze(1).to_broadcast([KT, KT, P]),
                            c.diag[:, :].rearrange("p (i n) -> p i n", i=KT), ALU.mult).then_inc(s_lo.sem, 1)
                    elif u[0] == "rcp":
                        h, q = u[1], m - u[1]
                        s_den.wait(eng, q, h + 1)
                        part = rden[:, h, u[2] * P:u[2] * P + P]
                        eng.reciprocal(part, part).then_inc(s_rcp.sem, 1)
                    elif u[0] == "norm":
                        h, q = u[1], m - u[1]
                        s_rcp.wait(eng, q, 4 * (h + 1))
                        s_pv.wait(eng, q, KT * (h + 1))
                        s_fin.wait(eng, q - 1, 2 * h + 2)
                        eng.tensor_tensor(o_n[:, h, :], o_ps[:, h, :], rden[:, h, :], ALU.mult)\
                           .then_inc(s_on.sem, 1)
                    elif u[0] == "out":
                        h, q = u[1], m - u[1]
                        wait(eng, written(u, m))
                        s_out.wait(eng, q - 1, h + 1)
                        seq = q // PAIRS
                        y = c.y[:, bass.ds(seq * LEN + h * CH, CH)]
                        eng.tensor_tensor(y, src, y, ALU.add).then_inc(s_out.sem, 1)
                    elif u[0] == "tile":
                        n = u[1]
                        h, i, keys = n // 16, n % 16 // 2, n % 2
                        s_mx.wait(eng, m + 1, n + 1)
                        if n % 16 == 0:
                            s_row.wait(eng, m, h + 1)
                        eng.reduce_max(mx_part[:, h, i, keys:keys + 1], mx_ps[:, n % 2, :], AX_X)\
                           .then_inc(s_mxr.sem, 1)
                        if n % 16 == 15:
                            s_mxr.wait(eng, m + 1, n + 1)
                            s_prep.wait(eng, m, prepare.index(("tr", h)) + 1)
                            eng.reduce_max(mx_row[:, h, :], mx_part[:, h, :, :], AX_X).then_inc(s_row.sem, 1)

        def pool(eng, m, par):
            if not parts(m)[0]:
                return
            for s in range(16):
                half, j = s // KT, s % KT
                if j == 0:
                    continue
                for h in range(2):
                    s_exp.wait(eng, m, 2 * s + h + 1)
                    new, a = prob[:, (2 * s + h) % RING, :], acc[:, half, h, :]
                    if j == 1:
                        s_fin.wait(eng, m - 1, 2 * half + 1)
                        first = prob[:, (2 * s + h - 2) % RING, :]
                    else:
                        s_acc.wait(eng, m, 14 * half + 2 * (j - 1) + h - 1)
                        first = a
                    eng.tensor_tensor(a, first, new, ALU.add).then_inc(s_acc.sem, 1)

        def load(eng, p, par):
            pair, seq = p % PAIRS, p // PAIRS
            late = not isinstance(p, int)
            if late:
                s_prep.wait(eng, p - 2, prepare.index(("v", 1)) + 1)
            eng.dma_start(x_cur[:, par, :].rearrange("p (h n) -> p h n", h=HALVES), c.src(seq)).then_inc(s_w[par].sem, 16)
            eng.dma_start(w_cur[:, par, :], w_pair(pair)).then_inc(s_w[par].sem, 16)
            if late:
                s_fin.wait(eng, p - 2, 4)
            eng.dma_start(wo_cur[:, par, :], w_out(pair)).then_inc(s_wo[par].sem, 16)

        with nc.Block() as block:
            @block.vector
            def _(eng):
                eng.memset(q_b[HD:P, :, :, :].bitcast(F32), 0.0).then_inc(s_init, 1)
                eng.memset(k_b[HD:P, :, :, :].bitcast(F32), 0.0).then_inc(s_init, 1)
                eng.wait_ge(s_init, 2)
                eng.memset(k_b[HD:HD + KT, :, :, :].bitcast(F32), -1.0)

                for k in (s_on, s_out):
                    eng.sem_inc(k.sem, k.ahead)

            @block.tensor
            def _(eng):
                eng.sem_inc(s_fin.sem, s_fin.ahead)

            @block.scalar
            def _(eng):
                eng.sem_inc(s_den.sem, s_den.ahead)

            @block.gpsimd
            def _(eng):
                eng.memset(c.y[:, :], 0.0)

        with nc.Block() as block:
            @block.sync
            def _(eng):
                load(eng, 0, 0)
                load(eng, 1, 1)
                with eng.Fori(1, STEPS // 2) as i:
                    load(eng, 2 * i, 0)
                    load(eng, 2 * i + 1, 1)

            block.tensor(lambda eng: periods(eng, pe))
            block.scalar(lambda eng: periods(eng, act))
            block.vector(lambda eng: periods(eng, dve))
            block.gpsimd(lambda eng: periods(eng, pool))


def head_attention(nc, c, a, xn):
    BLK = 128
    TURNS = 8
    GROUPS = 4
    G = 8
    with ExitStack() as ctx:
        def sb(name, shape, dt=F32):
            return ctx.enter_context(nc.sbuf_tensor("ha_" + name, shape, dt))

        def ps(name, shape):
            return ctx.enter_context(nc.psum_tensor("ha_" + name, shape, F32))

        wq = sb("wq", [P, PAIRS, P])
        wkv = sb("wkv", [P, HEADS, P])
        wo = sb("wo", [P, PAIRS, P])
        bq, bkv = sb("bq", [P, PAIRS]), sb("bkv", [P, HEADS])
        pos = sb("pos", [P, LEN])
        mask = sb("mask", [P, P])
        q = [sb(f"q{i}", [P, BLK * HEADS]) for i in range(2)]
        kv = [sb(f"kv{i}", [P, BLK * HEADS]) for i in range(2)]
        masked = [sb(f"masked{i}", [P, GROUPS, P]) for i in range(2)]
        top = [sb(f"top{i}", [P, GROUPS]) for i in range(2)]
        shift = [sb(f"shift{i}", [P, GROUPS]) for i in range(2)]
        total = [sb(f"total{i}", [P, GROUPS]) for i in range(4)]
        rtotal = [sb(f"rtotal{i}", [P, GROUPS]) for i in range(4)]
        ex = [sb(f"ex{i}", [P, GROUPS, P]) for i in range(4)]
        prob = [sb(f"prob{i}", [P, GROUPS, P]) for i in range(4)]
        prob_t = [sb(f"prob_t{i}", [P, GROUPS, P]) for i in range(2)]
        v_t = [sb(f"v_t{i}", [P, GROUPS, HD]) for i in range(4)]
        o = [sb(f"o{i}", [P, PAIRS, BLK]) for i in range(2)]
        pj_ps = [ps(f"pj_ps{i}", [P, 4, BLK]) for i in range(2)]
        s_ps = [ps(f"s_ps{i}", [P, GROUPS, P]) for i in range(2)]
        v_ps, p_ps = ps("v_ps", [P, GROUPS, P]), ps("p_ps", [P, GROUPS, P])
        o_ps, y_ps = ps("o_ps", [P, GROUPS, G * PAIRS]), ps("y_ps", [P, BLK])
        s_l = ctx.enter_context(nc.semaphore("s_l0"))
        s_pad = ctx.enter_context(nc.semaphore("s_pad0"))

        with nc.Block() as block:
            @block.sync
            def _(eng):
                loads = [(wq[:, :, :], a["wq0"].rearrange("k (h n) -> k h n", n=P)),
                         (wkv[:, :, :], a["wkv0"].rearrange("k (h n) -> k h n", n=P)),
                         (wo[:, :, :], a["wo0"].rearrange("k (h n) -> k h n", n=P)),
                         (bq[:, :], a["bq0"]), (bkv[:, :], a["bkv0"]), (pos[:, :], a["pos"]),
                         (mask[:, :], a["mask"])]
                for to, of in loads:
                    eng.dma_start(to, of).then_inc(s_l, 16)
                eng.wait_ge(s_l, 16 * len(loads))

            @block.vector
            def _(eng):
                for i in range(2):
                    eng.memset(q[i][HD:P, :], 0.0)

        def project(st, tag, to, x_at, pos_at, free):
            q_out = q[to][0:HD, :].rearrange("r (t h) -> r h t", h=HEADS)
            kv_out = kv[to][:, :].rearrange("r (t h) -> r h t", h=HEADS)
            units = [("q", n) for n in range(2)] + [("kv", n) for n in range(4)]
            steps = []
            for n, (kind, i) in enumerate(units):
                b = n % 2
                w = wq if kind == "q" else wkv
                name = f"{tag}{kind}{i}"

                def products(e, k, w=w, i=i, b=b):
                    for j in range(4):
                        mm = e.matmul(pj_ps[b][:, j, :], w[:, 4 * i + j, :], x_at(k), start=True, stop=True)
                    return mm

                bank_of = f"{tag}{units[n - 2][0]}{units[n - 2][1]}out" if n >= 2 else free["bank"][b]
                steps.append((f"{name}mm", "tensor", products, bank_of))
                if kind == "q":
                    def even(e, k, i=i, b=b):
                        return e.tensor_tensor(q_out[:, 8 * i:8 * i + 8:2, :], pj_ps[b][0:HD, :, :],
                                               bq[0:HD, 4 * i:4 * i + 4].unsqueeze(2).to_broadcast([HD, 4, BLK]), ALU.add)

                    def odd(e, k, i=i, b=b):
                        return e.tensor_tensor(q_out[:, 8 * i + 1:8 * i + 8:2, :], pj_ps[b][HD:P, :, :],
                                               bq[HD:P, 4 * i:4 * i + 4].unsqueeze(2).to_broadcast([HD, 4, BLK]), ALU.add)

                    steps.append((f"{name}even", "vector", even, f"{name}mm", *free["q"]))
                    steps.append((f"{name}out", "vector", odd, f"{name}mm"))
                else:
                    def out(e, k, i=i, b=b):
                        for j in range(4):
                            h = 4 * i + j
                            d = e.scalar_tensor_tensor(out=kv_out[:, h, :], in0=pj_ps[b][:, j, :],
                                                       scalar=bkv[:, h:h + 1], in1=pos_at(k), op0=ALU.add, op1=ALU.add)
                        return d

                    steps.append((f"{name}out", "vector", out, f"{name}mm", *free["kv"]))
            groups, at = [], 0
            for kind, _ in units:
                n = 3 if kind == "q" else 2
                groups.append(steps[at:at + n])
                at += n
            return groups

        def tokens(k, off):
            b = (2 * k + off) % (TOKENS // BLK)
            flat = xn[:, :, :].rearrange("p c n -> p (c n)")
            return flat[:, bass.ds((b // TT) * (HALO + CH) + (b % TT) * BLK + HALO, BLK)]

        def codes(k, off):
            b = (2 * k + off) % (LEN // BLK)
            return pos[:, bass.ds(b * BLK, BLK)]

        st = Steps(nc, "pro0", ctx, 1)
        for group in project(st, "x", 0, lambda k: xn[:, 0, HALO:HALO + BLK], lambda k: pos[:, 0:BLK],
                             {"bank": ("-xkv2out", "-xkv3out"), "q": (), "kv": ()}):
            for step in group:
                st.add(*step)
        st.run()

        st = Steps(nc, "ha", ctx, TOKENS // (2 * BLK))

        def past(name, n, depth):
            return f"{name}{n - depth}" if n >= depth else f"-{name}{n - depth + TURNS}"

        def scores(n):
            f, t = n // 4, n % 4
            cut = lambda g: slice((t * GROUPS + g) * P, (t * GROUPS + g + 1) * P)

            def products(e, k):
                for g in range(GROUPS):
                    mm = e.matmul(s_ps[n % 2][:, g, :], q[f][:, cut(g)], kv[f][:, cut(g)], start=True, stop=True)
                return mm

            def turn_v(e, k):
                for g in range(GROUPS):
                    mm = e.transpose(v_ps[:, g, :], kv[f][:, cut(g)], c.ident[:, :])
                return mm

            def mask_max(e, k):
                e.sem_inc(s_pad, 1)
                for g in range(GROUPS):
                    d = e.tensor_tensor_reduce(masked[n % 2][:, g, :], s_ps[n % 2][:, g, :], mask[:, :], 1.0, LOWEST,
                                               ALU.add, ALU.max, top[n % 2][:, g:g + 1])
                return d

            def exps(e, k):
                for g in range(GROUPS):
                    d = e.activation(ex[n % 4][:, g, :], masked[n % 2][:, g, :], ACT.Exp, bias=shift[n % 2][:, g:g + 1],
                                     scale=SCALE, accum_out=total[n % 4][:, g:g + 1])
                return d

            ready = (f"bkv3out",) if f else ("-ckv3out",)
            st.add(f"s{n}", "tensor", products, past("mm", n, 2), *(ready if t == 0 else ()))
            st.add(f"tv{n}", "tensor", turn_v, past("vt", n, 1))
            st.add(f"mm{n}", "vector", mask_max, f"s{n}", past("ex", n, 2))
            st.add(f"shift{n}", "vector", lambda e, k: e.tensor_scalar(
                shift[n % 2][:, :], top[n % 2][:, :], -SCALE, None, ALU.mult), f"mm{n}")
            st.add(f"ex{n}", "scalar", exps, f"shift{n}", past("norm", n, 4), past("rt", n, 4))
            st.add(f"vt{n}", "scalar", lambda e, k: e.activation(
                v_t[n % 4][:, :, :], v_ps[:, :, HD:P], ACT.Copy), f"tv{n}", past("o", n, 4))
            st.add(f"rt{n}", "vector", lambda e, k: e.reciprocal(rtotal[n % 4][:, :], total[n % 4][:, :]),
                   f"ex{n}", past("norm", n, 4))
            st.add(f"norm{n}", "gpsimd", lambda e, k: e.tensor_tensor(
                prob[n % 4][:, :, :], ex[n % 4][:, :, :],
                rtotal[n % 4][:, :].unsqueeze(2).to_broadcast([P, GROUPS, P]), ALU.mult), f"rt{n}", past("tp", n, 4))

        def turned(n):
            def turn_p(e, k):
                for g in range(GROUPS):
                    mm = e.transpose(p_ps[:, g, :], prob[n % 4][:, g, :], c.ident[:, :])
                return mm

            st.add(f"tp{n}", "tensor", turn_p, f"norm{n}", past("pt", n, 1))
            st.add(f"pt{n}", "scalar", lambda e, k: e.activation(
                prob_t[n % 2][:, :, :], p_ps[:, :, :], ACT.Copy), f"tp{n}", past("o", n, 2))

        def outputs(n):
            f, t = n // 4, n % 4

            def products(e, k):
                for g in range(GROUPS):
                    for odd in range(2):
                        mm = e.matmul(o_ps[HD * odd:HD * odd + HD, g, :], v_t[n % 4][:, g, :],
                                      prob_t[n % 2][:, g, odd:P:2], start=True, stop=True, skip_group_check=True)
                return mm

            st.add(f"o{n}", "tensor", products, f"pt{n}", f"vt{n}", past("oc", n, 1))
            cut = slice(t * GROUPS * G, (t + 1) * GROUPS * G)
            st.add(f"oc{n}", "vector", lambda e, k: e.tensor_copy(
                o[f][:, :, cut].rearrange("r p t -> r t p"),
                o_ps[:, :, :].rearrange("r g (t p) -> r (g t) p", p=PAIRS)), f"o{n}", *((f"-y{f}",) if t == 0 else ()))

        def project_out(f):
            def products(e, k):
                for p in range(PAIRS):
                    mm = e.matmul(y_ps[:, :], wo[:, p, :], o[f][:, p, :], start=p == 0, stop=p == PAIRS - 1)
                return mm

            st.add(f"y{f}", "tensor", products, f"oc{4 * f + 3}", f"yc{f - 1}" if f else "-yc1")
            st.add(f"yc{f}", "scalar", lambda e, k: e.activation(
                c.y[:, bass.ds(k * (2 * BLK) + f * BLK, BLK)], y_ps[:, :], ACT.Copy), f"y{f}")

        nexts = [project(st, "b", 1, lambda k: tokens(k, 1), lambda k: codes(k, 1),
                         {"bank": ("-ckv2out", "-ckv3out"), "q": ("-s7", "-tv7"), "kv": ("-s7", "-tv7")}),
                 project(st, "c", 0, lambda k: tokens(k, 2), lambda k: codes(k, 2),
                         {"bank": ("bkv2out", "bkv3out"), "q": ("s3", "tv3"), "kv": ("s3", "tv3")})]
        when = {0: (0, 0, 2), 1: (0, 2, 4), 2: (0, 4, 6), 4: (1, 0, 1), 5: (1, 1, 2), 6: (1, 2, 3),
                7: (1, 3, 4), 8: (1, 4, 5), 9: (1, 5, 6)}
        for n in range(TURNS + 3):
            if n < TURNS:
                scores(n)
            if n in when:
                which, lo, hi = when[n]
                for group in nexts[which][lo:hi]:
                    for step in group:
                        st.add(*step)
            if 0 <= n - 2 < TURNS:
                turned(n - 2)
            if 0 <= n - 3 < TURNS:
                outputs(n - 3)
            if n == 8:
                project_out(0)
        project_out(1)
        st.run()


def norm_steps(st, tag, c, x, center, eps, out_name, finish, *after):
    cen, sq, sd, rs, pm, pv = (c.nb[tag][k] for k in ("cen", "sq", "sd", "rs", "pm", "pv"))
    weights = c.mean if center else c.ones
    if center:
        st.add(f"{tag}mean", "tensor", lambda e, k: e.matmul(pm[:, :], weights[:, :], x(k), start=True, stop=True),
               *after, f"-{tag}cen")
        st.add(f"{tag}cen", "vector", lambda e, k: e.tensor_tensor(cen[:, :], x(k), pm[:, :], ALU.subtract),
               f"{tag}mean", f"-{out_name}", f"-{tag}sq")
        src = lambda k: cen[:, :]
        last = (f"{tag}cen",)
    else:
        src, last = x, after
    st.add(f"{tag}sq", "scalar", lambda e, k: e.activation(sq[:, :], src(k), ACT.Square), *last, f"-{tag}var")
    st.add(f"{tag}var", "tensor", lambda e, k: e.matmul(pv[:, :], weights[:, :], sq[:, :], start=True, stop=True),
           f"{tag}sq", f"-{tag}sd")
    if center:
        st.add(f"{tag}sd", "scalar", lambda e, k: e.activation(sd[:, :], pv[:, :], ACT.Sqrt, bias=eps),
               f"{tag}var", f"-{tag}rs")
        st.add(f"{tag}rs", "vector", lambda e, k: e.reciprocal(rs[:, :], sd[:, :]), f"{tag}sd", f"-{out_name}")
    else:
        st.add(f"{tag}sd", "scalar", lambda e, k: e.activation(sd[:, :], pv[:, :], ACT.Sqrt),
               f"{tag}var", f"-{tag}clip")
        st.add(f"{tag}clip", "vector", lambda e, k: e.tensor_scalar(cen[:, :], sd[:, :], eps, None, ALU.max),
               f"{tag}sd", f"-{tag}rs")
        st.add(f"{tag}rs", "vector", lambda e, k: e.reciprocal(rs[:, :], cen[:, :]), f"{tag}clip", f"-{out_name}")
    st.add(out_name, "vector", lambda e, k: finish(e, k, src(k), rs[:, :]), f"{tag}rs")


class Const:
    pass


def two_layers(nc, a, out):
    with ExitStack() as ctx:
        def sb(name, shape, dt=F32, at=ctx):
            return at.enter_context(nc.sbuf_tensor(name, shape, dt))

        c = Const()
        c.nb = {}
        c.ident = sb("ident", [P, P])
        c.diag = sb("diag", [KT, LEN])
        c.ones = sb("ones", [P, P])
        c.mean = sb("mean", [P, P])
        c.y = sb("y", [P, TOKENS])
        x = sb("x", [P, CHUNKS, CH])
        xn = sb("xn", [P, CHUNKS, HALO + CH])
        xr = sb("xr", [P, CHUNKS, CH])
        eps = sb("eps", [P, 1])
        cols = sb("cols", [P, 2 + 4 * HT + 1 + 1])
        s_in = ctx.enter_context(nc.semaphore("s_in"))

        with nc.Block() as block:
            @block.sync
            def _(eng):
                loads = [(x[:, k, :], a["x"][:, k * CH:k * CH + CH]) for k in range(CHUNKS)]
                loads += [(c.ident[:, :], a["ident"]), (c.diag[:, :], a["diag"]), (cols[:, :], a["cols"])]
                for to, of in loads:
                    eng.dma_start(to, of).then_inc(s_in, 16)
                eng.wait_ge(s_in, 16 * len(loads))

            @block.gpsimd
            def _(eng):
                eng.memset(c.ones[:, :], 1.0)
                eng.memset(c.mean[:, :], 1.0 / P)
                eng.memset(eps[:, :], LN_EPS)
                eng.memset(xn[:, 0, 0:HALO], 0.0)
                eng.memset(xn[:, HALVES, 0:HALO], 0.0)

        with ExitStack() as moe:
            weights_t = sb("weights_t", [CW, CHUNKS, CH], F32R, moe)
            first_norm(nc, c, a, x, xn, eps, weights_t)
            head_attention(nc, c, a, xn)
            moe_ffn(nc, c, a, x, xn, xr, eps, cols, weights_t)
        c.src = lambda seq: xr[:, bass.ds(seq * HALVES, HALVES), :]
        attention(nc, c, lambda p: a["w1"][bass.ds(p, 1), :, :].rearrange("o k n -> (o k) n"),
                  lambda p: a["wo1"][bass.ds(p, 1), :, :].rearrange("o k n -> (o k) n"))
        mlp_ffn(nc, c, a, x, xn, cols, out)


def norm_buffers(nc, ctx, c, tags, names):
    for tag in tags:
        c.nb[tag] = {k: ctx.enter_context(nc.sbuf_tensor(f"{tag}{k}{names}", [P, CH], F32))
                     for k in ("cen", "sq", "sd", "rs")}


def first_norm(nc, c, a, x, xn, eps, weights_t):
    with ExitStack() as ctx:
        def sb(name, shape, dt=F32):
            return ctx.enter_context(nc.sbuf_tensor(name, shape, dt))

        def ps(name, shape):
            return ctx.enter_context(nc.psum_tensor(name, shape, F32))

        SENT = 8
        norm_buffers(nc, ctx, c, ("n0",), "")
        c.nb["n0"].update(pm=ps("n0pm", [P, CH]), pv=ps("n0pv", [P, CH]))
        cur = sb("cur", [P, CH])
        rw = sb("rw", [P, EXPERTS])
        rb = sb("rb", [P, TT, EXPERTS])
        lg = sb("lg", [P, TT, EXPERTS])
        top = sb("top", [P, TT])
        sh = sb("sh", [P, TT, EXPERTS])
        ex = sb("ex", [P, TT, EXPERTS])
        sm = sb("sm", [P, TT])
        rsm = sb("rsm", [P, TT])
        pr = sb("pr", [P, TT, EXPERTS + SENT])
        m8 = sb("m8", [P, TT, 8])
        rep = sb("rep", [P, TT, EXPERTS + SENT])
        two = sb("two", [P, TT])
        rtwo = sb("rtwo", [P, TT])
        mask = sb("mask", [P, TT, EXPERTS])
        wt = sb("wt", [P, TT, EXPERTS])
        cm = sb("cm", [P, TT, CW])
        r_ps = ps("r_ps", [P, TT, EXPERTS])
        t_ps = ps("t_ps", [CW, TT, P])
        s_l = ctx.enter_context(nc.semaphore("s_l"))
        s_pad = ctx.enter_context(nc.semaphore("s_pad"))
        with nc.Block() as block:
            @block.sync
            def _(eng):
                eng.dma_start(rw[:, :], a["rw"]).then_inc(s_l, 16)
                eng.dma_start(rb[:, :, :], a["rb"].rearrange("p (t n) -> p t n", t=TT)).then_inc(s_l, 16)
                eng.wait_ge(s_l, 32)

            @block.gpsimd
            def _(eng):
                eng.memset(pr[:, :, EXPERTS:], -2.0)
                eng.memset(cm[:, :, EXPERTS + 1:LO], 0.0)
                eng.memset(cm[:, :, LO + EXPERTS:], 0.0)
                eng.memset(cm[:, :, EXPERTS:EXPERTS + 1], 1.0)

        def wide(v):
            return v[:, :].unsqueeze(2).to_broadcast([P, TT, EXPERTS])

        st = Steps(nc, "fn", ctx)
        norm_steps(st, "n0", c, lambda k: x[:, bass.ds(k, 1), :].rearrange("p o n -> p (o n)"), True, eps[:, :], "cur",
                   lambda e, k, cen, rs: e.tensor_tensor(cur[:, :], cen, rs, ALU.mult), "-logits", "-keep")
        st.add("keep", "gpsimd", lambda e, k: e.tensor_copy(
            xn[:, bass.ds(k, 1), HALO:].rearrange("p o n -> p (o n)"), cur[:, :]), "cur")

        def logits(e, k):
            for t in range(TT):
                mm = e.matmul(r_ps[:, t, :], cur[:, t * P:t * P + P], rw[:, :], start=True, stop=True)
            return mm

        def each(f):
            def emit(e, k):
                e.sem_inc(s_pad, 1)
                for t in range(TT):
                    i = f(e, t)
                return i
            return emit

        E = slice(0, EXPERTS)
        st.add("logits", "tensor", logits, "cur", "-lg")
        st.add("lg", "vector", lambda e, k: e.tensor_tensor(lg[:, :, :], r_ps[:, :, :], rb[:, :, :], ALU.add),
               "logits", "-sh")
        st.add("top", "vector", lambda e, k: e.reduce_max(top[:, :], lg[:, :, :], AX_X), "lg", "-sh")
        st.add("sh", "vector", lambda e, k: e.tensor_tensor(sh[:, :, :], lg[:, :, :], wide(top), ALU.subtract),
               "top", "-ex")
        st.add("ex", "scalar", lambda e, k: e.activation(ex[:, :, :], sh[:, :, :], ACT.Exp), "sh", "-pr")
        st.add("sm", "vector", lambda e, k: e.reduce_sum(sm[:, :], ex[:, :, :], AX_X), "ex", "-rsm")
        st.add("rsm", "vector", lambda e, k: e.reciprocal(rsm[:, :], sm[:, :]), "sm", "-pr")
        st.add("pr", "vector", lambda e, k: e.tensor_tensor(pr[:, :, E], ex[:, :, :], wide(rsm), ALU.mult),
               "rsm", "-wt")
        st.add("m8", "vector", each(lambda e, t: e.max(m8[:, t, :], pr[:, t, E])), "pr", "-two")
        st.add("m8b", "vector", lambda e, k: e.memset(m8[:, :, 2:8], -2.0), "m8")
        st.add("rep", "vector", each(lambda e, t: e.match_replace(rep[:, t, :], m8[:, t, :], pr[:, t, :], -1.0)),
               "m8b", "-mask")
        st.add("two", "vector", lambda e, k: e.reduce_sum(two[:, :], m8[:, :, 0:2], AX_X), "m8b", "-rtwo0")
        st.add("rtwo0", "vector", lambda e, k: e.tensor_scalar(top[:, :], two[:, :], 1e-6, None, ALU.add), "two", "sh")
        st.add("rtwo", "vector", lambda e, k: e.reciprocal(rtwo[:, :], top[:, :]), "rtwo0", "-cmw")
        st.add("mask", "vector", lambda e, k: e.tensor_scalar(mask[:, :, :], rep[:, :, E], 0.0, None, ALU.is_lt),
               "rep", "-wt")
        st.add("wt", "vector", lambda e, k: e.tensor_tensor(wt[:, :, :], mask[:, :, :], pr[:, :, E], ALU.mult),
               "mask", "-cmw")
        st.add("cmw", "vector", lambda e, k: e.tensor_tensor(ex[:, :, :], wt[:, :, :], wide(rtwo), ALU.mult),
               "wt", "rtwo", "pr")
        st.add("hi", "vector", lambda e, k: e.tensor_copy(cm[:, :, E].bitcast(F32R), ex[:, :, :]), "cmw", "-turn")
        st.add("lo", "vector", lambda e, k: e.tensor_tensor(cm[:, :, LO:LO + EXPERTS].bitcast(F32R), ex[:, :, :],
                                                            cm[:, :, E], ALU.subtract), "hi")

        def turn(e, k):
            for t in range(TT):
                mm = e.transpose(t_ps[:, t, :], cm[:, t, :], c.ident[:, :])
            return mm

        st.add("turn", "tensor", turn, "lo", "-keep_w")
        st.add("keep_w", "vector", lambda e, k: e.tensor_copy(
            weights_t[:, bass.ds(k, 1), :].rearrange("p o n -> p (o n)"),
            t_ps[:, :, :].rearrange("p t n -> p (t n)")), "turn")
        st.run()
        with nc.Block() as block:
            @block.gpsimd
            def _(eng):
                for k in range(1, CHUNKS, HALVES):
                    eng.tensor_copy(xn[:, k, 0:HALO], xn[:, k - 1, CH:CH + HALO])


def moe_ffn(nc, c, a, x, xn, xr, eps, cols, weights_t):
    with ExitStack() as ctx:
        def sb(name, shape, dt=F32):
            return ctx.enter_context(nc.sbuf_tensor(name, shape, dt))

        def ps(name):
            return ctx.enter_context(nc.psum_tensor(name, [P, CH], F32))

        wg, wu, wd = (sb(n, [P, EPAIRS, P]) for n in ("wg", "wu", "wd"))
        wc = sb("wc", [P, HALO, P])
        sel_f = sb("sel_f", [CW, EPAIRS + 1, P])
        sel = sb("sel", [CW, EPAIRS + 1, P], F32R)
        gcol = sb("gcol", [P, 1])
        g_ps, u_ps, w_ps = ([ps(f"{n}{i}") for i in range(2)] for n in ("g_ps", "u_ps", "w_ps"))
        y_ps, n_ps = ps("y_ps"), ps("n_ps")
        sg, su, h = ([sb(f"{n}{i}", [P, CH]) for i in range(2)] for n in ("sg", "su", "h"))
        own, gate, res = sb("own", [P, CH]), sb("gate", [P, CH]), sb("res", [P, CH])
        s_l = ctx.enter_context(nc.semaphore("s_l2"))
        norm_buffers(nc, ctx, c, ("n1", "r1"), "")
        c.nb["n1"].update(pm=n_ps, pv=n_ps)
        c.nb["r1"].update(pm=n_ps, pv=n_ps)
        with nc.Block() as block:
            @block.sync
            def _(eng):
                for t, n in ((wg, "wg"), (wu, "wu"), (wd, "wd"), (wc, "wc"), (sel_f, "sel")):
                    eng.dma_start(t[:, :, :], a[n].rearrange("k (e n) -> k e n", n=P)).then_inc(s_l, 16)
                eng.wait_ge(s_l, 80)
        with nc.Block() as block:
            @block.vector
            def _(eng):
                eng.tensor_copy(sel[:, :, :], sel_f[:, :, :])
                eng.tensor_scalar(gcol[:, :], cols[:, 1:2], 1.0, float(P) ** 0.5, ALU.add, ALU.mult)

        def flat(t, k, cut=slice(None)):
            return t[:, bass.ds(k, 1), cut].rearrange("p o n -> p (o n)")

        now = slice(HALO, HALO + CH)
        st = Steps(nc, "moe", ctx)
        for e in range(EPAIRS):
            b = e % 2

            def gates(eng, k, e=e, b=b):
                taps = [(wg[:, e, :], now)]
                if e == EPAIRS - 1:
                    taps += [(wc[:, t, :], slice(t, t + CH)) for t in range(HALO)]
                for n, (w, cut) in enumerate(taps):
                    mm = eng.matmul(g_ps[b][:, :], w, flat(xn, k, cut), start=n == 0, stop=n == len(taps) - 1)
                return mm

            old = "" if e >= 2 else "-"
            o = (e - 2) % EPAIRS
            st.add(f"g{e}", "tensor", gates, f"{old}sg{o}", *(("-xnew",) if e == 0 else ()))
            st.add(f"u{e}", "tensor", lambda eng, k, e=e, b=b: eng.matmul(
                u_ps[b][:, :], wu[:, e, :], flat(xn, k, now), start=True, stop=True), f"{old}su{o}")
            st.add(f"w{e}", "tensor", lambda eng, k, e=e, b=b: eng.matmul(
                w_ps[b][:, :], sel[:, e, :], flat(weights_t, k), start=True, stop=True),
                f"{old}h{o}", *(("-own",) if e == 0 else ()))
            st.add(f"sg{e}", "scalar", lambda eng, k, b=b: eng.activation(sg[b][:, :], g_ps[b][:, :], ACT.Silu),
                   f"g{e}", f"{old}su{o}")
            st.add(f"su{e}", "vector", lambda eng, k, b=b: eng.tensor_tensor(
                su[b][:, :], sg[b][:, :], u_ps[b][:, :], ALU.mult), f"sg{e}", f"u{e}", f"{old}h{o}")
            st.add(f"h{e}", "vector", lambda eng, k, b=b: eng.tensor_tensor(
                h[b][:, :], su[b][:, :], w_ps[b][:, :], ALU.mult), f"su{e}", f"w{e}", f"{old}y{o}")
            for d in ([e - 1] if e else []) + ([e] if e == EPAIRS - 1 else []):
                st.add(f"y{d}", "tensor", lambda eng, k, d=d: eng.matmul(
                    y_ps[:, :], wd[:, d, :], h[d % 2][:, :], start=d == 0, stop=d == EPAIRS - 1),
                    f"h{d}", *(("-sum",) if d == 0 else ()))
        st.add("w8", "tensor", lambda eng, k: eng.matmul(
            w_ps[0][:, :], sel[:, EPAIRS, :], flat(weights_t, k), start=True, stop=True), f"h{EPAIRS - 2}")
        st.add("own", "vector", lambda eng, k: eng.tensor_tensor(own[:, :], flat(xn, k, now), w_ps[0][:, :], ALU.mult),
               "w8", "-sum")
        st.add("sum", "vector", lambda eng, k: eng.tensor_tensor(res[:, :], own[:, :], y_ps[:, :], ALU.add),
               "own", f"y{EPAIRS - 1}", "-gate")
        st.add("gate", "scalar", lambda eng, k: eng.activation(gate[:, :], res[:, :], ACT.Silu), "sum", "-gated")
        st.add("gated", "vector", lambda eng, k: eng.scalar_tensor_tensor(
            out=own[:, :], in0=c.y[:, bass.ds(k * CH, CH)], scalar=cols[:, 0:1], in1=gate[:, :],
            op0=ALU.add, op1=ALU.mult), "gate", "sum")
        st.add("xnew", "vector", lambda eng, k: eng.tensor_tensor(flat(x, k), flat(x, k), own[:, :], ALU.add),
               "gated")
        norm_steps(st, "n1", c, lambda k: flat(x, k), True, eps[:, :], "xn1",
                   lambda e, k, cen, rs: e.tensor_tensor(flat(xn, k, now), cen, rs, ALU.mult),
                   "xnew", f"u{EPAIRS - 1}", f"g{EPAIRS - 1}", "own", "-r1sd")
        norm_steps(st, "r1", c, lambda k: flat(xn, k, now), False, RMS_EPS, "xr1",
                   lambda e, k, v, rs: e.scalar_tensor_tensor(out=flat(xr, k), in0=v, scalar=gcol[:, :], in1=rs,
                                                              op0=ALU.mult, op1=ALU.mult), "xn1", "n1sd")
        st.run()


def mlp_ffn(nc, c, a, x, xn, cols, out):
    with ExitStack() as ctx:
        def sb(name, shape, dt=F32):
            return ctx.enter_context(nc.sbuf_tensor(name, shape, dt))

        m1, m2 = sb("m1", [P, HID]), sb("m2", [P, HID])
        h1, h2, m3 = sb("m_h1", [P, HT, HID]), sb("m_h2", [P, HT, HID]), sb("m3", [P, HT, P])
        bank = [ctx.enter_context(nc.psum_tensor(f"bank{i}", [P, CH], F32)) for i in range(8)]
        sg = [sb(f"sgm{i}", [P, CH]) for i in range(2)]
        act = [[sb(f"act{i}{m}", [P, CH]) for m in range(HT)] for i in range(3)]
        gate, res, fin = sb("gate_m", [P, CH]), sb("res_m", [P, CH]), [sb(f"fin{i}", [P, CH]) for i in range(1)]
        s_l = ctx.enter_context(nc.semaphore("s_l3"))
        with nc.Block() as block:
            @block.sync
            def _(eng):
                for t, n in ((m1, "m1"), (m2, "m2")):
                    eng.dma_start(t[:, :], a[n]).then_inc(s_l, 16)
                for t, n in ((h1, "h1"), (h2, "h2"), (m3, "m3")):
                    eng.dma_start(t[:, :, :], a[n].rearrange("k (t n) -> k t n", t=HT)).then_inc(s_l, 16)
                eng.wait_ge(s_l, 80)

        def col(n, m):
            return cols[:, 2 + n * HT + m:3 + n * HT + m]

        def cur(k):
            return xn[:, bass.ds(k, 1), HALO:].rearrange("p o n -> p (o n)")

        st = Steps(nc, "mlp", ctx)
        last = {}
        turn = [0]

        def take():
            b = turn[0] % 8
            turn[0] += 1
            return b

        def freed(b):
            return last.get(b, f"-{final[b]}")

        names = []
        for m in range(HT):
            names += [f"s{m}", f"t{m}"]
        names += [f"a{i}{m}" for i in (1, 2) for m in range(HT)] + ["gate"]
        final = {n % 8: name for n, name in enumerate(names)}

        for m in range(HT):
            ba, bb = take(), take()
            st.add(f"p{m}", "tensor", lambda e, k, m=m, ba=ba: e.matmul(
                bank[ba][:, :], m1[:, m * P:m * P + P], cur(k), start=True, stop=True), freed(ba))
            st.add(f"q{m}", "tensor", lambda e, k, m=m, bb=bb: e.matmul(
                bank[bb][:, :], m2[:, m * P:m * P + P], cur(k), start=True, stop=True), freed(bb))
            last[ba], last[bb] = f"s{m}", f"t{m}"
            old = f"t{m - 2}" if m >= 2 else f"-t{m + 2}"
            st.add(f"s{m}", "scalar", lambda e, k, m=m, ba=ba: e.activation(
                sg[m % 2][:, :], bank[ba][:, :], ACT.Silu, scale=col(0, m)), f"p{m}", old)
            st.add(f"t{m}", "vector", lambda e, k, m=m, bb=bb: e.scalar_tensor_tensor(
                out=act[0][m][:, :], in0=bank[bb][:, :], scalar=col(1, m), in1=sg[m % 2][:, :],
                op0=ALU.mult, op1=ALU.mult), f"s{m}", f"q{m}", f"-r1{HT - 1}")
        for i, w in ((1, h1), (2, h2)):
            for m in range(HT):
                b = take()

                def layer(e, k, i=i, w=w, m=m, b=b):
                    for j in range(HT):
                        mm = e.matmul(bank[b][:, :], w[:, j, m * P:m * P + P], act[i - 1][j][:, :],
                                      start=j == 0, stop=j == HT - 1)
                    return mm

                inputs = [f"t{j}" if i == 1 else f"a1{j}" for j in range(HT)]
                st.add(f"r{i}{m}", "tensor", layer, freed(b), *inputs)
                last[b] = f"a{i}{m}"
                reader = f"-r2{HT - 1}" if i == 1 else "-r3"
                st.add(f"a{i}{m}", "scalar", lambda e, k, i=i, m=m, b=b: e.activation(
                    act[i][m][:, :], bank[b][:, :], ACT.Gelu, scale=col(1 + i, m)), f"r{i}{m}", reader)
        b = take()

        def last_layer(e, k):
            for j in range(HT):
                mm = e.matmul(bank[b][:, :], m3[:, j, :], act[2][j][:, :], start=j == 0, stop=j == HT - 1)
            return mm

        st.add("r3", "tensor", last_layer, freed(b), *[f"a2{j}" for j in range(HT)])
        st.add("gate", "scalar", lambda e, k: e.activation(gate[:, :], bank[b][:, :], ACT.Silu, scale=col(4, 0)),
               "r3", "-mul")
        st.add("mul", "vector", lambda e, k: e.tensor_tensor(res[:, :], c.y[:, bass.ds(k * CH, CH)], gate[:, :], ALU.mult),
               "gate", "-fin")
        st.add("fin", "vector", lambda e, k: e.tensor_tensor(
            fin[0][:, :], x[:, bass.ds(k, 1), :].rearrange("p o n -> p (o n)"), res[:, :], ALU.add), "mul", "-store")
        st.add("store", "sync", lambda e, k: e.dma_start(out[:, bass.ds(k * CH, CH)], fin[0][:, :]), "fin")
        st.run()


def kernel(**inputs):
    import numpy as np
    import concourse.bacc as bacc
    from concourse.bass_utils import run_bass_kernel_spmd

    i = {k: np.asarray(v) for k, v in inputs.items()}
    f = np.float32
    a = {"x": i["L0_attn_x"].reshape(TOKENS, P).T}

    w = i["L0_attn_w_qkv"].reshape(P, HEADS, 3, HD)
    b = i["L0_attn_b_qkv"].reshape(HEADS, 3, HD)
    a["wq0"] = w[:, :, 0].reshape(P, -1)
    a["wkv0"] = w[:, :, 1:].reshape(P, -1)
    a["bq0"] = b[:, 0].reshape(PAIRS, P).T
    a["bkv0"] = b[:, 1:].reshape(HEADS, P).T
    a["wo0"] = i["L0_attn_w_out"].reshape(PAIRS, P, P).transpose(1, 0, 2).reshape(P, -1)

    w = i["L1_attn_w_qkv"].reshape(P, 3, HEADS, HD)
    a["w1"] = np.zeros((PAIRS, P, W_V), f)
    for p in range(PAIRS):
        for n in range(2):
            for h in range(2):
                for at in ((2 * n + h) * P, (2 * n + h) * P + HD):
                    a["w1"][p, :, at:at + HD] = w[:, n, 2 * p + h]
        a["w1"][p, :, W_QK:] = w[:, 2, 2 * p:2 * p + 2].reshape(P, P)
    a["wo1"] = i["L1_attn_w_out"].reshape(PAIRS, P, P)

    a["rw"] = i["L0_ffn_router_w"]
    a["rb"] = np.tile(i["L0_ffn_router_bias"], (P, TT))
    conv = i["L0_ffn_conv_w"]
    for n, name, shared in (("wg", "gate", conv[:, :, HALO].T), ("wu", "up", i["L0_ffn_shared_up_w"])):
        each = list(i[f"L0_ffn_expert_{name}_w"]) + [shared]
        a[n] = np.concatenate(each, axis=1)
    down = list(i["L0_ffn_expert_down_w"]) + [i["L0_ffn_shared_down_w"]]
    a["wd"] = np.concatenate([np.concatenate(down[2 * e:2 * e + 2], axis=0) for e in range(EPAIRS)], axis=1)
    a["wc"] = np.zeros((P, HALO * P), f)
    for t in range(HALO):
        a["wc"][:, t * P + HD:(t + 1) * P] = conv[:, :, t].T
    cols = [i["L0_attn_b_out"][:, None], i["L1_attn_gamma"][:, None]]
    for n in ("w1", "w2", "h1", "h2"):
        cols.append(i[f"L1_ffn_{n}_s"].reshape(HT, P).T)
    cols += [i["L1_ffn_w3_s"][:, None], np.zeros((P, 1), f)]
    a["cols"] = np.concatenate(cols, axis=1)
    a["m1"], a["m2"] = i["L1_ffn_w1_w"].T, i["L1_ffn_w2_w"].T
    for n, name in (("h1", "h1"), ("h2", "h2"), ("m3", "w3")):
        t = i[f"L1_ffn_{name}_w"].T
        a[n] = t.reshape(HT, P, -1).transpose(1, 0, 2).reshape(P, -1)

    a["ident"] = np.eye(P, dtype=f)
    a["diag"] = np.repeat(np.eye(KT, dtype=f), P, axis=1)
    sel = np.zeros((CW, EPAIRS + 1, P), f)
    for e in range(EXPERTS):
        rows = [e, LO + e] if e < EXPERTS - 1 else [EXPERTS]
        sel[rows, e // 2, (e % 2) * HD:(e % 2 + 1) * HD] = 1.0
    sel[[EXPERTS - 1, LO + EXPERTS - 1], EPAIRS, :] = 1.0
    a["sel"] = sel.reshape(CW, -1)
    steps = np.exp(np.arange(0, HD, 2, dtype=f) * f(-(np.log(10000.0) / HD)))
    angle = np.arange(LEN, dtype=f)[:, None] * steps
    pos = np.zeros((LEN, HD), f)
    pos[:, 0::2], pos[:, 1::2] = np.sin(angle), np.cos(angle)
    a["pos"] = np.zeros((P, LEN), f)
    a["pos"][0:HD] = pos.T
    tokens = np.arange(P) // HEADS
    a["mask"] = np.where(tokens[:, None] == tokens, 0.0, LOWEST).astype(f)

    nc = bacc.Bacc("TRN2", target_bir_lowering=False, num_devices=1)
    arrays, args = {}, {}
    for n, v in a.items():
        v = np.ascontiguousarray(v)
        arrays[f"in_{n}"] = v
        args[n] = nc.dram_tensor(f"in_{n}", v.shape, mybir.dt.from_np(v.dtype), kind="ExternalInput").ap()
    out = nc.dram_tensor("out", (P, TOKENS), F32, kind="ExternalOutput").ap()
    two_layers(nc, args, out)
    r = run_bass_kernel_spmd(nc, [arrays], core_ids=[0])
    return r.results[0]["out"].T.reshape(SEQS, LEN, P)
```

```python
from contextlib import ExitStack

import concourse.bass as bass
from concourse import mybir

F32 = mybir.dt.float32
F32R = mybir.dt.float32r
ACT = mybir.ActivationFunctionType
ALU = mybir.AluOpType
AX_X = mybir.AxisListType.X

P = 128
SEQS, LEN = 2, 1024
TOKENS = SEQS * LEN
CH = 512
CHUNKS = TOKENS // CH
HALVES = LEN // CH
HEADS, HD = 16, 64
PAIRS = HEADS // 2
STEPS = SEQS * PAIRS
KT = LEN // P
TT = CH // P
EXPERTS = 16
EPAIRS = EXPERTS // 2
HALO = 2
HID = 512
HT = HID // P
LOWEST = -3.0e38
LN_EPS = 1e-5
RMS_EPS = 1e-12
SCALE = HD ** -0.5
CW = 128
LO = 32

W_QK = 2 * P
W_V = W_QK + P



class Counter:

    def __init__(self, sem, per, ahead=0):
        self.sem, self.per, self.ahead = sem, per, ahead

    def wait(self, eng, period, n):
        value = period * self.per + n + self.ahead
        if not isinstance(value, int) or value > self.ahead:
            eng.wait_ge(self.sem, value)


class Steps:

    ENGINES = ("tensor", "vector", "scalar", "gpsimd", "sync")

    def __init__(self, nc, name, ctx, periods=CHUNKS):
        self.nc, self.list, self.at, self.periods = nc, [], {}, periods
        self.name, self.ctx, self.count, self.sem = name, ctx, {}, {}

    def add(self, name, engine, emit, *after, late=False):
        assert name not in self.at
        key = (engine, late)
        if key not in self.sem:
            self.count[key] = 0
            self.sem[key] = self.ctx.enter_context(self.nc.semaphore(f"{self.name}_{engine}{'_late' if late else ''}"))
        self.count[key] += 16 if engine == "sync" else 1
        self.at[name] = (key, self.count[key])
        self.list.append((name, key, emit, after))

    def run(self):
        with self.nc.Block() as block:
            programs = {"tensor": block.tensor, "vector": block.vector, "scalar": block.scalar,
                        "gpsimd": block.gpsimd, "sync": block.sync}
            for engine, program in programs.items():
                if any(engine == of for of, _ in self.sem):
                    program(lambda eng, engine=engine: self._run(eng, engine))

    def _run(self, eng, engine):
        for late in (False, True):
            if (engine, late) in self.sem:
                eng.sem_inc(self.sem[engine, late], self.count[engine, late])
        if any(late for _, late in self.sem):
            self._period(eng, engine, 0, (False,))
            with eng.Fori(1, self.periods) as period:
                self._period(eng, engine, period, (False, True))
            self._period(eng, engine, self.periods, (True,))
        elif self.periods == 1:
            self._period(eng, engine, 0, (False,))
        else:
            with eng.Fori(0, self.periods) as period:
                self._period(eng, engine, period, (False,))
        if engine == "sync":
            eng.wait_ge(self.sem[engine, False], (self.periods + 1) * self.count[engine, False])

    def _period(self, eng, engine, period, lates):
        for name, key, emit, after in self.list:
            if key[0] != engine or key[1] not in lates:
                continue
            chunk = period - 1 if key[1] else period
            latest = {}
            for what in after:
                of, n = self.at[what.lstrip("-")]
                latest[of] = max(latest.get(of, (0, 0)), (0 if what.startswith("-") else 1, n))
            for of, (this, n) in latest.items():
                eng.wait_ge(self.sem[of], (chunk + this) * self.count[of] + n)
            emit(eng, chunk).then_inc(self.sem[key], 16 if engine == "sync" else 1)


class Recorded:

    def __init__(self):
        self.list = []

    def add(self, *step):
        self.list.append(step)

    def take(self, st, n):
        for step in self.list[:n]:
            st.add(*step, late=True)
        self.list = self.list[n:]


def attention(nc, c, w_pair, w_out):
    with ExitStack() as ctx:
        def sb(name, shape, dt=F32):
            return ctx.enter_context(nc.sbuf_tensor(name, shape, dt))

        def ps(name, shape):
            return ctx.enter_context(nc.psum_tensor(name, shape, F32))

        def counter(name, per, ahead=0):
            return Counter(ctx.enter_context(nc.semaphore(name)), per, ahead)

        x_cur = sb("x_cur", [P, 2, LEN])
        w_cur = sb("w_cur", [P, 2, W_V])
        wo_cur = sb("wo_cur", [P, 2, P])
        q_a = sb("q_a", [P, 2, 2, LEN], F32R)
        k_a = sb("k_a", [P, 2, 2, LEN], F32R)
        q_b = sb("q_b", [P, 2, 2, LEN], F32R)
        k_b = sb("k_b", [P, 2, 2, LEN], F32R)
        own_rows = [slice(0, HD), slice(HD, P)]
        other_rows = [slice(HD, P), slice(0, HD)]
        v_cur = sb("v_cur", [P, 2, KT, P])
        RING = 8
        prob = sb("prob", [P, RING, CH])
        acc = sb("acc", [P, HALVES, 2, CH])
        mx_part = sb("mx_part", [P, 2, KT, 2])
        mx_row = sb("mx_row", [P, 2, KT])
        rden = sb("rden", [P, HALVES, CH])
        o_n = sb("o_n", [P, HALVES, CH])

        st_ps = ps("st_ps", [P, 2, CH])
        mx_ps = ps("mx_ps", [P, 2, CH])
        o_ps = ps("o_ps", [P, HALVES, CH])
        pj_ps = ps("pj_ps", [P, 2, CH])

        s_init = ctx.enter_context(nc.semaphore("s_init"))
        s_w = [counter(f"s_w{par}", 32) for par in range(2)]
        s_wo = [counter(f"s_wo{par}", 16) for par in range(2)]
        s_prep = counter("s_prep", 8)
        s_hi = counter("s_hi", 16)
        s_lo = counter("s_lo", 10)
        s_v = counter("s_v", 2)
        s_mx = counter("s_mx", 32)
        s_mxr = counter("s_mxr", 32)
        s_row = counter("s_row", 2)
        s_st = counter("s_st", 32)
        s_exp = counter("s_exp", 32)
        s_pv = counter("s_pv", 16)
        s_acc = counter("s_acc", 28)
        s_fin = counter("s_fin", 4, 4)
        s_den = counter("s_den", 2, 2)
        s_out = counter("s_out", 2, 2)
        s_rcp = counter("s_rcp", 8)
        s_on = counter("s_on", 2, 2)

        slots = [[] for _ in range(48)]
        QK_AT, DEN_AT, V_AT, TR_AT = (0, 4, 7, 11), (27, 1), (16, 20), (36, 47)
        RCP, NORM, OUT = 2, 9, 12
        for at, (t, half) in zip(QK_AT, ((0, 0), (1, 0), (1, 1), (0, 1))):
            slots[at].append(("qk", t, half))
        for half, at in enumerate(DEN_AT):
            slots[at].append(("den", half))
            for n in range(4):
                slots[at + 1 + RCP * n].append(("rcp", half, n))
            slots[at + NORM].append(("norm", half))
            slots[at + OUT].append(("out", half))
        for n, at in enumerate(V_AT):
            slots[at].append(("v", n))
        for n, at in enumerate([s for s in range(9, 48) if s not in (30, 34, 35)][:32]):
            slots[at].append(("tile", n))
        for h, at in enumerate(TR_AT):
            slots[at].append(("tr", h))
        tiles = [(h, i, 0) for h in range(2) for i in range(TT)]
        tiles += [(h, i, 1) for h in range(2) for i in range(TT)]
        tiles += [(h, i, keys) for h in range(2) for i in range(TT, KT) for keys in range(2)]
        UNITS = ("qk", "v", "tr", "den", "out")
        PREPARE = ("qk", "v", "tr", "tile")
        order = [u for slot in slots for u in slot if u[0] in UNITS]
        prepare = [u for u in order if u[0] in PREPARE]
        qks = [u for u in prepare if u[0] == "qk"]
        lows = [u for u in prepare if u[0] in ("qk", "tr") for _ in range(2 if u[0] == "qk" else 1)]
        last_low = {u: n + 1 for n, u in enumerate(lows)}
        assert len(order) % 2 == 0
        assert (len(prepare), len(lows), 4 * len(qks)) == (s_prep.per, s_lo.per, s_hi.per)

        def written(u, m):
            if u in prepare:
                return s_prep, m + 1, prepare.index(u) + 1
            return s_fin, m - u[1], 2 * u[1] + (u[0] == "out") + 1

        def read(u, m):
            if u[0] == "v":
                return s_v, m + 1, u[1] + 1
            if u in prepare:
                return s_lo, m + 1, last_low[u]
            return (s_den if u[0] == "den" else s_out), m - u[1], u[1] + 1

        def exists(u, m):
            if not isinstance(m, int):
                return True
            if u[0] in PREPARE:
                return -1 <= m < STEPS - 1
            return 0 <= m - u[1] < STEPS

        def bank(u):
            return order.index(u) % 2

        def wait(eng, event):
            event[0].wait(eng, event[1], event[2])

        def extras(slot, m):
            return [u for u in slots[slot] if exists(u, m)]

        def bank_free(eng, u, m):
            n, period = order.index(u) - 2, m
            for _ in range(2 * len(order)):
                if n < 0:
                    n, period = n + len(order), period - 1
                if exists(order[n], period):
                    return wait(eng, read(order[n], period))
                n -= 2

        def needed_adds(s):
            return 14 * (s // KT) + 2 * max(1, s % KT)

        def parts(m):
            if not isinstance(m, int):
                return True, True, True
            return 0 <= m < STEPS, m < STEPS - 1, m > 0

        def periods(eng, body):
            body(eng, -1, 1)
            body(eng, 0, 0)
            with eng.Fori(0, STEPS // 2 - 1) as i:
                body(eng, 2 * i + 1, 1)
                body(eng, 2 * i + 2, 0)
            body(eng, STEPS - 1, 1)
            body(eng, STEPS, 0)

        def pe(eng, m, par):
            own, prep, fin = parts(m)
            nxt = 1 - par

            def pv(step, period, par_v):
                half, j = step // KT, step % KT
                s_exp.wait(eng, period, 2 * step + 2)
                if j == 0:
                    s_on.wait(eng, period - 1, half + 1)
                for h in range(2):
                    mm = eng.matmul(o_ps[64 * h:64 * h + 64, half, :], v_cur[:, par_v, j, HD * h:HD * h + HD],
                                    prob[:, (2 * step + h) % RING, :], start=(j == 0), stop=(j == KT - 1),
                                    skip_group_check=True)
                mm.then_inc(s_pv.sem, 1)

            def unit(u):
                if u == prepare[0]:
                    s_w[nxt].wait(eng, (m + 1) // 2, 32)
                bank_free(eng, u, m)
                out = pj_ps[:, bank(u), :]
                if u[0] == "qk":
                    _, t, half = u
                    tok = slice(half * CH, half * CH + CH)
                    mm = eng.matmul(out, w_cur[:, nxt, t * P:t * P + P], x_cur[:, nxt, tok],
                                    start=True, stop=True)
                elif u[0] == "v":
                    for i in range(TT):
                        j = TT * u[1] + i
                        mm = eng.matmul(out[:, i * P:i * P + P], x_cur[:, nxt, j * P:j * P + P],
                                        w_cur[:, nxt, W_QK:W_V], start=True, stop=True)
                elif u[0] == "tr":
                    s_row.wait(eng, m + 1, u[1] + 1)
                    mm = eng.transpose(out[0:KT, 0:P], mx_row[:, u[1], :], c.ident[:, :])
                elif u[0] == "den":
                    s_acc.wait(eng, m - u[1], 14 * (u[1] + 1))
                    for h in range(2):
                        mm = eng.matmul(out[64 * h:64 * h + 64, :], c.ones[:, 0:64], acc[:, u[1], h, :],
                                        start=True, stop=True, skip_group_check=True)
                else:
                    q, par_q = m - u[1], par if u[1] == 0 else nxt
                    s_wo[par_q].wait(eng, q // 2, 16)
                    s_on.wait(eng, q, u[1] + 1)
                    mm = eng.matmul(out, wo_cur[:, par_q, :], o_n[:, u[1], :],
                                    start=True, stop=True)
                mm.then_inc(written(u, m)[0].sem, 1)

            def score_tile(n):
                h, i, keys = tiles[n]
                if n in (0, TT * 2, TT * 4):
                    wait(eng, read(qks[n // (TT * 2) + 1], m))
                s_mxr.wait(eng, m + 1, n - 1)
                eng.matmul(mx_ps[:, n % 2, :], q_a[:, nxt, h, i * P:i * P + P],
                           k_a[:, nxt, h, keys * CH:keys * CH + CH], start=True, stop=True)\
                   .then_inc(s_mx.sem, 1)

            def beside(slot):
                for u in extras(slot, m):
                    if u[0] in UNITS:
                        unit(u)
                    elif u[0] == "tile":
                        score_tile(u[1])

            for s in range(16):
                half, j = s // KT, s % KT
                if own and s == 0:
                    s_v.wait(eng, m, 2)
                for h in range(2):
                    if own and s == 0:
                        s_lo.wait(eng, m, 9 + h)
                    if own:
                        s_exp.wait(eng, m, 2 * s + h - 1)
                        keys, tok = slice(j * P, j * P + P), slice(half * CH, half * CH + CH)
                        eng.matmul(st_ps[:, h, :], k_a[:, par, h, keys], q_a[:, par, h, tok],
                                   start=True, stop=False)
                        eng.matmul(st_ps[:, h, :], k_b[:, par, h, keys], q_b[:, par, h, tok],
                                   start=False, stop=True).then_inc(s_st.sem, 1)
                    beside(3 * s + h)
                if s == 0 and fin:
                    pv(15, m - 1, nxt)
                if s > 0 and own:
                    pv(s - 1, m, par)
                beside(3 * s + 2)

        def act(eng, m, par):
            own, prep, fin = parts(m)
            nxt = 1 - par
            for slot in range(48):
                s, h = slot // 3, slot % 3
                if own and h < 2:
                    s_st.wait(eng, m, 2 * s + h + 1)
                    s_pv.wait(eng, m, s - 3)
                    s_acc.wait(eng, *((m, needed_adds(s - 4)) if s >= 4 else (m - 1, needed_adds(s + 12))))
                    eng.activation(prob[:, (2 * s + h) % RING, :], st_ps[:, h, :], ACT.Exp, scale=SCALE)\
                       .then_inc(s_exp.sem, 1)
                for u in extras(slot, m):
                    if u[0] == "qk":
                        _, t, half = u
                        if u == prepare[0]:
                            s_st.wait(eng, m, 0)
                        wait(eng, written(u, m))
                        tok = slice(half * CH, half * CH + CH)
                        to = q_a if t == 0 else k_a
                        for h in range(2):
                            second = q_b[own_rows[h], nxt, h, tok] if t == 0 else k_a[other_rows[h], nxt, h, tok]
                            for o in (to[own_rows[h], nxt, h, tok], second):
                                eng.activation(o, pj_ps[own_rows[h], bank(u), :], ACT.Copy).then_inc(s_hi.sem, 1)
                    elif u[0] == "den":
                        wait(eng, written(u, m))
                        s_on.wait(eng, m - u[1] - 1, u[1] + 1)
                        eng.activation(rden[:, u[1], :], pj_ps[:, bank(u), :], ACT.Copy).then_inc(s_den.sem, 1)
                    elif u[0] == "v":
                        if u[1] == 0:
                            s_pv.wait(eng, m, 0)
                        wait(eng, written(u, m))
                        eng.activation(v_cur[:, nxt, TT * u[1]:TT * u[1] + TT, :],
                                       pj_ps[:, bank(u), :].rearrange("p (t n) -> p t n", t=TT), ACT.Copy)\
                           .then_inc(s_v.sem, 1)

        def dve(eng, m, par):
            own, prep, fin = parts(m)
            nxt = 1 - par
            for slot in range(48):
                for u in extras(slot, m):
                    if u[0] in UNITS:
                        src = pj_ps[:, bank(u), :]
                    if u[0] == "qk":
                        _, t, half = u
                        tok = slice(half * CH, half * CH + CH)
                        for h in range(2):
                            s_hi.wait(eng, m + 1, 4 * qks.index(u) + 2 * (h + 1))
                            r = own_rows[h]
                            hi = (q_a if t == 0 else k_a)[r, nxt, h, tok]
                            out = q_a[other_rows[h], nxt, h, tok] if t == 0 else k_b[r, nxt, h, tok]
                            eng.tensor_tensor(out, src[r, :], hi.bitcast(F32), ALU.subtract).then_inc(s_lo.sem, 1)
                    elif u[0] == "tr":
                        wait(eng, written(u, m))
                        at = other_rows[u[1]].start
                        eng.tensor_tensor(
                            q_b[at:at + KT, nxt, u[1], :].rearrange("p (i n) -> p i n", i=KT),
                            src[0:KT, 0:P].unsqueeze(1).to_broadcast([KT, KT, P]),
                            c.diag[:, :].rearrange("p (i n) -> p i n", i=KT), ALU.mult).then_inc(s_lo.sem, 1)
                    elif u[0] == "rcp":
                        h, q = u[1], m - u[1]
                        s_den.wait(eng, q, h + 1)
                        part = rden[:, h, u[2] * P:u[2] * P + P]
                        eng.reciprocal(part, part).then_inc(s_rcp.sem, 1)
                    elif u[0] == "norm":
                        h, q = u[1], m - u[1]
                        s_rcp.wait(eng, q, 4 * (h + 1))
                        s_pv.wait(eng, q, KT * (h + 1))
                        s_fin.wait(eng, q - 1, 2 * h + 2)
                        eng.tensor_tensor(o_n[:, h, :], o_ps[:, h, :], rden[:, h, :], ALU.mult)\
                           .then_inc(s_on.sem, 1)
                    elif u[0] == "out":
                        h, q = u[1], m - u[1]
                        wait(eng, written(u, m))
                        s_out.wait(eng, q - 1, h + 1)
                        seq = q // PAIRS
                        y = c.y[:, bass.ds(seq * LEN + h * CH, CH)]
                        eng.tensor_tensor(y, src, y, ALU.add).then_inc(s_out.sem, 1)
                    elif u[0] == "tile":
                        n = u[1]
                        h, i, keys = tiles[n]
                        s_mx.wait(eng, m + 1, n + 1)
                        if (i, keys) == (0, 0):
                            s_row.wait(eng, m, h + 1)
                        eng.reduce_max(mx_part[:, h, i, keys:keys + 1], mx_ps[:, n % 2, :], AX_X)\
                           .then_inc(s_mxr.sem, 1)
                        if (i, keys) == (KT - 1, 1):
                            s_mxr.wait(eng, m + 1, n + 1)
                            s_prep.wait(eng, m, prepare.index(("tr", h)) + 1)
                            eng.reduce_max(mx_row[:, h, :], mx_part[:, h, :, :], AX_X).then_inc(s_row.sem, 1)

        def pool(eng, m, par):
            if not parts(m)[0]:
                return
            for s in range(16):
                half, j = s // KT, s % KT
                if j == 0:
                    continue
                for h in range(2):
                    s_exp.wait(eng, m, 2 * s + h + 1)
                    new, a = prob[:, (2 * s + h) % RING, :], acc[:, half, h, :]
                    if j == 1:
                        s_fin.wait(eng, m - 1, 2 * half + 1)
                        first = prob[:, (2 * s + h - 2) % RING, :]
                    else:
                        s_acc.wait(eng, m, 14 * half + 2 * (j - 1) + h - 1)
                        first = a
                    eng.tensor_tensor(a, first, new, ALU.add).then_inc(s_acc.sem, 1)

        def load(eng, p, par):
            pair, seq = p % PAIRS, p // PAIRS
            late = not isinstance(p, int)
            if late:
                s_prep.wait(eng, p - 2, prepare.index(("v", 1)) + 1)
            eng.dma_start(x_cur[:, par, :].rearrange("p (h n) -> p h n", h=HALVES), c.src(seq)).then_inc(s_w[par].sem, 16)
            eng.dma_start(w_cur[:, par, :], w_pair(pair)).then_inc(s_w[par].sem, 16)
            if late:
                s_fin.wait(eng, p - 2, 4)
            eng.dma_start(wo_cur[:, par, :], w_out(pair)).then_inc(s_wo[par].sem, 16)

        with nc.Block() as block:
            @block.vector
            def _(eng):
                for h in range(2):
                    for t in (k_b, q_b):
                        eng.memset(t[other_rows[h], :, h, :].bitcast(F32), 0.0).then_inc(s_init, 1)
                eng.wait_ge(s_init, 4)
                for h in range(2):
                    at = other_rows[h].start
                    eng.memset(k_b[at:at + KT, :, h, :].bitcast(F32), -1.0)
                for k in (s_on, s_out):
                    eng.sem_inc(k.sem, k.ahead)

            @block.tensor
            def _(eng):
                eng.sem_inc(s_fin.sem, s_fin.ahead)

            @block.scalar
            def _(eng):
                eng.sem_inc(s_den.sem, s_den.ahead)

            @block.gpsimd
            def _(eng):
                eng.memset(c.y[:, :], 0.0)

        with nc.Block() as block:
            @block.sync
            def _(eng):
                load(eng, 0, 0)
                load(eng, 1, 1)
                with eng.Fori(1, STEPS // 2) as i:
                    load(eng, 2 * i, 0)
                    load(eng, 2 * i + 1, 1)

            block.tensor(lambda eng: periods(eng, pe))
            block.scalar(lambda eng: periods(eng, act))
            block.vector(lambda eng: periods(eng, dve))
            block.gpsimd(lambda eng: periods(eng, pool))


def head_attention(nc, c, a, xn):
    BLK = 128
    TURNS = 8
    GROUPS = 4
    G = 8
    with ExitStack() as ctx:
        def sb(name, shape, dt=F32):
            return ctx.enter_context(nc.sbuf_tensor("ha_" + name, shape, dt))

        def ps(name, shape):
            return ctx.enter_context(nc.psum_tensor("ha_" + name, shape, F32))

        wq = sb("wq", [P, PAIRS, P])
        wkv = sb("wkv", [P, HEADS, P])
        wo = sb("wo", [P, PAIRS, P])
        bq, bkv = sb("bq", [P, PAIRS]), sb("bkv", [P, HEADS])
        pos = sb("pos", [P, LEN])
        mask = sb("mask", [P, P])
        q = [sb(f"q{i}", [P, BLK * HEADS]) for i in range(2)]
        kv = [sb(f"kv{i}", [P, BLK * HEADS]) for i in range(2)]
        masked = [sb(f"masked{i}", [P, GROUPS, P]) for i in range(2)]
        top = [sb(f"top{i}", [P, GROUPS]) for i in range(2)]
        shift = [sb(f"shift{i}", [P, GROUPS]) for i in range(2)]
        total = [sb(f"total{i}", [P, GROUPS]) for i in range(4)]
        rtotal = [sb(f"rtotal{i}", [P, GROUPS]) for i in range(4)]
        ex = [sb(f"ex{i}", [P, GROUPS, P]) for i in range(4)]
        prob = [sb(f"prob{i}", [P, GROUPS, P]) for i in range(4)]
        prob_t = [sb(f"prob_t{i}", [P, GROUPS, P]) for i in range(2)]
        v_t = [sb(f"v_t{i}", [P, GROUPS, HD]) for i in range(4)]
        o = [sb(f"o{i}", [P, PAIRS, BLK]) for i in range(2)]
        pj_ps = [ps(f"pj_ps{i}", [P, 4, BLK]) for i in range(2)]
        s_ps = [ps(f"s_ps{i}", [P, GROUPS, P]) for i in range(2)]
        v_ps, p_ps = ps("v_ps", [P, GROUPS, P]), ps("p_ps", [P, GROUPS, P])
        o_ps, y_ps = ps("o_ps", [P, GROUPS, G * PAIRS]), ps("y_ps", [P, BLK])
        s_l = ctx.enter_context(nc.semaphore("s_l0"))
        s_pad = ctx.enter_context(nc.semaphore("s_pad0"))

        with nc.Block() as block:
            @block.sync
            def _(eng):
                loads = [(wq[:, :, :], a["wq0"].rearrange("k (h n) -> k h n", n=P)),
                         (wkv[:, :, :], a["wkv0"].rearrange("k (h n) -> k h n", n=P)),
                         (wo[:, :, :], a["wo0"].rearrange("k (h n) -> k h n", n=P)),
                         (bq[:, :], a["bq0"]), (bkv[:, :], a["bkv0"]), (pos[:, :], a["pos"]),
                         (mask[:, :], a["mask"])]
                for to, of in loads:
                    eng.dma_start(to, of).then_inc(s_l, 16)
                eng.wait_ge(s_l, 16 * len(loads))

            @block.vector
            def _(eng):
                for i in range(2):
                    eng.memset(q[i][HD:P, :], 0.0)

        def project(st, tag, to, x_at, pos_at, free):
            q_out = q[to][0:HD, :].rearrange("r (t h) -> r h t", h=HEADS)
            kv_out = kv[to][:, :].rearrange("r (t h) -> r h t", h=HEADS)
            units = [("q", n) for n in range(2)] + [("kv", n) for n in range(4)]
            steps = []
            for n, (kind, i) in enumerate(units):
                b = n % 2
                w = wq if kind == "q" else wkv
                name = f"{tag}{kind}{i}"

                def products(e, k, w=w, i=i, b=b):
                    for j in range(4):
                        mm = e.matmul(pj_ps[b][:, j, :], w[:, 4 * i + j, :], x_at(k), start=True, stop=True)
                    return mm

                bank_of = f"{tag}{units[n - 2][0]}{units[n - 2][1]}out" if n >= 2 else free["bank"][b]
                steps.append((f"{name}mm", "tensor", products, bank_of))
                if kind == "q":
                    def even(e, k, i=i, b=b):
                        return e.tensor_tensor(q_out[:, 8 * i:8 * i + 8:2, :], pj_ps[b][0:HD, :, :],
                                               bq[0:HD, 4 * i:4 * i + 4].unsqueeze(2).to_broadcast([HD, 4, BLK]), ALU.add)

                    def odd(e, k, i=i, b=b):
                        return e.tensor_tensor(q_out[:, 8 * i + 1:8 * i + 8:2, :], pj_ps[b][HD:P, :, :],
                                               bq[HD:P, 4 * i:4 * i + 4].unsqueeze(2).to_broadcast([HD, 4, BLK]), ALU.add)

                    steps.append((f"{name}even", "vector", even, f"{name}mm", *free["q"]))
                    steps.append((f"{name}out", "vector", odd, f"{name}mm"))
                else:
                    def out(e, k, i=i, b=b):
                        for j in range(4):
                            h = 4 * i + j
                            d = e.scalar_tensor_tensor(out=kv_out[:, h, :], in0=pj_ps[b][:, j, :],
                                                       scalar=bkv[:, h:h + 1], in1=pos_at(k), op0=ALU.add, op1=ALU.add)
                        return d

                    steps.append((f"{name}out", "vector", out, f"{name}mm", *free["kv"]))
            groups, at = [], 0
            for kind, _ in units:
                n = 3 if kind == "q" else 2
                groups.append(steps[at:at + n])
                at += n
            return groups

        def tokens(k, off):
            b = (2 * k + off) % (TOKENS // BLK)
            flat = xn[:, :, :].rearrange("p c n -> p (c n)")
            return flat[:, bass.ds((b // TT) * (HALO + CH) + (b % TT) * BLK + HALO, BLK)]

        def codes(k, off):
            b = (2 * k + off) % (LEN // BLK)
            return pos[:, bass.ds(b * BLK, BLK)]

        st = Steps(nc, "pro0", ctx, 1)
        for group in project(st, "x", 0, lambda k: xn[:, 0, HALO:HALO + BLK], lambda k: pos[:, 0:BLK],
                             {"bank": ("-xkv2out", "-xkv3out"), "q": (), "kv": ()}):
            for step in group:
                st.add(*step)
        st.run()

        st = Steps(nc, "ha", ctx, TOKENS // (2 * BLK))

        def past(name, n, depth):
            return f"{name}{n - depth}" if n >= depth else f"-{name}{n - depth + TURNS}"

        def scores(n):
            f, t = n // 4, n % 4
            cut = lambda g: slice((t * GROUPS + g) * P, (t * GROUPS + g + 1) * P)

            def products(e, k):
                for g in range(GROUPS):
                    mm = e.matmul(s_ps[n % 2][:, g, :], q[f][:, cut(g)], kv[f][:, cut(g)], start=True, stop=True)
                return mm

            def turn_v(e, k):
                for g in range(GROUPS):
                    mm = e.transpose(v_ps[:, g, :], kv[f][:, cut(g)], c.ident[:, :])
                return mm

            def mask_max(e, k):
                e.sem_inc(s_pad, 1)
                for g in range(GROUPS):
                    d = e.tensor_tensor_reduce(masked[n % 2][:, g, :], s_ps[n % 2][:, g, :], mask[:, :], 1.0, LOWEST,
                                               ALU.add, ALU.max, top[n % 2][:, g:g + 1])
                return d

            def exps(e, k):
                for g in range(GROUPS):
                    d = e.activation(ex[n % 4][:, g, :], masked[n % 2][:, g, :], ACT.Exp, bias=shift[n % 2][:, g:g + 1],
                                     scale=SCALE, accum_out=total[n % 4][:, g:g + 1])
                return d

            ready = (f"bkv3out",) if f else ("-ckv3out",)
            st.add(f"s{n}", "tensor", products, past("mm", n, 2), *(ready if t == 0 else ()))
            st.add(f"tv{n}", "tensor", turn_v, past("vt", n, 1))
            st.add(f"mm{n}", "vector", mask_max, f"s{n}", past("ex", n, 2))
            st.add(f"shift{n}", "vector", lambda e, k: e.tensor_scalar(
                shift[n % 2][:, :], top[n % 2][:, :], -SCALE, None, ALU.mult), f"mm{n}")
            st.add(f"ex{n}", "scalar", exps, f"shift{n}", past("norm", n, 4), past("rt", n, 4))
            st.add(f"vt{n}", "scalar", lambda e, k: e.activation(
                v_t[n % 4][:, :, :], v_ps[:, :, HD:P], ACT.Copy), f"tv{n}", past("o", n, 4))

        def normalised(n, late):
            st.add(f"rt{n}", "vector", lambda e, k: e.reciprocal(rtotal[n % 4][:, :], total[n % 4][:, :]),
                   f"ex{n}", past("norm", n, 4), late=late)
            st.add(f"norm{n}", "gpsimd", lambda e, k: e.tensor_tensor(
                prob[n % 4][:, :, :], ex[n % 4][:, :, :],
                rtotal[n % 4][:, :].unsqueeze(2).to_broadcast([P, GROUPS, P]), ALU.mult), f"rt{n}", past("tp", n, 4),
                late=late)

        def turned(n, late):
            def turn_p(e, k):
                for g in range(GROUPS):
                    mm = e.transpose(p_ps[:, g, :], prob[n % 4][:, g, :], c.ident[:, :])
                return mm

            st.add(f"tp{n}", "tensor", turn_p, f"norm{n}", past("pt", n, 1), late=late)
            st.add(f"pt{n}", "scalar", lambda e, k: e.activation(
                prob_t[n % 2][:, :, :], p_ps[:, :, :], ACT.Copy), f"tp{n}", past("o", n, 2), late=late)

        def outputs(n, late):
            f, t = n // 4, n % 4

            def products(e, k):
                for g in range(GROUPS):
                    for odd in range(2):
                        mm = e.matmul(o_ps[HD * odd:HD * odd + HD, g, :], v_t[n % 4][:, g, :],
                                      prob_t[n % 2][:, g, odd:P:2], start=True, stop=True, skip_group_check=True)
                return mm

            st.add(f"o{n}", "tensor", products, f"pt{n}", f"vt{n}", past("oc", n, 1), late=late)
            cut = slice(t * GROUPS * G, (t + 1) * GROUPS * G)
            st.add(f"oc{n}", "vector", lambda e, k: e.tensor_copy(
                o[f][:, :, cut].rearrange("r p t -> r t p"),
                o_ps[:, :, :].rearrange("r g (t p) -> r (g t) p", p=PAIRS)), f"o{n}", *((f"-y{f}",) if t == 0 else ()),
                late=late)

        def project_out(f, late):
            def products(e, k):
                for p in range(PAIRS):
                    mm = e.matmul(y_ps[:, :], wo[:, p, :], o[f][:, p, :], start=p == 0, stop=p == PAIRS - 1)
                return mm

            st.add(f"y{f}", "tensor", products, f"oc{4 * f + 3}", f"yc{f - 1}" if f else "-yc1",
                   late=late)
            st.add(f"yc{f}", "scalar", lambda e, k: e.activation(
                c.y[:, bass.ds(k * (2 * BLK) + f * BLK, BLK)], y_ps[:, :], ACT.Copy), f"y{f}", late=late)

        nexts = [project(st, "b", 1, lambda k: tokens(k, 1), lambda k: codes(k, 1),
                         {"bank": ("-ckv2out", "-ckv3out"), "q": ("-s7", "-tv7"), "kv": ("-s7", "-tv7")}),
                 project(st, "c", 0, lambda k: tokens(k, 2), lambda k: codes(k, 2),
                         {"bank": ("bkv2out", "bkv3out"), "q": ("s3", "tv3"), "kv": ("s3", "tv3")})]
        when = {0: (0, 0, 2), 1: (0, 2, 4), 2: (0, 4, 6), 4: (1, 0, 2), 5: (1, 2, 4), 6: (1, 4, 6)}
        for n in range(TURNS):
            scores(n)
            if n in when:
                which, lo, hi = when[n]
                for group in nexts[which][lo:hi]:
                    for step in group:
                        st.add(*step)
            for depth, add in ((1, normalised), (2, turned), (3, outputs)):
                add((n - depth) % TURNS, n < depth)
            if n in (3, 7):
                project_out(1 if n == 3 else 0, n == 3)
        st.run()


def norm_steps(st, tag, c, x, center, eps, out_name, finish, *after):
    cen, sq, sd, rs, pm, pv = (c.nb[tag][k] for k in ("cen", "sq", "sd", "rs", "pm", "pv"))
    weights = c.mean if center else c.ones
    if center:
        st.add(f"{tag}mean", "tensor", lambda e, k: e.matmul(pm[:, :], weights[:, :], x(k), start=True, stop=True),
               *after, f"-{tag}cen")
        st.add(f"{tag}cen", "vector", lambda e, k: e.tensor_tensor(cen[:, :], x(k), pm[:, :], ALU.subtract),
               f"{tag}mean", f"-{out_name}", f"-{tag}sq")
        src = lambda k: cen[:, :]
        last = (f"{tag}cen",)
    else:
        src, last = x, after
    st.add(f"{tag}sq", "scalar", lambda e, k: e.activation(sq[:, :], src(k), ACT.Square), *last, f"-{tag}var")
    st.add(f"{tag}var", "tensor", lambda e, k: e.matmul(pv[:, :], weights[:, :], sq[:, :], start=True, stop=True),
           f"{tag}sq", f"-{tag}sd")
    if center:
        st.add(f"{tag}sd", "scalar", lambda e, k: e.activation(sd[:, :], pv[:, :], ACT.Sqrt, bias=eps),
               f"{tag}var", f"-{tag}rs")
        st.add(f"{tag}rs", "vector", lambda e, k: e.reciprocal(rs[:, :], sd[:, :]), f"{tag}sd", f"-{out_name}")
    else:
        st.add(f"{tag}sd", "scalar", lambda e, k: e.activation(sd[:, :], pv[:, :], ACT.Sqrt),
               f"{tag}var", f"-{tag}clip")
        st.add(f"{tag}clip", "vector", lambda e, k: e.tensor_scalar(cen[:, :], sd[:, :], eps, None, ALU.max),
               f"{tag}sd", f"-{tag}rs")
        st.add(f"{tag}rs", "vector", lambda e, k: e.reciprocal(rs[:, :], cen[:, :]), f"{tag}clip", f"-{out_name}")
    st.add(out_name, "vector", lambda e, k: finish(e, k, src(k), rs[:, :]), f"{tag}rs")


class Const:
    pass


def two_layers(nc, a, out):
    with ExitStack() as ctx:
        def sb(name, shape, dt=F32, at=ctx):
            return at.enter_context(nc.sbuf_tensor(name, shape, dt))

        c = Const()
        c.nb = {}
        c.ident = sb("ident", [P, P])
        c.diag = sb("diag", [KT, LEN])
        c.ones = sb("ones", [P, P])
        c.mean = sb("mean", [P, P])
        c.y = sb("y", [P, TOKENS])
        x = sb("x", [P, CHUNKS, CH])
        xn = sb("xn", [P, CHUNKS, HALO + CH])
        xr = sb("xr", [P, CHUNKS, CH])
        eps = sb("eps", [P, 1])
        cols = sb("cols", [P, 2 + 4 * HT + 1 + 1])
        s_in = ctx.enter_context(nc.semaphore("s_in"))

        with nc.Block() as block:
            @block.sync
            def _(eng):
                loads = [(x[:, k, :], a["x"][:, k * CH:k * CH + CH]) for k in range(CHUNKS)]
                loads += [(c.ident[:, :], a["ident"]), (c.diag[:, :], a["diag"]), (cols[:, :], a["cols"])]
                for to, of in loads:
                    eng.dma_start(to, of).then_inc(s_in, 16)
                eng.wait_ge(s_in, 16 * len(loads))

            @block.gpsimd
            def _(eng):
                eng.memset(c.ones[:, :], 1.0)
                eng.memset(c.mean[:, :], 1.0 / P)
                eng.memset(eps[:, :], LN_EPS)
                eng.memset(xn[:, 0, 0:HALO], 0.0)
                eng.memset(xn[:, HALVES, 0:HALO], 0.0)

        with ExitStack() as moe:
            weights_t = sb("weights_t", [CW, CHUNKS, CH], F32R, moe)
            first_norm(nc, c, a, x, xn, eps, weights_t)
            head_attention(nc, c, a, xn)
            moe_ffn(nc, c, a, x, xn, xr, eps, cols, weights_t)
        c.src = lambda seq: xr[:, bass.ds(seq * HALVES, HALVES), :]
        attention(nc, c, lambda p: a["w1"][bass.ds(p, 1), :, :].rearrange("o k n -> (o k) n"),
                  lambda p: a["wo1"][bass.ds(p, 1), :, :].rearrange("o k n -> (o k) n"))
        mlp_ffn(nc, c, a, x, xn, cols, out)


def norm_buffers(nc, ctx, c, tags, names):
    for tag in tags:
        c.nb[tag] = {k: ctx.enter_context(nc.sbuf_tensor(f"{tag}{k}{names}", [P, CH], F32))
                     for k in ("cen", "sq", "sd", "rs")}


def first_norm(nc, c, a, x, xn, eps, weights_t):
    with ExitStack() as ctx:
        def sb(name, shape, dt=F32):
            return ctx.enter_context(nc.sbuf_tensor(name, shape, dt))

        def ps(name, shape):
            return ctx.enter_context(nc.psum_tensor(name, shape, F32))

        SENT = 8
        norm_buffers(nc, ctx, c, ("n0",), "")
        c.nb["n0"].update(pm=ps("n0pm", [P, CH]), pv=ps("n0pv", [P, CH]))
        cur = sb("cur", [P, CH])
        rw = sb("rw", [P, EXPERTS])
        rb = sb("rb", [P, TT, EXPERTS])
        lg = sb("lg", [P, TT, EXPERTS])
        top = sb("top", [P, TT])
        sh = sb("sh", [P, TT, EXPERTS])
        ex = sb("ex", [P, TT, EXPERTS])
        sm = sb("sm", [P, TT])
        rsm = sb("rsm", [P, TT])
        pr = sb("pr", [P, TT, EXPERTS + SENT])
        m8 = sb("m8", [P, TT, 8])
        rep = sb("rep", [P, TT, EXPERTS + SENT])
        two = sb("two", [P, TT])
        rtwo = sb("rtwo", [P, TT])
        mask = sb("mask", [P, TT, EXPERTS])
        wt = sb("wt", [P, TT, EXPERTS])
        cm = sb("cm", [P, TT, CW])
        r_ps = ps("r_ps", [P, TT, EXPERTS])
        t_ps = ps("t_ps", [CW, TT, P])
        s_l = ctx.enter_context(nc.semaphore("s_l"))
        s_pad = ctx.enter_context(nc.semaphore("s_pad"))
        with nc.Block() as block:
            @block.sync
            def _(eng):
                eng.dma_start(rw[:, :], a["rw"]).then_inc(s_l, 16)
                eng.dma_start(rb[:, :, :], a["rb"].rearrange("p (t n) -> p t n", t=TT)).then_inc(s_l, 16)
                eng.wait_ge(s_l, 32)

            @block.gpsimd
            def _(eng):
                eng.memset(pr[:, :, EXPERTS:], -2.0)
                eng.memset(cm[:, :, EXPERTS + 1:LO], 0.0)
                eng.memset(cm[:, :, LO + EXPERTS:], 0.0)
                eng.memset(cm[:, :, EXPERTS:EXPERTS + 1], 1.0)

        def wide(v):
            return v[:, :].unsqueeze(2).to_broadcast([P, TT, EXPERTS])

        st = Steps(nc, "fn", ctx)
        norm = Recorded()
        norm_steps(norm, "n0", c, lambda k: x[:, bass.ds(k, 1), :].rearrange("p o n -> p (o n)"), True, eps[:, :], "cur",
                   lambda e, k, cen, rs: e.tensor_tensor(cur[:, :], cen, rs, ALU.mult), "-logits", "-keep")
        norm.add("keep", "gpsimd", lambda e, k: e.tensor_copy(
            xn[:, bass.ds(k, 1), HALO:].rearrange("p o n -> p (o n)"), cur[:, :]), "cur")

        def logits(e, k):
            for t in range(TT):
                mm = e.matmul(r_ps[:, t, :], cur[:, t * P:t * P + P], rw[:, :], start=True, stop=True)
            return mm

        def each(f):
            def emit(e, k):
                e.sem_inc(s_pad, 1)
                for t in range(TT):
                    i = f(e, t)
                return i
            return emit

        E = slice(0, EXPERTS)
        norm.add("logits", "tensor", logits, "cur", "-lg")
        router = Recorded()
        router.add("lg", "vector", lambda e, k: e.tensor_tensor(lg[:, :, :], r_ps[:, :, :], rb[:, :, :], ALU.add),
               "logits", "-sh")
        router.add("top", "vector", lambda e, k: e.reduce_max(top[:, :], lg[:, :, :], AX_X), "lg", "-sh")
        router.add("sh", "vector", lambda e, k: e.tensor_tensor(sh[:, :, :], lg[:, :, :], wide(top), ALU.subtract),
               "top", "-ex")
        router.add("ex", "scalar", lambda e, k: e.activation(ex[:, :, :], sh[:, :, :], ACT.Exp), "sh", "-pr")
        router.add("sm", "vector", lambda e, k: e.reduce_sum(sm[:, :], ex[:, :, :], AX_X), "ex", "-rsm")
        router.add("rsm", "vector", lambda e, k: e.reciprocal(rsm[:, :], sm[:, :]), "sm", "-pr")
        router.add("pr", "vector", lambda e, k: e.tensor_tensor(pr[:, :, E], ex[:, :, :], wide(rsm), ALU.mult),
               "rsm", "-wt")
        router.add("m8", "vector", each(lambda e, t: e.max(m8[:, t, :], pr[:, t, E])), "pr", "-two")
        router.add("m8b", "vector", lambda e, k: e.memset(m8[:, :, 2:8], -2.0), "m8")
        router.add("rep", "vector", each(lambda e, t: e.match_replace(rep[:, t, :], m8[:, t, :], pr[:, t, :], -1.0)),
               "m8b", "-mask")
        router.add("two", "vector", lambda e, k: e.reduce_sum(two[:, :], m8[:, :, 0:2], AX_X), "m8b", "-rtwo0")
        router.add("rtwo0", "vector", lambda e, k: e.tensor_scalar(top[:, :], two[:, :], 1e-6, None, ALU.add), "two", "sh")
        router.add("rtwo", "vector", lambda e, k: e.reciprocal(rtwo[:, :], top[:, :]), "rtwo0", "-cmw")
        router.add("mask", "vector", lambda e, k: e.tensor_scalar(mask[:, :, :], rep[:, :, E], 0.0, None, ALU.is_lt),
               "rep", "-wt")
        router.add("wt", "vector", lambda e, k: e.tensor_tensor(wt[:, :, :], mask[:, :, :], pr[:, :, E], ALU.mult),
               "mask", "-cmw")
        router.add("cmw", "vector", lambda e, k: e.tensor_tensor(ex[:, :, :], wt[:, :, :], wide(rtwo), ALU.mult),
               "wt", "rtwo", "pr")
        router.add("hi", "vector", lambda e, k: e.tensor_copy(cm[:, :, E].bitcast(F32R), ex[:, :, :]), "cmw", "-turn")
        router.add("lo", "vector", lambda e, k: e.tensor_tensor(cm[:, :, LO:LO + EXPERTS].bitcast(F32R), ex[:, :, :],
                                                            cm[:, :, E], ALU.subtract), "hi")

        def turn(e, k):
            for t in range(TT):
                mm = e.transpose(t_ps[:, t, :], cm[:, t, :], c.ident[:, :])
            return mm

        router.add("turn", "tensor", turn, "lo", "-keep_w")
        router.add("keep_w", "vector", lambda e, k: e.tensor_copy(
            weights_t[:, bass.ds(k, 1), :].rearrange("p o n -> p (o n)"),
            t_ps[:, :, :].rearrange("p t n -> p (t n)")), "turn")
        for step in norm.list:
            st.add(*step)
            router.take(st, 2)
        router.take(st, len(router.list))
        st.run()
        with nc.Block() as block:
            @block.gpsimd
            def _(eng):
                for k in range(1, CHUNKS, HALVES):
                    eng.tensor_copy(xn[:, k, 0:HALO], xn[:, k - 1, CH:CH + HALO])


def moe_ffn(nc, c, a, x, xn, xr, eps, cols, weights_t):
    with ExitStack() as ctx:
        def sb(name, shape, dt=F32):
            return ctx.enter_context(nc.sbuf_tensor(name, shape, dt))

        def ps(name):
            return ctx.enter_context(nc.psum_tensor(name, [P, CH], F32))

        wg, wu, wd = (sb(n, [P, EPAIRS, P]) for n in ("wg", "wu", "wd"))
        wc = sb("wc", [P, HALO, P])
        sel_f = sb("sel_f", [CW, EPAIRS + 1, P])
        sel = sb("sel", [CW, EPAIRS + 1, P], F32R)
        gcol = sb("gcol", [P, 1])
        g_ps, u_ps, w_ps = ([ps(f"{n}{i}") for i in range(2)] for n in ("g_ps", "u_ps", "w_ps"))
        y_ps, n_ps = ps("y_ps"), ps("n_ps")
        sg, su, h = ([sb(f"{n}{i}", [P, CH]) for i in range(2)] for n in ("sg", "su", "h"))
        own, gate, res = sb("own", [P, CH]), sb("gate", [P, CH]), sb("res", [P, CH])
        s_l = ctx.enter_context(nc.semaphore("s_l2"))
        norm_buffers(nc, ctx, c, ("n1", "r1"), "")
        c.nb["n1"].update(pm=n_ps, pv=n_ps)
        c.nb["r1"].update(pm=n_ps, pv=n_ps)
        with nc.Block() as block:
            @block.sync
            def _(eng):
                for t, n in ((wg, "wg"), (wu, "wu"), (wd, "wd"), (wc, "wc"), (sel_f, "sel")):
                    eng.dma_start(t[:, :, :], a[n].rearrange("k (e n) -> k e n", n=P)).then_inc(s_l, 16)
                eng.wait_ge(s_l, 80)
        with nc.Block() as block:
            @block.vector
            def _(eng):
                eng.tensor_copy(sel[:, :, :], sel_f[:, :, :])
                eng.tensor_scalar(gcol[:, :], cols[:, 1:2], 1.0, float(P) ** 0.5, ALU.add, ALU.mult)

        def flat(t, k, cut=slice(None)):
            return t[:, bass.ds(k, 1), cut].rearrange("p o n -> p (o n)")

        now = slice(HALO, HALO + CH)
        st = Steps(nc, "moe", ctx)
        norms = Recorded()
        norm_steps(norms, "n1", c, lambda k: flat(x, k), True, eps[:, :], "xn1",
                   lambda e, k, cen, rs: e.tensor_tensor(flat(xn, k, now), cen, rs, ALU.mult),
                   "xnew", f"u{EPAIRS - 1}", f"g{EPAIRS - 1}", "own", "-r1sd")
        norm_steps(norms, "r1", c, lambda k: flat(xn, k, now), False, RMS_EPS, "xr1",
                   lambda e, k, v, rs: e.scalar_tensor_tensor(out=flat(xr, k), in0=v, scalar=gcol[:, :], in1=rs,
                                                              op0=ALU.mult, op1=ALU.mult), "xn1", "n1sd")
        for e in range(EPAIRS):
            b = e % 2

            def gates(eng, k, e=e, b=b):
                taps = [(wg[:, e, :], now)]
                if e == EPAIRS - 1:
                    taps += [(wc[:, t, :], slice(t, t + CH)) for t in range(HALO)]
                for n, (w, cut) in enumerate(taps):
                    mm = eng.matmul(g_ps[b][:, :], w, flat(xn, k, cut), start=n == 0, stop=n == len(taps) - 1)
                return mm

            old = "" if e >= 2 else "-"
            o = (e - 2) % EPAIRS
            st.add(f"g{e}", "tensor", gates, f"{old}sg{o}", *(("-xnew",) if e == 0 else ()))
            st.add(f"u{e}", "tensor", lambda eng, k, e=e, b=b: eng.matmul(
                u_ps[b][:, :], wu[:, e, :], flat(xn, k, now), start=True, stop=True), f"{old}su{o}")
            st.add(f"w{e}", "tensor", lambda eng, k, e=e, b=b: eng.matmul(
                w_ps[b][:, :], sel[:, e, :], flat(weights_t, k), start=True, stop=True),
                f"{old}h{o}", *(("-own",) if e == 0 else ()))
            st.add(f"sg{e}", "scalar", lambda eng, k, b=b: eng.activation(sg[b][:, :], g_ps[b][:, :], ACT.Silu),
                   f"g{e}", f"{old}su{o}")
            st.add(f"su{e}", "vector", lambda eng, k, b=b: eng.tensor_tensor(
                su[b][:, :], sg[b][:, :], u_ps[b][:, :], ALU.mult), f"sg{e}", f"u{e}", f"{old}h{o}")
            st.add(f"h{e}", "vector", lambda eng, k, b=b: eng.tensor_tensor(
                h[b][:, :], su[b][:, :], w_ps[b][:, :], ALU.mult), f"su{e}", f"w{e}", f"{old}y{o}")
            for d in ([e - 1] if e else []) + ([e] if e == EPAIRS - 1 else []):
                st.add(f"y{d}", "tensor", lambda eng, k, d=d: eng.matmul(
                    y_ps[:, :], wd[:, d, :], h[d % 2][:, :], start=d == 0, stop=d == EPAIRS - 1),
                    f"h{d}", *(("-sum",) if d == 0 else ()))
            norms.take(st, 2)
        st.add("w8", "tensor", lambda eng, k: eng.matmul(
            w_ps[0][:, :], sel[:, EPAIRS, :], flat(weights_t, k), start=True, stop=True), f"h{EPAIRS - 2}")
        st.add("own", "vector", lambda eng, k: eng.tensor_tensor(own[:, :], flat(xn, k, now), w_ps[0][:, :], ALU.mult),
               "w8", "-sum")
        st.add("sum", "vector", lambda eng, k: eng.tensor_tensor(res[:, :], own[:, :], y_ps[:, :], ALU.add),
               "own", f"y{EPAIRS - 1}", "-gate")
        st.add("gate", "scalar", lambda eng, k: eng.activation(gate[:, :], res[:, :], ACT.Silu), "sum", "-gated")
        st.add("gated", "vector", lambda eng, k: eng.scalar_tensor_tensor(
            out=own[:, :], in0=c.y[:, bass.ds(k * CH, CH)], scalar=cols[:, 0:1], in1=gate[:, :],
            op0=ALU.add, op1=ALU.mult), "gate", "sum")
        st.add("xnew", "vector", lambda eng, k: eng.tensor_tensor(flat(x, k), flat(x, k), own[:, :], ALU.add),
               "gated")
        st.run()


def mlp_ffn(nc, c, a, x, xn, cols, out):
    with ExitStack() as ctx:
        def sb(name, shape, dt=F32):
            return ctx.enter_context(nc.sbuf_tensor(name, shape, dt))

        m1, m2 = sb("m1", [P, HID]), sb("m2", [P, HID])
        h1, h2, m3 = sb("m_h1", [P, HT, HID]), sb("m_h2", [P, HT, HID]), sb("m3", [P, HT, P])
        bank = [ctx.enter_context(nc.psum_tensor(f"bank{i}", [P, CH], F32)) for i in range(8)]
        sg = [sb(f"sgm{i}", [P, CH]) for i in range(2)]
        act = [[sb(f"act{i}{m}", [P, CH]) for m in range(HT)] for i in range(3)]
        gate, res, fin = sb("gate_m", [P, CH]), sb("res_m", [P, CH]), [sb(f"fin{i}", [P, CH]) for i in range(1)]
        s_l = ctx.enter_context(nc.semaphore("s_l3"))
        with nc.Block() as block:
            @block.sync
            def _(eng):
                for t, n in ((m1, "m1"), (m2, "m2")):
                    eng.dma_start(t[:, :], a[n]).then_inc(s_l, 16)
                for t, n in ((h1, "h1"), (h2, "h2"), (m3, "m3")):
                    eng.dma_start(t[:, :, :], a[n].rearrange("k (t n) -> k t n", t=HT)).then_inc(s_l, 16)
                eng.wait_ge(s_l, 80)

        def col(n, m):
            return cols[:, 2 + n * HT + m:3 + n * HT + m]

        def cur(k):
            return xn[:, bass.ds(k, 1), HALO:].rearrange("p o n -> p (o n)")

        st = Steps(nc, "mlp", ctx)
        last = {}
        turn = [0]

        def take():
            b = turn[0] % 8
            turn[0] += 1
            return b

        def freed(b):
            return last.get(b, f"-{final[b]}")

        names = []
        for m in range(HT):
            names += [f"s{m}", f"t{m}"]
        names += [f"a{i}{m}" for i in (1, 2) for m in range(HT)] + ["gate"]
        final = {n % 8: name for n, name in enumerate(names)}

        for m in range(HT):
            ba, bb = take(), take()
            st.add(f"p{m}", "tensor", lambda e, k, m=m, ba=ba: e.matmul(
                bank[ba][:, :], m1[:, m * P:m * P + P], cur(k), start=True, stop=True), freed(ba))
            st.add(f"q{m}", "tensor", lambda e, k, m=m, bb=bb: e.matmul(
                bank[bb][:, :], m2[:, m * P:m * P + P], cur(k), start=True, stop=True), freed(bb))
            last[ba], last[bb] = f"s{m}", f"t{m}"
            old = f"t{m - 2}" if m >= 2 else f"-t{m + 2}"
            st.add(f"s{m}", "scalar", lambda e, k, m=m, ba=ba: e.activation(
                sg[m % 2][:, :], bank[ba][:, :], ACT.Silu, scale=col(0, m)), f"p{m}", old)
            st.add(f"t{m}", "vector", lambda e, k, m=m, bb=bb: e.scalar_tensor_tensor(
                out=act[0][m][:, :], in0=bank[bb][:, :], scalar=col(1, m), in1=sg[m % 2][:, :],
                op0=ALU.mult, op1=ALU.mult), f"s{m}", f"q{m}", f"-r1{HT - 1}")
        for i, w in ((1, h1), (2, h2)):
            for m in range(HT):
                b = take()

                def layer(e, k, i=i, w=w, m=m, b=b):
                    for j in range(HT):
                        mm = e.matmul(bank[b][:, :], w[:, j, m * P:m * P + P], act[i - 1][j][:, :],
                                      start=j == 0, stop=j == HT - 1)
                    return mm

                inputs = [f"t{j}" if i == 1 else f"a1{j}" for j in range(HT)]
                st.add(f"r{i}{m}", "tensor", layer, freed(b), *inputs)
                last[b] = f"a{i}{m}"
                reader = f"-r2{HT - 1}" if i == 1 else "-r3"
                st.add(f"a{i}{m}", "scalar", lambda e, k, i=i, m=m, b=b: e.activation(
                    act[i][m][:, :], bank[b][:, :], ACT.Gelu, scale=col(1 + i, m)), f"r{i}{m}", reader)
        b = take()

        def last_layer(e, k):
            for j in range(HT):
                mm = e.matmul(bank[b][:, :], m3[:, j, :], act[2][j][:, :], start=j == 0, stop=j == HT - 1)
            return mm

        st.add("r3", "tensor", last_layer, freed(b), *[f"a2{j}" for j in range(HT)])
        st.add("gate", "scalar", lambda e, k: e.activation(gate[:, :], bank[b][:, :], ACT.Silu, scale=col(4, 0)),
               "r3", "-mul")
        st.add("mul", "vector", lambda e, k: e.tensor_tensor(res[:, :], c.y[:, bass.ds(k * CH, CH)], gate[:, :], ALU.mult),
               "gate", "-fin")
        st.add("fin", "vector", lambda e, k: e.tensor_tensor(
            fin[0][:, :], x[:, bass.ds(k, 1), :].rearrange("p o n -> p (o n)"), res[:, :], ALU.add), "mul", "-store")
        st.add("store", "sync", lambda e, k: e.dma_start(out[:, bass.ds(k * CH, CH)], fin[0][:, :]), "fin")
        st.run()


def kernel(**inputs):
    import numpy as np
    import concourse.bacc as bacc
    from concourse.bass_utils import run_bass_kernel_spmd

    i = {k: np.asarray(v) for k, v in inputs.items()}
    f = np.float32
    a = {"x": i["L0_attn_x"].reshape(TOKENS, P).T}

    w = i["L0_attn_w_qkv"].reshape(P, HEADS, 3, HD)
    b = i["L0_attn_b_qkv"].reshape(HEADS, 3, HD)
    a["wq0"] = w[:, :, 0].reshape(P, -1)
    a["wkv0"] = w[:, :, 1:].reshape(P, -1)
    a["bq0"] = b[:, 0].reshape(PAIRS, P).T
    a["bkv0"] = b[:, 1:].reshape(HEADS, P).T
    a["wo0"] = i["L0_attn_w_out"].reshape(PAIRS, P, P).transpose(1, 0, 2).reshape(P, -1)

    w = i["L1_attn_w_qkv"].reshape(P, 3, HEADS, HD)
    a["w1"] = np.zeros((PAIRS, P, W_V), f)
    for p in range(PAIRS):
        for n in range(2):
            for h in range(2):
                at = n * P + h * HD
                a["w1"][p, :, at:at + HD] = w[:, n, 2 * p + h]
        a["w1"][p, :, W_QK:] = w[:, 2, 2 * p:2 * p + 2].reshape(P, P)
    a["wo1"] = i["L1_attn_w_out"].reshape(PAIRS, P, P)

    a["rw"] = i["L0_ffn_router_w"]
    a["rb"] = np.tile(i["L0_ffn_router_bias"], (P, TT))
    conv = i["L0_ffn_conv_w"]
    for n, name, shared in (("wg", "gate", conv[:, :, HALO].T), ("wu", "up", i["L0_ffn_shared_up_w"])):
        each = list(i[f"L0_ffn_expert_{name}_w"]) + [shared]
        a[n] = np.concatenate(each, axis=1)
    down = list(i["L0_ffn_expert_down_w"]) + [i["L0_ffn_shared_down_w"]]
    a["wd"] = np.concatenate([np.concatenate(down[2 * e:2 * e + 2], axis=0) for e in range(EPAIRS)], axis=1)
    a["wc"] = np.zeros((P, HALO * P), f)
    for t in range(HALO):
        a["wc"][:, t * P + HD:(t + 1) * P] = conv[:, :, t].T
    cols = [i["L0_attn_b_out"][:, None], i["L1_attn_gamma"][:, None]]
    for n in ("w1", "w2", "h1", "h2"):
        cols.append(i[f"L1_ffn_{n}_s"].reshape(HT, P).T)
    cols += [i["L1_ffn_w3_s"][:, None], np.zeros((P, 1), f)]
    a["cols"] = np.concatenate(cols, axis=1)
    a["m1"], a["m2"] = i["L1_ffn_w1_w"].T, i["L1_ffn_w2_w"].T
    for n, name in (("h1", "h1"), ("h2", "h2"), ("m3", "w3")):
        t = i[f"L1_ffn_{name}_w"].T
        a[n] = t.reshape(HT, P, -1).transpose(1, 0, 2).reshape(P, -1)

    a["ident"] = np.eye(P, dtype=f)
    a["diag"] = np.repeat(np.eye(KT, dtype=f), P, axis=1)
    sel = np.zeros((CW, EPAIRS + 1, P), f)
    for e in range(EXPERTS):
        rows = [e, LO + e] if e < EXPERTS - 1 else [EXPERTS]
        sel[rows, e // 2, (e % 2) * HD:(e % 2 + 1) * HD] = 1.0
    sel[[EXPERTS - 1, LO + EXPERTS - 1], EPAIRS, :] = 1.0
    a["sel"] = sel.reshape(CW, -1)
    steps = np.exp(np.arange(0, HD, 2, dtype=f) * f(-(np.log(10000.0) / HD)))
    angle = np.arange(LEN, dtype=f)[:, None] * steps
    pos = np.zeros((LEN, HD), f)
    pos[:, 0::2], pos[:, 1::2] = np.sin(angle), np.cos(angle)
    a["pos"] = np.zeros((P, LEN), f)
    a["pos"][0:HD] = pos.T
    tokens = np.arange(P) // HEADS
    a["mask"] = np.where(tokens[:, None] == tokens, 0.0, LOWEST).astype(f)

    nc = bacc.Bacc("TRN2", target_bir_lowering=False, num_devices=1)
    arrays, args = {}, {}
    for n, v in a.items():
        v = np.ascontiguousarray(v)
        arrays[f"in_{n}"] = v
        args[n] = nc.dram_tensor(f"in_{n}", v.shape, mybir.dt.from_np(v.dtype), kind="ExternalInput").ap()
    out = nc.dram_tensor("out", (P, TOKENS), F32, kind="ExternalOutput").ap()
    two_layers(nc, args, out)
    r = run_bass_kernel_spmd(nc, [arrays], core_ids=[0])
    return r.results[0]["out"].T.reshape(SEQS, LEN, P)
```

```python
from contextlib import ExitStack

import concourse.bass as bass
from concourse import mybir

F32 = mybir.dt.float32
F32R = mybir.dt.float32r
ACT = mybir.ActivationFunctionType
ALU = mybir.AluOpType
AX_X = mybir.AxisListType.X

P = 128
SEQS, LEN = 2, 1024
TOKENS = SEQS * LEN
CH = 512
CHUNKS = TOKENS // CH
HALVES = LEN // CH
HEADS, HD = 16, 64
PAIRS = HEADS // 2
STEPS = SEQS * PAIRS
KT = LEN // P
TT = CH // P
EXPERTS = 16
EPAIRS = EXPERTS // 2
HALO = 2
HID = 512
HT = HID // P
MOE_LATE = (0, 2, 2, 3, 3, 3, 3, 3)
MOE_W = {"wg": EPAIRS * P, "wu": EPAIRS * P, "wd": EPAIRS * P, "wc": HALO * P}
LOWEST = -3.0e38
LN_EPS = 1e-5
RMS_EPS = 1e-12
SCALE = HD ** -0.5
CW = 128
LO = 32

W_QK = 2 * P
W_V = W_QK + P



class Counter:

    def __init__(self, sem, per, ahead=0):
        self.sem, self.per, self.ahead = sem, per, ahead

    def wait(self, eng, period, n):
        value = period * self.per + n + self.ahead
        if not isinstance(value, int) or value > self.ahead:
            eng.wait_ge(self.sem, value)


class Steps:

    ENGINES = ("tensor", "vector", "scalar", "gpsimd", "sync")

    def __init__(self, nc, name, ctx, periods=CHUNKS):
        self.nc, self.list, self.at, self.periods = nc, [], {}, periods
        self.name, self.ctx, self.count, self.sem = name, ctx, {}, {}

    def add(self, name, engine, emit, *after, late=False):
        assert name not in self.at
        key = (engine, late)
        if key not in self.sem:
            self.count[key] = 0
            self.sem[key] = self.ctx.enter_context(self.nc.semaphore(f"{self.name}_{engine}{'_late' if late else ''}"))
        self.count[key] += 16 if engine == "sync" else 1
        self.at[name] = (key, self.count[key])
        self.list.append((name, key, emit, after))

    def run(self, before={}):
        with self.nc.Block() as block:
            programs = {"tensor": block.tensor, "vector": block.vector, "scalar": block.scalar,
                        "gpsimd": block.gpsimd, "sync": block.sync}
            for engine, program in programs.items():
                if any(engine == of for of, _ in self.sem):
                    program(lambda eng, engine=engine: self._run(eng, engine, before.get(engine)))

    def _run(self, eng, engine, before):
        for late in (False, True):
            if (engine, late) in self.sem:
                eng.sem_inc(self.sem[engine, late], self.count[engine, late])
        if before:
            before(eng)
        if any(late for _, late in self.sem):
            self._period(eng, engine, 0, (False,))
            with eng.Fori(1, self.periods) as period:
                self._period(eng, engine, period, (False, True))
            self._period(eng, engine, self.periods, (True,))
        elif self.periods == 1:
            self._period(eng, engine, 0, (False,))
        else:
            with eng.Fori(0, self.periods) as period:
                self._period(eng, engine, period, (False,))
        if engine == "sync":
            for key in self.sem:
                if key[0] == engine:
                    eng.wait_ge(self.sem[key], (self.periods + 1) * self.count[key])

    def _period(self, eng, engine, period, lates):
        for name, key, emit, after in self.list:
            if key[0] != engine or key[1] not in lates:
                continue
            chunk = period - 1 if key[1] else period
            latest = {}
            for what in after:
                of, n = self.at[what.lstrip("-")]
                latest[of] = max(latest.get(of, (0, 0)), (0 if what.startswith("-") else 1, n))
            for of, (this, n) in latest.items():
                eng.wait_ge(self.sem[of], (chunk + this) * self.count[of] + n)
            emit(eng, chunk).then_inc(self.sem[key], 16 if engine == "sync" else 1)


class Recorded:

    def __init__(self):
        self.list = []

    def add(self, *step):
        self.list.append(step)

    def take(self, st, n):
        for step in self.list[:n]:
            st.add(*step, late=True)
        self.list = self.list[n:]


def attention(nc, c, w_pair, w_out):
    with ExitStack() as ctx:
        def sb(name, shape, dt=F32):
            return ctx.enter_context(nc.sbuf_tensor(name, shape, dt))

        def ps(name, shape):
            return ctx.enter_context(nc.psum_tensor(name, shape, F32))

        def counter(name, per, ahead=0):
            return Counter(ctx.enter_context(nc.semaphore(name)), per, ahead)

        x_cur = sb("x_cur", [P, 2, LEN])
        w_cur = sb("w_cur", [P, 2, W_V])
        wo_cur = sb("wo_cur", [P, 2, P])
        q_a = sb("q_a", [P, 2, 2, LEN], F32R)
        k_a = sb("k_a", [P, 2, 2, LEN], F32R)
        q_b = sb("q_b", [P, 2, 2, LEN], F32R)
        k_b = sb("k_b", [P, 2, 2, LEN], F32R)
        own_rows = [slice(0, HD), slice(HD, P)]
        other_rows = [slice(HD, P), slice(0, HD)]
        v_cur = sb("v_cur", [P, 2, KT, P])
        RING = 8
        prob = sb("prob", [P, RING, CH])
        acc = sb("acc", [P, HALVES, 2, CH])
        mx_part = sb("mx_part", [P, 2, KT, 2])
        mx_row = sb("mx_row", [P, 2, KT])
        rden = sb("rden", [P, HALVES, CH])
        o_n = sb("o_n", [P, HALVES, CH])

        st_ps = ps("st_ps", [P, 2, CH])
        mx_ps = ps("mx_ps", [P, 2, CH])
        o_ps = ps("o_ps", [P, HALVES, CH])
        pj_ps = ps("pj_ps", [P, 2, CH])

        s_init = ctx.enter_context(nc.semaphore("s_init"))
        s_w = [counter(f"s_w{par}", 32) for par in range(2)]
        s_wo = [counter(f"s_wo{par}", 16) for par in range(2)]
        s_prep = counter("s_prep", 8)
        s_hi = counter("s_hi", 16)
        s_lo = counter("s_lo", 10)
        s_v = counter("s_v", 2)
        s_mx = counter("s_mx", 32)
        s_mxr = counter("s_mxr", 32)
        s_row = counter("s_row", 2)
        s_st = counter("s_st", 32)
        s_exp = counter("s_exp", 32)
        s_pv = counter("s_pv", 16)
        s_acc = counter("s_acc", 28)
        s_fin = counter("s_fin", 4, 4)
        s_den = counter("s_den", 2, 2)
        s_out = counter("s_out", 2, 2)
        s_rcp = counter("s_rcp", 8)
        s_on = counter("s_on", 2, 2)

        slots = [[] for _ in range(48)]
        QK_AT, DEN_AT, V_AT, TR_AT = (0, 4, 7, 11), (27, 3), (17, 19), (36, 46)
        RCP, NORM, OUT = 2, 9, 12
        for at, (t, half) in zip(QK_AT, ((0, 0), (1, 0), (1, 1), (0, 1))):
            slots[at].append(("qk", t, half))
        for half, at in enumerate(DEN_AT):
            slots[at].append(("den", half))
            for n in range(4):
                slots[at + 1 + RCP * n].append(("rcp", half, n))
            slots[at + NORM].append(("norm", half))
            slots[at + OUT].append(("out", half))
        for n, at in enumerate(V_AT):
            slots[at].append(("v", n))
        for n, at in enumerate([s for s in range(9, 48) if s not in (30, 34, 35)][:32]):
            slots[at].append(("tile", n))
        for h, at in enumerate(TR_AT):
            slots[at].append(("tr", h))
        tiles = [(h, i, 0) for h in range(2) for i in range(TT)]
        tiles += [(h, i, 1) for h in range(2) for i in range(TT)]
        tiles += [(h, i, keys) for h in range(2) for i in range(TT, KT) for keys in range(2)]
        UNITS = ("qk", "v", "tr", "den", "out")
        PREPARE = ("qk", "v", "tr", "tile")
        order = [u for slot in slots for u in slot if u[0] in UNITS]
        prepare = [u for u in order if u[0] in PREPARE]
        qks = [u for u in prepare if u[0] == "qk"]
        lows = [u for u in prepare if u[0] in ("qk", "tr") for _ in range(2 if u[0] == "qk" else 1)]
        last_low = {u: n + 1 for n, u in enumerate(lows)}
        assert len(order) % 2 == 0
        assert (len(prepare), len(lows), 4 * len(qks)) == (s_prep.per, s_lo.per, s_hi.per)

        def written(u, m):
            if u in prepare:
                return s_prep, m + 1, prepare.index(u) + 1
            return s_fin, m - u[1], 2 * u[1] + (u[0] == "out") + 1

        def read(u, m):
            if u[0] == "v":
                return s_v, m + 1, u[1] + 1
            if u in prepare:
                return s_lo, m + 1, last_low[u]
            return (s_den if u[0] == "den" else s_out), m - u[1], u[1] + 1

        def exists(u, m):
            if not isinstance(m, int):
                return True
            if u[0] in PREPARE:
                return -1 <= m < STEPS - 1
            return 0 <= m - u[1] < STEPS

        def bank(u):
            return order.index(u) % 2

        def wait(eng, event):
            event[0].wait(eng, event[1], event[2])

        def extras(slot, m):
            return [u for u in slots[slot] if exists(u, m)]

        def bank_free(eng, u, m):
            n, period = order.index(u) - 2, m
            for _ in range(2 * len(order)):
                if n < 0:
                    n, period = n + len(order), period - 1
                if exists(order[n], period):
                    return wait(eng, read(order[n], period))
                n -= 2

        def needed_adds(s):
            return 14 * (s // KT) + 2 * max(1, s % KT)

        def parts(m):
            if not isinstance(m, int):
                return True, True, True
            return 0 <= m < STEPS, m < STEPS - 1, m > 0

        def periods(eng, body):
            body(eng, -1, 1)
            body(eng, 0, 0)
            with eng.Fori(0, STEPS // 2 - 1) as i:
                body(eng, 2 * i + 1, 1)
                body(eng, 2 * i + 2, 0)
            body(eng, STEPS - 1, 1)
            body(eng, STEPS, 0)

        def pe(eng, m, par):
            own, prep, fin = parts(m)
            nxt = 1 - par

            def pv(step, period, par_v):
                half, j = step // KT, step % KT
                s_exp.wait(eng, period, 2 * step + 2)
                if j == 0:
                    s_on.wait(eng, period - 1, half + 1)
                for h in range(2):
                    mm = eng.matmul(o_ps[64 * h:64 * h + 64, half, :], v_cur[:, par_v, j, HD * h:HD * h + HD],
                                    prob[:, (2 * step + h) % RING, :], start=(j == 0), stop=(j == KT - 1),
                                    skip_group_check=True)
                mm.then_inc(s_pv.sem, 1)

            def unit(u):
                if u == prepare[0]:
                    s_w[nxt].wait(eng, (m + 1) // 2, 32)
                bank_free(eng, u, m)
                out = pj_ps[:, bank(u), :]
                if u[0] == "qk":
                    _, t, half = u
                    tok = slice(half * CH, half * CH + CH)
                    mm = eng.matmul(out, w_cur[:, nxt, t * P:t * P + P], x_cur[:, nxt, tok],
                                    start=True, stop=True)
                elif u[0] == "v":
                    for i in range(TT):
                        j = TT * u[1] + i
                        mm = eng.matmul(out[:, i * P:i * P + P], x_cur[:, nxt, j * P:j * P + P],
                                        w_cur[:, nxt, W_QK:W_V], start=True, stop=True)
                elif u[0] == "tr":
                    s_row.wait(eng, m + 1, u[1] + 1)
                    mm = eng.transpose(out[0:KT, 0:P], mx_row[:, u[1], :], c.ident[:, :])
                elif u[0] == "den":
                    s_acc.wait(eng, m - u[1], 14 * (u[1] + 1))
                    for h in range(2):
                        mm = eng.matmul(out[64 * h:64 * h + 64, :], c.ones[:, 0:64], acc[:, u[1], h, :],
                                        start=True, stop=True, skip_group_check=True)
                else:
                    q, par_q = m - u[1], par if u[1] == 0 else nxt
                    s_wo[par_q].wait(eng, q // 2, 16)
                    s_on.wait(eng, q, u[1] + 1)
                    mm = eng.matmul(out, wo_cur[:, par_q, :], o_n[:, u[1], :],
                                    start=True, stop=True)
                mm.then_inc(written(u, m)[0].sem, 1)

            def score_tile(n):
                h, i, keys = tiles[n]
                if n in (0, TT * 2, TT * 4):
                    wait(eng, read(qks[n // (TT * 2) + 1], m))
                s_mxr.wait(eng, m + 1, n - 1)
                eng.matmul(mx_ps[:, n % 2, :], q_a[:, nxt, h, i * P:i * P + P],
                           k_a[:, nxt, h, keys * CH:keys * CH + CH], start=True, stop=True)\
                   .then_inc(s_mx.sem, 1)

            def beside(slot):
                for u in extras(slot, m):
                    if u[0] in UNITS:
                        unit(u)
                    elif u[0] == "tile":
                        score_tile(u[1])

            for s in range(16):
                half, j = s // KT, s % KT
                if own and s == 0:
                    s_v.wait(eng, m, 2)
                for h in range(2):
                    if own and s == 0:
                        s_lo.wait(eng, m, 9 + h)
                    if own:
                        s_exp.wait(eng, m, 2 * s + h - 1)
                        keys, tok = slice(j * P, j * P + P), slice(half * CH, half * CH + CH)
                        eng.matmul(st_ps[:, h, :], k_a[:, par, h, keys], q_a[:, par, h, tok],
                                   start=True, stop=False)
                        eng.matmul(st_ps[:, h, :], k_b[:, par, h, keys], q_b[:, par, h, tok],
                                   start=False, stop=True).then_inc(s_st.sem, 1)
                    beside(3 * s + h)
                if s == 0 and fin:
                    pv(15, m - 1, nxt)
                if s > 0 and own:
                    pv(s - 1, m, par)
                beside(3 * s + 2)

        def act(eng, m, par):
            own, prep, fin = parts(m)
            nxt = 1 - par
            for slot in range(48):
                s, h = slot // 3, slot % 3
                if own and h < 2:
                    s_st.wait(eng, m, 2 * s + h + 1)
                    s_pv.wait(eng, m, s - 3)
                    s_acc.wait(eng, *((m, needed_adds(s - 4)) if s >= 4 else (m - 1, needed_adds(s + 12))))
                    eng.activation(prob[:, (2 * s + h) % RING, :], st_ps[:, h, :], ACT.Exp, scale=SCALE)\
                       .then_inc(s_exp.sem, 1)
                for u in extras(slot, m):
                    if u[0] == "qk":
                        _, t, half = u
                        if u == prepare[0]:
                            s_st.wait(eng, m, 0)
                        wait(eng, written(u, m))
                        tok = slice(half * CH, half * CH + CH)
                        to = q_a if t == 0 else k_a
                        for h in range(2):
                            second = q_b[own_rows[h], nxt, h, tok] if t == 0 else k_a[other_rows[h], nxt, h, tok]
                            for o in (to[own_rows[h], nxt, h, tok], second):
                                eng.activation(o, pj_ps[own_rows[h], bank(u), :], ACT.Copy).then_inc(s_hi.sem, 1)
                    elif u[0] == "den":
                        wait(eng, written(u, m))
                        s_on.wait(eng, m - u[1] - 1, u[1] + 1)
                        eng.activation(rden[:, u[1], :], pj_ps[:, bank(u), :], ACT.Copy).then_inc(s_den.sem, 1)
                    elif u[0] == "v":
                        if u[1] == 0:
                            s_pv.wait(eng, m, 0)
                        wait(eng, written(u, m))
                        eng.activation(v_cur[:, nxt, TT * u[1]:TT * u[1] + TT, :],
                                       pj_ps[:, bank(u), :].rearrange("p (t n) -> p t n", t=TT), ACT.Copy)\
                           .then_inc(s_v.sem, 1)

        def dve(eng, m, par):
            own, prep, fin = parts(m)
            nxt = 1 - par
            for slot in range(48):
                for u in extras(slot, m):
                    if u[0] in UNITS:
                        src = pj_ps[:, bank(u), :]
                    if u[0] == "qk":
                        _, t, half = u
                        tok = slice(half * CH, half * CH + CH)
                        for h in range(2):
                            s_hi.wait(eng, m + 1, 4 * qks.index(u) + 2 * (h + 1))
                            r = own_rows[h]
                            hi = (q_a if t == 0 else k_a)[r, nxt, h, tok]
                            out = q_a[other_rows[h], nxt, h, tok] if t == 0 else k_b[r, nxt, h, tok]
                            eng.tensor_tensor(out, src[r, :], hi.bitcast(F32), ALU.subtract).then_inc(s_lo.sem, 1)
                    elif u[0] == "tr":
                        wait(eng, written(u, m))
                        at = other_rows[u[1]].start
                        eng.tensor_tensor(
                            q_b[at:at + KT, nxt, u[1], :].rearrange("p (i n) -> p i n", i=KT),
                            src[0:KT, 0:P].unsqueeze(1).to_broadcast([KT, KT, P]),
                            c.diag[:, :].rearrange("p (i n) -> p i n", i=KT), ALU.mult).then_inc(s_lo.sem, 1)
                    elif u[0] == "rcp":
                        h, q = u[1], m - u[1]
                        s_den.wait(eng, q, h + 1)
                        part = rden[:, h, u[2] * P:u[2] * P + P]
                        eng.reciprocal(part, part).then_inc(s_rcp.sem, 1)
                    elif u[0] == "norm":
                        h, q = u[1], m - u[1]
                        s_rcp.wait(eng, q, 4 * (h + 1))
                        s_pv.wait(eng, q, KT * (h + 1))
                        s_fin.wait(eng, q - 1, 2 * h + 2)
                        eng.tensor_tensor(o_n[:, h, :], o_ps[:, h, :], rden[:, h, :], ALU.mult)\
                           .then_inc(s_on.sem, 1)
                    elif u[0] == "out":
                        h, q = u[1], m - u[1]
                        wait(eng, written(u, m))
                        s_out.wait(eng, q - 1, h + 1)
                        seq = q // PAIRS
                        y = c.y[:, bass.ds(seq * LEN + h * CH, CH)]
                        eng.tensor_tensor(y, src, y, ALU.add).then_inc(s_out.sem, 1)
                    elif u[0] == "tile":
                        n = u[1]
                        h, i, keys = tiles[n]
                        s_mx.wait(eng, m + 1, n + 1)
                        if (i, keys) == (0, 0):
                            s_row.wait(eng, m, h + 1)
                        eng.reduce_max(mx_part[:, h, i, keys:keys + 1], mx_ps[:, n % 2, :], AX_X)\
                           .then_inc(s_mxr.sem, 1)
                        if (i, keys) == (KT - 1, 1):
                            s_mxr.wait(eng, m + 1, n + 1)
                            s_prep.wait(eng, m, prepare.index(("tr", h)) + 1)
                            eng.reduce_max(mx_row[:, h, :], mx_part[:, h, :, :], AX_X).then_inc(s_row.sem, 1)

        def pool(eng, m, par):
            if not parts(m)[0]:
                return
            for s in range(16):
                half, j = s // KT, s % KT
                if j == 0:
                    continue
                for h in range(2):
                    s_exp.wait(eng, m, 2 * s + h + 1)
                    new, a = prob[:, (2 * s + h) % RING, :], acc[:, half, h, :]
                    if j == 1:
                        s_fin.wait(eng, m - 1, 2 * half + 1)
                        first = prob[:, (2 * s + h - 2) % RING, :]
                    else:
                        s_acc.wait(eng, m, 14 * half + 2 * (j - 1) + h - 1)
                        first = a
                    eng.tensor_tensor(a, first, new, ALU.add).then_inc(s_acc.sem, 1)

        def load(eng, p, par):
            pair, seq = p % PAIRS, p // PAIRS
            late = not isinstance(p, int)
            if late:
                s_prep.wait(eng, p - 2, prepare.index(("v", 1)) + 1)
            eng.dma_start(x_cur[:, par, :].rearrange("p (h n) -> p h n", h=HALVES), c.src(seq)).then_inc(s_w[par].sem, 16)
            eng.dma_start(w_cur[:, par, :], w_pair(pair)).then_inc(s_w[par].sem, 16)
            if late:
                s_fin.wait(eng, p - 2, 4)
            eng.dma_start(wo_cur[:, par, :], w_out(pair)).then_inc(s_wo[par].sem, 16)

        with nc.Block() as block:
            @block.sync
            def _(eng):
                load(eng, 0, 0)
                load(eng, 1, 1)

            @block.vector
            def _(eng):
                eng.memset(c.y[:, :], 0.0)
                for h in range(2):
                    eng.memset(q_b[other_rows[h], :, h, :].bitcast(F32), 0.0)
                for k in (s_on, s_out):
                    eng.sem_inc(k.sem, k.ahead)

            @block.tensor
            def _(eng):
                eng.sem_inc(s_fin.sem, s_fin.ahead)

            @block.scalar
            def _(eng):
                eng.sem_inc(s_den.sem, s_den.ahead)

            @block.gpsimd
            def _(eng):
                for h in range(2):
                    eng.memset(k_b[other_rows[h], :, h, :].bitcast(F32), 0.0).then_inc(s_init, 1)
                eng.wait_ge(s_init, 2)
                for h in range(2):
                    at = other_rows[h].start
                    eng.memset(k_b[at:at + KT, :, h, :].bitcast(F32), -1.0)

        with nc.Block() as block:
            @block.sync
            def _(eng):
                with eng.Fori(1, STEPS // 2) as i:
                    load(eng, 2 * i, 0)
                    load(eng, 2 * i + 1, 1)

            block.tensor(lambda eng: periods(eng, pe))
            block.scalar(lambda eng: periods(eng, act))
            block.vector(lambda eng: periods(eng, dve))
            block.gpsimd(lambda eng: periods(eng, pool))


HEAD_W = {"wq0": PAIRS * P, "wkv0": HEADS * P, "wo0": PAIRS * P, "bq0": PAIRS, "bkv0": HEADS, "pos": LEN, "mask": P}


def head_weights(nc, ctx):
    return ({n: ctx.enter_context(nc.sbuf_tensor("head_" + n, [P, size], F32)) for n, size in HEAD_W.items()},
            ctx.enter_context(nc.semaphore("s_head")))


def head_attention(nc, c, a, xn, w, s_head, mlp_w, s_mlp):
    BLK = 128
    TURNS = 8
    GROUPS = 4
    G = 8
    with ExitStack() as ctx:
        def sb(name, shape, dt=F32):
            return ctx.enter_context(nc.sbuf_tensor("ha_" + name, shape, dt))

        def ps(name, shape):
            return ctx.enter_context(nc.psum_tensor("ha_" + name, shape, F32))

        wq, wkv, wo = (w[n][:, :].rearrange("k (h n) -> k h n", n=P)
                       for n in ("wq0", "wkv0", "wo0"))
        bq, bkv, mask = w["bq0"], w["bkv0"], w["mask"]
        pos = w["pos"]
        q = [sb(f"q{i}", [P, BLK * HEADS]) for i in range(2)]
        kv = [sb(f"kv{i}", [P, BLK * HEADS]) for i in range(2)]
        masked = [sb(f"masked{i}", [P, GROUPS, P]) for i in range(2)]
        top = [sb(f"top{i}", [P, GROUPS]) for i in range(2)]
        shift = [sb(f"shift{i}", [P, GROUPS]) for i in range(2)]
        total = [sb(f"total{i}", [P, GROUPS]) for i in range(4)]
        rtotal = [sb(f"rtotal{i}", [P, GROUPS]) for i in range(4)]
        ex = [sb(f"ex{i}", [P, GROUPS, P]) for i in range(4)]
        prob = [sb(f"prob{i}", [P, GROUPS, P]) for i in range(4)]
        prob_t = [sb(f"prob_t{i}", [P, GROUPS, P]) for i in range(2)]
        v_t = [sb(f"v_t{i}", [P, GROUPS, HD]) for i in range(4)]
        o = [sb(f"o{i}", [P, PAIRS, BLK]) for i in range(2)]
        pj_ps = [ps(f"pj_ps{i}", [P, 4, BLK]) for i in range(2)]
        s_ps = [ps(f"s_ps{i}", [P, GROUPS, P]) for i in range(2)]
        v_ps, p_ps = ps("v_ps", [P, GROUPS, P]), ps("p_ps", [P, GROUPS, P])
        o_ps, y_ps = ps("o_ps", [P, GROUPS, G * PAIRS]), ps("y_ps", [P, BLK])
        s_pad = ctx.enter_context(nc.semaphore("s_pad0"))

        with nc.Block() as block:
            @block.sync
            def _(eng):
                for n, t in mlp_w.items():
                    eng.dma_start(t[:, :, :], a[n].rearrange("k (t n) -> k t n", t=t.shape[1])).then_inc(s_mlp, 16)
                eng.wait_ge(s_head, 16 * len(w))

            @block.vector
            def _(eng):
                for i in range(2):
                    eng.memset(q[i][HD:P, :], 0.0)

        def project(st, tag, to, x_at, pos_at, free):
            q_out = q[to][0:HD, :].rearrange("r (t h) -> r h t", h=HEADS)
            kv_out = kv[to][:, :].rearrange("r (t h) -> r h t", h=HEADS)
            units = [("q", n) for n in range(2)] + [("kv", n) for n in range(4)]
            steps = []
            for n, (kind, i) in enumerate(units):
                b = n % 2
                w = wq if kind == "q" else wkv
                name = f"{tag}{kind}{i}"

                def products(e, k, w=w, i=i, b=b):
                    for j in range(4):
                        mm = e.matmul(pj_ps[b][:, j, :], w[:, 4 * i + j, :], x_at(k), start=True, stop=True)
                    return mm

                bank_of = f"{tag}{units[n - 2][0]}{units[n - 2][1]}out" if n >= 2 else free["bank"][b]
                steps.append((f"{name}mm", "tensor", products, bank_of))
                if kind == "q":
                    def even(e, k, i=i, b=b):
                        return e.tensor_tensor(q_out[:, 8 * i:8 * i + 8:2, :], pj_ps[b][0:HD, :, :],
                                               bq[0:HD, 4 * i:4 * i + 4].unsqueeze(2).to_broadcast([HD, 4, BLK]), ALU.add)

                    def odd(e, k, i=i, b=b):
                        return e.tensor_tensor(q_out[:, 8 * i + 1:8 * i + 8:2, :], pj_ps[b][HD:P, :, :],
                                               bq[HD:P, 4 * i:4 * i + 4].unsqueeze(2).to_broadcast([HD, 4, BLK]), ALU.add)

                    steps.append((f"{name}even", "vector", even, f"{name}mm", *free["q"]))
                    steps.append((f"{name}out", "vector", odd, f"{name}mm"))
                else:
                    def out(e, k, i=i, b=b):
                        for j in range(4):
                            h = 4 * i + j
                            d = e.scalar_tensor_tensor(out=kv_out[:, h, :], in0=pj_ps[b][:, j, :],
                                                       scalar=bkv[:, h:h + 1], in1=pos_at(k), op0=ALU.add, op1=ALU.add)
                        return d

                    steps.append((f"{name}out", "vector", out, f"{name}mm", *free["kv"]))
            groups, at = [], 0
            for kind, _ in units:
                n = 3 if kind == "q" else 2
                groups.append(steps[at:at + n])
                at += n
            return groups

        def tokens(k, off):
            b = (2 * k + off) % (TOKENS // BLK)
            flat = xn[:, :, :].rearrange("p c n -> p (c n)")
            return flat[:, bass.ds((b // TT) * (HALO + CH) + (b % TT) * BLK + HALO, BLK)]

        def codes(k, off):
            b = (2 * k + off) % (LEN // BLK)
            return pos[:, bass.ds(b * BLK, BLK)]

        st = Steps(nc, "pro0", ctx, 1)
        for group in project(st, "x", 0, lambda k: xn[:, 0, HALO:HALO + BLK], lambda k: pos[:, 0:BLK],
                             {"bank": ("-xkv2out", "-xkv3out"), "q": (), "kv": ()}):
            for step in group:
                st.add(*step)
        st.run()

        st = Steps(nc, "ha", ctx, TOKENS // (2 * BLK))

        def past(name, n, depth):
            return f"{name}{n - depth}" if n >= depth else f"-{name}{n - depth + TURNS}"

        def scores(n):
            f, t = n // 4, n % 4
            cut = lambda g: slice((t * GROUPS + g) * P, (t * GROUPS + g + 1) * P)

            def products(e, k):
                for g in range(GROUPS):
                    mm = e.matmul(s_ps[n % 2][:, g, :], q[f][:, cut(g)], kv[f][:, cut(g)], start=True, stop=True)
                return mm

            def turn_v(e, k):
                for g in range(GROUPS):
                    mm = e.transpose(v_ps[:, g, :], kv[f][:, cut(g)], c.ident[:, :])
                return mm

            def mask_max(e, k):
                e.sem_inc(s_pad, 1)
                for g in range(GROUPS):
                    d = e.tensor_tensor_reduce(masked[n % 2][:, g, :], s_ps[n % 2][:, g, :], mask[:, :], 1.0, LOWEST,
                                               ALU.add, ALU.max, top[n % 2][:, g:g + 1])
                return d

            def exps(e, k):
                for g in range(GROUPS):
                    d = e.activation(ex[n % 4][:, g, :], masked[n % 2][:, g, :], ACT.Exp, bias=shift[n % 2][:, g:g + 1],
                                     scale=SCALE, accum_out=total[n % 4][:, g:g + 1])
                return d

            ready = (f"bkv3out",) if f else ("-ckv3out",)
            st.add(f"s{n}", "tensor", products, past("mm", n, 2), *(ready if t == 0 else ()))
            st.add(f"tv{n}", "tensor", turn_v, past("vt", n, 1))
            st.add(f"mm{n}", "vector", mask_max, f"s{n}", past("ex", n, 2))
            st.add(f"shift{n}", "vector", lambda e, k: e.tensor_scalar(
                shift[n % 2][:, :], top[n % 2][:, :], -SCALE, None, ALU.mult), f"mm{n}")
            st.add(f"ex{n}", "scalar", exps, f"shift{n}", past("norm", n, 4), past("rt", n, 4))
            st.add(f"vt{n}", "scalar", lambda e, k: e.activation(
                v_t[n % 4][:, :, :], v_ps[:, :, HD:P], ACT.Copy), f"tv{n}", past("o", n, 4))

        def normalised(n, late):
            st.add(f"rt{n}", "vector", lambda e, k: e.reciprocal(rtotal[n % 4][:, :], total[n % 4][:, :]),
                   f"ex{n}", past("norm", n, 4), late=late)
            st.add(f"norm{n}", "gpsimd", lambda e, k: e.tensor_tensor(
                prob[n % 4][:, :, :], ex[n % 4][:, :, :],
                rtotal[n % 4][:, :].unsqueeze(2).to_broadcast([P, GROUPS, P]), ALU.mult), f"rt{n}", past("tp", n, 4),
                late=late)

        def turned(n, late):
            def turn_p(e, k):
                for g in range(GROUPS):
                    mm = e.transpose(p_ps[:, g, :], prob[n % 4][:, g, :], c.ident[:, :])
                return mm

            st.add(f"tp{n}", "tensor", turn_p, f"norm{n}", past("pt", n, 1), late=late)
            st.add(f"pt{n}", "scalar", lambda e, k: e.activation(
                prob_t[n % 2][:, :, :], p_ps[:, :, :], ACT.Copy), f"tp{n}", past("o", n, 2), late=late)

        def outputs(n, late):
            f, t = n // 4, n % 4

            def products(e, k):
                for g in range(GROUPS):
                    for odd in range(2):
                        mm = e.matmul(o_ps[HD * odd:HD * odd + HD, g, :], v_t[n % 4][:, g, :],
                                      prob_t[n % 2][:, g, odd:P:2], start=True, stop=True, skip_group_check=True)
                return mm

            st.add(f"o{n}", "tensor", products, f"pt{n}", f"vt{n}", past("oc", n, 1), late=late)
            cut = slice(t * GROUPS * G, (t + 1) * GROUPS * G)
            st.add(f"oc{n}", "vector", lambda e, k: e.tensor_copy(
                o[f][:, :, cut].rearrange("r p t -> r t p"),
                o_ps[:, :, :].rearrange("r g (t p) -> r (g t) p", p=PAIRS)), f"o{n}", *((f"-y{f}",) if t == 0 else ()),
                late=late)

        def project_out(f, late):
            def products(e, k):
                for p in range(PAIRS):
                    mm = e.matmul(y_ps[:, :], wo[:, p, :], o[f][:, p, :], start=p == 0, stop=p == PAIRS - 1)
                return mm

            st.add(f"y{f}", "tensor", products, f"oc{4 * f + 3}", f"yc{f - 1}" if f else "-yc1",
                   late=late)
            st.add(f"yc{f}", "scalar", lambda e, k: e.activation(
                c.y[:, bass.ds(k * (2 * BLK) + f * BLK, BLK)], y_ps[:, :], ACT.Copy), f"y{f}", late=late)

        nexts = [project(st, "b", 1, lambda k: tokens(k, 1), lambda k: codes(k, 1),
                         {"bank": ("-ckv2out", "-ckv3out"), "q": ("-s7", "-tv7"), "kv": ("-s7", "-tv7")}),
                 project(st, "c", 0, lambda k: tokens(k, 2), lambda k: codes(k, 2),
                         {"bank": ("bkv2out", "bkv3out"), "q": ("s3", "tv3"), "kv": ("s3", "tv3")})]
        when = {0: (0, 0, 2), 1: (0, 2, 4), 2: (0, 4, 6), 4: (1, 0, 2), 5: (1, 2, 4), 6: (1, 4, 6)}
        for n in range(TURNS):
            scores(n)
            if n in when:
                which, lo, hi = when[n]
                for group in nexts[which][lo:hi]:
                    for step in group:
                        st.add(*step)
            for depth, add in ((1, normalised), (2, turned), (3, outputs)):
                add((n - depth) % TURNS, n < depth)
            if n in (3, 7):
                project_out(1 if n == 3 else 0, n == 3)
        st.run()


class NormBuffers:
    def __init__(self, nc, ctx, tag, bank):
        self.bank = bank
        self.centred, self.squares = (ctx.enter_context(nc.sbuf_tensor(f"{tag}{n}", [P, CH], F32)) for n in ("cen", "sq"))
        self.norm, self.clipped, self.inverse = (
            ctx.enter_context(nc.sbuf_tensor(f"{tag}{n}", [P, TT], F32)) for n in ("norm", "clip", "inv"))


def norm_steps(st, tag, c, b, x, center, eps, out_name, finish, *after, landed=None):
    weights = c.mean if center else c.ones
    sums = b.bank[:, 0:TT]

    def tile(t):
        return slice(t * P, t * P + P)

    if center:
        def mean(e, k):
            if landed:
                landed(e, k)
            return e.matmul(b.bank[:, :], weights[:, :], x(k), start=True, stop=True)

        st.add(f"{tag}mean", "tensor", mean, *after, f"-{out_name}")
        st.add(f"{tag}cen", "vector", lambda e, k: e.tensor_tensor(b.centred[:, :], x(k), b.bank[:, :], ALU.subtract),
               f"{tag}mean")
        src = lambda k: b.centred[:, :]
        last = (f"{tag}cen",)
    else:
        src, last = x, (*after, f"-{out_name}")

    def variance(e, k):
        for t in range(TT):
            mm = e.matmul(sums[:, t:t + 1], b.squares[:, tile(t)], weights[:, 0:1], start=True, stop=True)
        return mm

    def spread(e, k):
        for t in range(TT):
            mm = e.matmul(b.bank[:, tile(t)], b.inverse[:, t:t + 1].to_broadcast([P, P]), c.ident[:, :],
                          start=True, stop=True)
        return mm

    st.add(f"{tag}sq", "scalar", lambda e, k: e.activation(b.squares[:, :], src(k), ACT.Square), *last)
    st.add(f"{tag}var", "tensor", variance, f"{tag}sq")
    if center:
        st.add(f"{tag}sd", "scalar", lambda e, k: e.activation(b.norm[:, :], sums, ACT.Sqrt, bias=eps), f"{tag}var")
        root, ready = b.norm, f"{tag}sd"
    else:
        st.add(f"{tag}sd", "scalar", lambda e, k: e.activation(b.norm[:, :], sums, ACT.Sqrt), f"{tag}var")
        st.add(f"{tag}clip", "vector", lambda e, k: e.tensor_scalar(b.clipped[:, :], b.norm[:, :], eps, None, ALU.max),
               f"{tag}sd")
        root, ready = b.clipped, f"{tag}clip"
    st.add(f"{tag}rs", "vector", lambda e, k: e.reciprocal(b.inverse[:, :], root[:, :]), ready)
    st.add(f"{tag}spread", "tensor", spread, f"{tag}rs")
    st.add(out_name, "vector", lambda e, k: finish(e, k, src(k), b.bank[:, :]), f"{tag}spread")


class Const:
    pass


def two_layers(nc, a, out):
    with ExitStack() as ctx:
        def sb(name, shape, dt=F32, at=ctx):
            return at.enter_context(nc.sbuf_tensor(name, shape, dt))

        c = Const()
        c.ident = sb("ident", [P, P])
        c.diag = sb("diag", [KT, LEN])
        c.ones = sb("ones", [P, P])
        c.mean = sb("mean", [P, P])
        c.y = sb("y", [P, TOKENS])
        x = sb("x", [P, CHUNKS, CH])
        xn = sb("xn", [P, CHUNKS, HALO + CH])
        xr = sb("xr", [P, CHUNKS, CH])
        eps = sb("eps", [P, 1])
        cols = sb("cols", [P, 2 + 4 * HT + 1 + 1])
        mlp_w = {n: sb(f"{n}_w", [P, tiles, n_out])
                 for n, tiles, n_out in (("m1", 1, HID), ("m2", 1, HID), ("h1", HT, HID), ("h2", HT, HID), ("m3", HT, P))}
        s_in = ctx.enter_context(nc.semaphore("s_in"))
        s_in2 = ctx.enter_context(nc.semaphore("s_in2"))
        s_mlp = ctx.enter_context(nc.semaphore("s_mlp"))

        with nc.Block() as block:
            @block.sync
            def _(eng):
                chunks = [(x[:, k, :], a["x"][:, k * CH:k * CH + CH]) for k in range(CHUNKS)]
                for to, of in chunks[:2] + [(c.ident[:, :], a["ident"])]:
                    eng.dma_start(to, of).then_inc(s_in, 16)
                for to, of in chunks[2:] + [(cols[:, :], a["cols"]), (c.diag[:, :], a["diag"])]:
                    eng.dma_start(to, of).then_inc(s_in2, 16)

            @block.gpsimd
            def _(eng):
                eng.memset(c.ones[:, :], 1.0)
                eng.memset(c.mean[:, :], 1.0 / P)
                eng.memset(eps[:, :], LN_EPS)
                eng.memset(xn[:, 0, 0:HALO], 0.0)
                eng.memset(xn[:, HALVES, 0:HALO], 0.0)

        with ExitStack() as moe:
            weights_t = sb("weights_t", [CW, CHUNKS, CH], F32R, moe)
            moe_w = {n: [sb(f"{n}_{part}", [P, size], F32R, moe) for part in ("hi", "lo")] for n, size in MOE_W.items()}
            sel = sb("sel", [CW, (EPAIRS + 1) * P], F32R, moe)
            head_w, s_head = head_weights(nc, moe)
            first_norm(nc, c, a, x, xn, eps, weights_t, moe_w, sel, s_in, s_in2, head_w, s_head)
            head_attention(nc, c, a, xn, head_w, s_head, mlp_w, s_mlp)
            moe_ffn(nc, c, x, xn, xr, eps, cols, weights_t, moe_w, sel)
        c.src = lambda seq: xr[:, bass.ds(seq * HALVES, HALVES), :]
        attention(nc, c, lambda p: a["w1"][bass.ds(p, 1), :, :].rearrange("o k n -> (o k) n"),
                  lambda p: a["wo1"][bass.ds(p, 1), :, :].rearrange("o k n -> (o k) n"))
        mlp_ffn(nc, c, x, xn, cols, out, mlp_w, s_mlp)


def first_norm(nc, c, a, x, xn, eps, weights_t, moe_w, sel, s_in, s_in2, head_w, s_head):
    with ExitStack() as ctx:
        def sb(name, shape, dt=F32):
            return ctx.enter_context(nc.sbuf_tensor(name, shape, dt))

        def ps(name, shape):
            return ctx.enter_context(nc.psum_tensor(name, shape, F32))

        SENT = 8
        raw = {n: sb(f"{n}_raw", [P, size]) for n, size in MOE_W.items()}
        raw["sel"] = sb("sel_raw", [CW, (EPAIRS + 1) * P])
        s_raw = ctx.enter_context(nc.semaphore("s_raw"))
        rw = sb("rw", [P, EXPERTS])
        rb = sb("rb", [P, TT, EXPERTS])
        ALL = TOKENS // P
        lg = sb("lg", [P, ALL, EXPERTS])
        top = sb("top", [P, ALL])
        sh = sb("sh", [P, ALL, EXPERTS])
        ex = sb("ex", [P, ALL, EXPERTS])
        sm = sb("sm", [P, ALL])
        rsm = sb("rsm", [P, ALL])
        pr = sb("pr", [P, ALL, EXPERTS + SENT])
        m8 = sb("m8", [P, ALL, 8])
        rep = sb("rep", [P, ALL, EXPERTS + SENT])
        two = sb("two", [P, ALL])
        rtwo = sb("rtwo", [P, ALL])
        mask = sb("mask", [P, ALL, EXPERTS])
        wt = sb("wt", [P, ALL, EXPERTS])
        cm = sb("cm", [P, ALL, CW])
        t_ps = ps("t_ps", [CW, ALL, P])
        s_l = ctx.enter_context(nc.semaphore("s_l"))
        s_pad = ctx.enter_context(nc.semaphore("s_pad"))
        with nc.Block() as block:
            @block.sync
            def _(eng):
                eng.dma_start(rw[:, :], a["rw"]).then_inc(s_l, 16)
                eng.dma_start(rb[:, :, :], a["rb"].rearrange("p (t n) -> p t n", t=TT)).then_inc(s_l, 16)
                for n, t in raw.items():
                    eng.dma_start(t[:, :], a[n]).then_inc(s_raw, 16)
                for n, t in head_w.items():
                    eng.dma_start(t[:, :], a[n]).then_inc(s_head, 16)

            @block.gpsimd
            def _(eng):
                eng.memset(pr[:, :, EXPERTS:], -2.0)
                eng.memset(cm[:, :, EXPERTS + 1:LO], 0.0)
                eng.memset(cm[:, :, LO + EXPERTS:], 0.0)
                eng.memset(cm[:, :, EXPERTS:EXPERTS + 1], 1.0)

        def wide(v):
            return v[:, :].unsqueeze(2).to_broadcast([P, ALL, EXPERTS])

        def quarter(t, k):
            size = t.shape[1] // CHUNKS
            return t[:, bass.ds(k * size, size)]

        def landed(e, k):
            e.wait_ge(s_in, 16 * 3)
            e.wait_ge(s_in2, 1 + k * (16 * 4))

        def one_chunk(n):
            nb = NormBuffers(nc, ctx, f"n0{n}", ps(f"n_ps{n}", [P, CH]))
            cur = sb(f"cur{n}", [P, CH])
            r_ps = ps(f"r_ps{n}", [P, TT, EXPERTS])
            steps = Recorded()

            def at(t, k, cut=slice(None)):
                return t[:, bass.ds(2 * k + n, 1), cut].rearrange("p o n -> p (o n)")

            def logits(e, k):
                e.wait_ge(s_l, 32)
                for t in range(TT):
                    mm = e.matmul(r_ps[:, t, :], cur[:, t * P:t * P + P], rw[:, :], start=True, stop=True)
                return mm

            def weights_hi(e, k):
                e.wait_ge(s_raw, 16 * len(raw))
                e.tensor_copy(quarter(sel, 2 * k + n), quarter(raw["sel"], 2 * k + n))
                for name, (hi, _) in moe_w.items():
                    i = e.tensor_copy(quarter(hi, 2 * k + n), quarter(raw[name], 2 * k + n))
                return i

            def weights_lo(e, k):
                for name, (hi, lo) in moe_w.items():
                    i = e.tensor_tensor(quarter(lo, 2 * k + n), quarter(raw[name], 2 * k + n),
                                        quarter(hi, 2 * k + n).bitcast(F32), ALU.subtract)
                return i

            norm_steps(steps, f"n0{n}", c, nb, lambda k: at(x, k), True, eps[:, :], f"cur{n}",
                       lambda e, k, cen, rs: e.tensor_tensor(cur[:, :], cen, rs, ALU.mult), f"-logits{n}", f"-keep{n}",
                       landed=landed)
            steps.add(f"logits{n}", "tensor", logits, f"cur{n}", f"-lg{n}")
            steps.add(f"keep{n}", "scalar", lambda e, k: e.activation(
                at(xn, k, slice(HALO, HALO + CH)), cur[:, :], ACT.Copy), f"cur{n}")
            steps.add(f"lg{n}", "vector", lambda e, k: e.tensor_tensor(
                lg[:, bass.ds((2 * k + n) * TT, TT), :], r_ps[:, :, :], rb[:, :, :], ALU.add), f"logits{n}")
            steps.add(f"w_hi{n}", "gpsimd", weights_hi)
            steps.add(f"w_lo{n}", "gpsimd", weights_lo, f"w_hi{n}")
            return steps.list

        st = Steps(nc, "fn", ctx, CHUNKS // 2)
        for steps in zip(one_chunk(0), one_chunk(1)):
            for step in steps:
                st.add(*step)
        st.run(before={"tensor": lambda e: e.sem_inc(s_in2, 1)})

        def each(f):
            def emit(e, k):
                e.sem_inc(s_pad, 1)
                for t in range(ALL):
                    i = f(e, t)
                return i
            return emit

        E = slice(0, EXPERTS)
        router = Steps(nc, "router", ctx, 1)
        router.add("top", "vector", lambda e, k: e.reduce_max(top[:, :], lg[:, :, :], AX_X))
        router.add("sh", "vector", lambda e, k: e.tensor_tensor(sh[:, :, :], lg[:, :, :], wide(top), ALU.subtract),
               "top")
        router.add("ex", "scalar", lambda e, k: e.activation(ex[:, :, :], sh[:, :, :], ACT.Exp), "sh")
        router.add("sm", "vector", lambda e, k: e.reduce_sum(sm[:, :], ex[:, :, :], AX_X), "ex")
        router.add("rsm", "vector", lambda e, k: e.reciprocal(rsm[:, :], sm[:, :]), "sm")
        router.add("pr", "vector", lambda e, k: e.tensor_tensor(pr[:, :, E], ex[:, :, :], wide(rsm), ALU.mult),
               "rsm")
        router.add("m8", "vector", each(lambda e, t: e.max(m8[:, t, :], pr[:, t, E])), "pr")
        router.add("m8b", "vector", lambda e, k: e.memset(m8[:, :, 2:8], -2.0), "m8")
        router.add("rep", "vector", each(lambda e, t: e.match_replace(rep[:, t, :], m8[:, t, :], pr[:, t, :], -1.0)),
               "m8b")
        router.add("two", "vector", lambda e, k: e.reduce_sum(two[:, :], m8[:, :, 0:2], AX_X), "m8b")
        router.add("rtwo0", "vector", lambda e, k: e.tensor_scalar(top[:, :], two[:, :], 1e-6, None, ALU.add), "two", "sh")
        router.add("rtwo", "vector", lambda e, k: e.reciprocal(rtwo[:, :], top[:, :]), "rtwo0")
        router.add("mask", "vector", lambda e, k: e.tensor_scalar(mask[:, :, :], rep[:, :, E], 0.0, None, ALU.is_lt),
               "rep")
        router.add("wt", "vector", lambda e, k: e.tensor_tensor(wt[:, :, :], mask[:, :, :], pr[:, :, E], ALU.mult),
               "mask")
        router.add("cmw", "vector", lambda e, k: e.tensor_tensor(ex[:, :, :], wt[:, :, :], wide(rtwo), ALU.mult),
               "wt", "rtwo", "pr")
        router.add("hi", "vector", lambda e, k: e.tensor_copy(cm[:, :, E].bitcast(F32R), ex[:, :, :]), "cmw")
        router.add("lo", "vector", lambda e, k: e.tensor_tensor(cm[:, :, LO:LO + EXPERTS].bitcast(F32R), ex[:, :, :],
                                                            cm[:, :, E], ALU.subtract), "hi")

        for n in range(CHUNKS):
            tiles = range(n * TT, n * TT + TT)

            def turn(e, k, tiles=tiles):
                for t in tiles:
                    mm = e.transpose(t_ps[:, t, :], cm[:, t, :], c.ident[:, :])
                return mm

            router.add(f"turn{n}", "tensor", turn, "lo")
            router.add(f"keep_w{n}", "vector", lambda e, k, n=n: e.tensor_copy(
                weights_t[:, n, :], t_ps[:, n * TT:n * TT + TT, :].rearrange("p t n -> p (t n)")), f"turn{n}")
        router.add("halo", "gpsimd", lambda e, k: e.tensor_copy(
            xn[:, 1:CHUNKS:HALVES, 0:HALO], xn[:, 0:CHUNKS:HALVES, CH:CH + HALO]))
        router.run()


def moe_ffn(nc, c, x, xn, xr, eps, cols, weights_t, moe_w, sel):
    with ExitStack() as ctx:
        def sb(name, shape, dt=F32):
            return ctx.enter_context(nc.sbuf_tensor(name, shape, dt))

        def ps(name):
            return ctx.enter_context(nc.psum_tensor(name, [P, CH], F32))

        gcol = sb("gcol", [P, 1])
        g_ps, u_ps, w_ps = ([ps(f"{n}{i}") for i in range(2)] for n in ("g_ps", "u_ps", "w_ps"))
        y_ps, n_ps = ps("y_ps"), ps("n_ps")
        x_hl = [sb(f"xm_{part}", [P, 2, HALO + CH], F32R) for part in ("hi", "lo")]
        sg, su = ([sb(f"{n}{i}", [P, CH]) for i in range(2)] for n in ("sg", "su"))
        RING = 4
        h = [sb(f"h{i}", [P, CH]) for i in range(RING)]
        h_hl = [[sb(f"h{i}{part}", [P, CH], F32R) for part in ("hi", "lo")] for i in range(RING)]
        own, gate, res = sb("own", [P, CH]), sb("gate", [P, CH]), sb("res", [P, CH])
        s_x0 = ctx.enter_context(nc.semaphore("s_x0"))
        nb, rb = (NormBuffers(nc, ctx, tag, n_ps) for tag in ("n1", "r1"))

        def flat(t, k, cut=slice(None)):
            return t[:, bass.ds(k, 1), cut].rearrange("p o n -> p (o n)")

        def products(eng, to, w, tiles, vs, first, last):
            passes = []
            for tile, v in zip(tiles, vs):
                hi, lo = (moe_w[w][part][:, tile * P:tile * P + P] for part in range(2))
                passes += [(hi, v[0]), (lo, v[0]), (hi, v[1])]
            for i, (weight, v) in enumerate(passes):
                mm = eng.matmul(to[:, :], weight, v, start=first and i == 0, stop=last and i == len(passes) - 1)
            return mm

        def token_parts(k, cut):
            return [flat(t, k % 2, cut) for t in x_hl]

        def next_hi(eng, k):
            return eng.activation(flat(x_hl[0], k % 2), flat(xn, k), ACT.Copy)

        def next_lo(eng, k):
            return eng.tensor_tensor(flat(x_hl[1], k % 2), flat(xn, k), flat(x_hl[0], k % 2).bitcast(F32), ALU.subtract)

        now = slice(HALO, HALO + CH)
        st = Steps(nc, "moe", ctx)
        norms = Recorded()
        norms.add("sum", "vector", lambda eng, k: eng.tensor_tensor(res[:, :], own[:, :], y_ps[:, :], ALU.add),
               "own", f"y{EPAIRS - 1}", "-gate")
        norms.add("gate", "scalar", lambda eng, k: eng.activation(gate[:, :], res[:, :], ACT.Silu), "sum", "-gated")
        norms.add("gated", "vector", lambda eng, k: eng.scalar_tensor_tensor(
            out=own[:, :], in0=c.y[:, bass.ds(k * CH, CH)], scalar=cols[:, 0:1], in1=gate[:, :],
            op0=ALU.add, op1=ALU.mult), "gate", "sum")
        norms.add("xnew", "vector", lambda eng, k: eng.tensor_tensor(flat(x, k), flat(x, k), own[:, :], ALU.add),
               "gated")
        norm_steps(norms, "n1", c, nb, lambda k: flat(x, k), True, eps[:, :], "xn1",
                   lambda e, k, cen, rs: e.tensor_tensor(flat(xn, k, now), cen, rs, ALU.mult),
                   "xnew", f"u{EPAIRS - 1}", f"g{EPAIRS - 1}", "own", "-xr1")
        norm_steps(norms, "r1", c, rb, lambda k: flat(xn, k, now), False, RMS_EPS, "xr1",
                   lambda e, k, v, rs: e.scalar_tensor_tensor(out=flat(xr, k), in0=v, scalar=gcol[:, :], in1=rs,
                                                              op0=ALU.mult, op1=ALU.mult), "xn1")
        LAG = 2
        for e in range(EPAIRS):
            b = e % 2

            def gates(eng, k, e=e, b=b):
                if e < EPAIRS - 1:
                    return products(eng, g_ps[b], "wg", [e], [token_parts(k, now)], True, True)
                products(eng, g_ps[b], "wg", [e], [token_parts(k, now)], True, False)
                return products(eng, g_ps[b], "wc", range(HALO),
                                [token_parts(k, slice(t, t + CH)) for t in range(HALO)], False, True)

            old = "" if e >= 2 else "-"
            o = (e - 2) % EPAIRS
            st.add(f"g{e}", "tensor", gates, f"{old}sg{o}", "-x_lo")
            st.add(f"u{e}", "tensor", lambda eng, k, e=e, b=b: products(
                eng, u_ps[b], "wu", [e], [token_parts(k, now)], True, True), f"{old}su{o}")
            st.add(f"w{e}", "tensor", lambda eng, k, e=e, b=b: eng.matmul(
                w_ps[b][:, :], sel[:, e * P:e * P + P], flat(weights_t, k), start=True, stop=True),
                f"{old}h{o}", *(("-own",) if e == 0 else ()))
            st.add(f"sg{e}", "scalar", lambda eng, k, b=b: eng.activation(sg[b][:, :], g_ps[b][:, :], ACT.Silu),
                   f"g{e}", f"{old}su{o}")
            st.add(f"su{e}", "vector", lambda eng, k, b=b: eng.tensor_tensor(
                su[b][:, :], sg[b][:, :], u_ps[b][:, :], ALU.mult), f"sg{e}", f"u{e}", f"{old}h{o}")
            ring = e % RING
            was = f"{'' if e >= RING else '-'}{{}}{(e - RING) % EPAIRS}"
            st.add(f"h{e}", "vector", lambda eng, k, b=b, ring=ring: eng.tensor_tensor(
                h[ring][:, :], su[b][:, :], w_ps[b][:, :], ALU.mult), f"su{e}", f"w{e}", was.format("h_lo"))
            hidden_parts(st, (e - 1) % EPAIRS, h, h_hl, e < 1)
            expert_out(st, (e - LAG) % EPAIRS, products, y_ps, h_hl, e < LAG)
            if e == 2:
                st.add("x_hi", "scalar", lambda eng, k: next_hi(eng, (k + 1) % CHUNKS), f"-g{EPAIRS - 1}", f"-u{EPAIRS - 1}")
                st.add("x_lo", "gpsimd", lambda eng, k: next_lo(eng, (k + 1) % CHUNKS), "x_hi")
            norms.take(st, MOE_LATE[e])
        st.add("w8", "tensor", lambda eng, k: eng.matmul(
            w_ps[0][:, :], sel[:, EPAIRS * P:], flat(weights_t, k), start=True, stop=True), f"h{EPAIRS - 2}")
        st.add("own", "vector", lambda eng, k: eng.tensor_tensor(own[:, :], flat(xn, k, now), w_ps[0][:, :], ALU.mult),
               "w8", "-sum")
        def first_hi(eng):
            next_hi(eng, 0).then_inc(s_x0, 1)

        def first_lo(eng):
            eng.tensor_scalar(gcol[:, :], cols[:, 1:2], 1.0, float(P) ** 0.5, ALU.add, ALU.mult)
            eng.wait_ge(s_x0, 1)
            next_lo(eng, 0).then_inc(s_x0, 1)

        st.run(before={"scalar": first_hi, "vector": first_lo, "tensor": lambda eng: eng.wait_ge(s_x0, 2)})


def hidden_parts(st, e, h, h_hl, late):
    ring = e % len(h)
    used = f"{'' if e >= len(h) else '-'}y{(e - len(h)) % EPAIRS}"
    hi, lo = h_hl[ring]
    st.add(f"h_hi{e}", "scalar", lambda eng, k: eng.activation(hi[:, :], h[ring][:, :], ACT.Copy),
           f"h{e}", used, late=late)
    st.add(f"h_lo{e}", "gpsimd", lambda eng, k: eng.tensor_tensor(
        lo[:, :], h[ring][:, :], hi[:, :].bitcast(F32), ALU.subtract), f"h_hi{e}", used, late=late)


def expert_out(st, e, products, y_ps, h_hl, late):
    st.add(f"y{e}", "tensor", lambda eng, k: products(
        eng, y_ps, "wd", [e], [[t[:, :] for t in h_hl[e % len(h_hl)]]], e == 0, e == EPAIRS - 1),
        f"h_lo{e}", *(("-sum",) if e == 0 else ()), late=late)


def mlp_ffn(nc, c, x, xn, cols, out, raw, s_mlp):
    with ExitStack() as ctx:
        def sb(name, shape, dt=F32):
            return ctx.enter_context(nc.sbuf_tensor(name, shape, dt))

        w_hi = {n: sb(f"{n}_hi", list(t.shape), F32R) for n, t in raw.items()}
        w_lo = {n: sb(f"{n}_lo", list(t.shape), F32R) for n, t in raw.items()}
        x_hl = [sb(f"x_hl{i}", [P, CH], F32R) for i in range(2)]
        act = [[[sb(f"act{i}{m}{part}", [P, CH], F32R) for part in ("hi", "lo")] for m in range(HT)]
               for i in range(3)]
        RING = 3
        whole = [sb(f"whole{i}", [P, CH]) for i in range(RING)]
        sg = [sb(f"sgm{i}", [P, CH]) for i in range(2)]
        gate, res, fin = sb("gate_m", [P, CH]), sb("res_m", [P, CH]), sb("fin", [P, CH])
        BANKS = 7
        bank = [ctx.enter_context(nc.psum_tensor(f"bank{i}", [P, CH], F32)) for i in range(BANKS + 1)]
        s_hi_w = ctx.enter_context(nc.semaphore("s_hi_w"))
        s_lo_w = ctx.enter_context(nc.semaphore("s_lo_w"))

        tiles = [(n, t) for n in raw for t in range(raw[n].shape[1])]
        split_by = {n: max(i for i, (of, _) in enumerate(tiles) if of == n) + 1 for n in raw}

        def weights_hi(eng):
            eng.wait_ge(s_mlp, 16 * len(raw))
            for n, t in tiles:
                eng.activation(w_hi[n][:, t, :], raw[n][:, t, :], ACT.Copy).then_inc(s_hi_w, 1)

        def weights_lo(eng):
            for i, (n, t) in enumerate(tiles):
                eng.wait_ge(s_hi_w, i + 1)
                eng.tensor_tensor(w_lo[n][:, t, :], raw[n][:, t, :], w_hi[n][:, t, :].bitcast(F32),
                                  ALU.subtract).then_inc(s_lo_w, 1)

        def product(e, ps, n, t, cut, hl, first, last):
            passes = [(w_hi[n][:, t, cut], hl[0]), (w_lo[n][:, t, cut], hl[0]), (w_hi[n][:, t, cut], hl[1])]
            for i, (w, v) in enumerate(passes):
                mm = e.matmul(ps[:, :], w, v[:, :], start=first and i == 0, stop=last and i == 2)
            return mm

        def col(n, m):
            return cols[:, 2 + n * HT + m:3 + n * HT + m]

        def cut(m):
            return slice(m * P, m * P + P)

        st = Steps(nc, "mlp", ctx)

        readers = [f"{kind}{m}" for m in range(HT) for kind in ("s", "t")]
        readers += [f"a{i}{m}" for i in (1, 2) for m in range(HT)]
        final = {n % BANKS: name for n, name in enumerate(readers)}

        def take(reader):
            n = readers.index(reader)
            return bank[n % BANKS], readers[n - BANKS] if n >= BANKS else f"-{final[n % BANKS]}"

        made = [f"t{m}" for m in range(HT)] + [f"a{i}{m}" for i in (1, 2) for m in range(HT)]

        def ring(name):
            n = made.index(name)
            free = f"lo_{made[n - RING]}" if n >= RING else f"-lo_{made[n - RING]}"
            return whole[n % RING], free

        def split(name, i, m):
            src, last_use = ring(name)[0], f"-r3{m}" if i == 2 else f"-r{i + 1}{HT - 1}{m}"
            hi, lo = act[i][m]
            if i == 0:
                st.add(f"hi_{name}", "scalar", lambda e, k: e.activation(hi[:, :], src[:, :], ACT.Copy), name, last_use)
            else:
                st.add(f"hi_{name}", "vector", lambda e, k: e.tensor_copy(hi[:, :], src[:, :]), name, last_use)
            st.add(f"lo_{name}", "vector", lambda e, k: e.tensor_tensor(
                lo[:, :], src[:, :], hi[:, :].bitcast(F32), ALU.subtract), f"hi_{name}")

        def xc(k):
            return xn[:, bass.ds(k, 1), HALO:].rearrange("p o n -> p (o n)")

        st.add("x_hi", "vector", lambda e, k: e.tensor_copy(x_hl[0][:, :], xc(k)), f"-q{HT - 1}")
        st.add("x_lo", "vector", lambda e, k: e.tensor_tensor(
            x_hl[1][:, :], xc(k), x_hl[0][:, :].bitcast(F32), ALU.subtract), "x_hi")

        for j in range(HT):
            def last_layer(e, k, j=j):
                if j == 0:
                    e.wait_ge(s_lo_w, split_by["m3"])
                return product(e, bank[BANKS], "m3", j, slice(0, P), act[2][j], j == 0, j == HT - 1)

            st.add(f"r3{j}", "tensor", last_layer, f"lo_a2{j}", "-gate", late=True)
        st.add("gate", "scalar", lambda e, k: e.activation(gate[:, :], bank[BANKS][:, :], ACT.Silu, scale=col(4, 0)),
               f"r3{HT - 1}", "-mul", late=True)
        st.add("mul", "vector", lambda e, k: e.tensor_tensor(res[:, :], c.y[:, bass.ds(k * CH, CH)], gate[:, :], ALU.mult),
               "gate", "-fin", late=True)
        st.add("fin", "vector", lambda e, k: e.tensor_tensor(
            fin[:, :], x[:, bass.ds(k, 1), :].rearrange("p o n -> p (o n)"), res[:, :], ALU.add), "mul", "-store", late=True)
        st.add("store", "sync", lambda e, k: e.dma_start(out[:, bass.ds(k * CH, CH)], fin[:, :]), "fin", late=True)

        for m in range(HT):
            for name, w, reader in (("p", "m1", f"s{m}"), ("q", "m2", f"t{m}")):
                ps, free = take(reader)

                def first_layer(e, k, w=w, m=m, ps=ps):
                    if m == 0:
                        e.wait_ge(s_lo_w, split_by[w])
                    return product(e, ps, w, 0, cut(m), x_hl, True, True)

                st.add(f"{name}{m}", "tensor", first_layer, "x_lo", free)
            pa, pb = take(f"s{m}")[0], take(f"t{m}")[0]
            old = f"t{m - 2}" if m >= 2 else f"-t{m + 2}"
            st.add(f"s{m}", "scalar", lambda e, k, m=m, pa=pa: e.activation(
                sg[m % 2][:, :], pa[:, :], ACT.Silu, scale=col(0, m)), f"p{m}", old)
            to, free = ring(f"t{m}")
            st.add(f"t{m}", "vector", lambda e, k, m=m, pb=pb, to=to: e.scalar_tensor_tensor(
                out=to[:, :], in0=pb[:, :], scalar=col(1, m), in1=sg[m % 2][:, :],
                op0=ALU.mult, op1=ALU.mult), f"s{m}", f"q{m}", free)
            if m:
                split(f"t{m - 1}", 0, m - 1)
        split(f"t{HT - 1}", 0, HT - 1)
        for i, w in ((1, "h1"), (2, "h2")):
            for m in range(HT):
                name = f"a{i}{m}"
                ps, bank_free = take(name)
                to, ring_free = ring(name)
                for j in range(HT):
                    def layer(e, k, i=i, w=w, m=m, j=j, ps=ps):
                        if m == 0 and j == 0:
                            e.wait_ge(s_lo_w, split_by[w])
                        return product(e, ps, w, j, cut(m), act[i - 1][j], j == 0, j == HT - 1)

                    st.add(f"r{i}{m}{j}", "tensor", layer, bank_free, f"lo_t{j}" if i == 1 else f"lo_a1{j}")
                st.add(name, "scalar", lambda e, k, i=i, m=m, ps=ps, to=to: e.activation(
                    to[:, :], ps[:, :], ACT.Gelu, scale=col(1 + i, m)), f"r{i}{m}{HT - 1}", ring_free)
                split(name, i, m)
        st.run(before={"scalar": weights_hi, "vector": weights_lo})


def kernel(**inputs):
    import numpy as np
    import concourse.bacc as bacc
    from concourse.bass_utils import run_bass_kernel_spmd

    i = {k: np.asarray(v) for k, v in inputs.items()}
    f = np.float32
    a = {"x": i["L0_attn_x"].reshape(TOKENS, P).T}

    w = i["L0_attn_w_qkv"].reshape(P, HEADS, 3, HD)
    b = i["L0_attn_b_qkv"].reshape(HEADS, 3, HD)
    a["wq0"] = w[:, :, 0].reshape(P, -1)
    a["wkv0"] = w[:, :, 1:].reshape(P, -1)
    a["bq0"] = b[:, 0].reshape(PAIRS, P).T
    a["bkv0"] = b[:, 1:].reshape(HEADS, P).T
    a["wo0"] = i["L0_attn_w_out"].reshape(PAIRS, P, P).transpose(1, 0, 2).reshape(P, -1)

    w = i["L1_attn_w_qkv"].reshape(P, 3, HEADS, HD)
    a["w1"] = np.zeros((PAIRS, P, W_V), f)
    for p in range(PAIRS):
        for n in range(2):
            for h in range(2):
                at = n * P + h * HD
                a["w1"][p, :, at:at + HD] = w[:, n, 2 * p + h]
        a["w1"][p, :, W_QK:] = w[:, 2, 2 * p:2 * p + 2].reshape(P, P)
    a["wo1"] = i["L1_attn_w_out"].reshape(PAIRS, P, P)

    a["rw"] = i["L0_ffn_router_w"]
    a["rb"] = np.tile(i["L0_ffn_router_bias"], (P, TT))
    conv = i["L0_ffn_conv_w"]
    for n, name, shared in (("wg", "gate", conv[:, :, HALO].T), ("wu", "up", i["L0_ffn_shared_up_w"])):
        each = list(i[f"L0_ffn_expert_{name}_w"]) + [shared]
        a[n] = np.concatenate(each, axis=1)
    down = list(i["L0_ffn_expert_down_w"]) + [i["L0_ffn_shared_down_w"]]
    a["wd"] = np.concatenate([np.concatenate(down[2 * e:2 * e + 2], axis=0) for e in range(EPAIRS)], axis=1)
    a["wc"] = np.zeros((P, HALO * P), f)
    for t in range(HALO):
        a["wc"][:, t * P + HD:(t + 1) * P] = conv[:, :, t].T
    cols = [i["L0_attn_b_out"][:, None], i["L1_attn_gamma"][:, None]]
    for n in ("w1", "w2", "h1", "h2"):
        cols.append(i[f"L1_ffn_{n}_s"].reshape(HT, P).T)
    cols += [i["L1_ffn_w3_s"][:, None], np.zeros((P, 1), f)]
    a["cols"] = np.concatenate(cols, axis=1)
    a["m1"], a["m2"] = i["L1_ffn_w1_w"].T, i["L1_ffn_w2_w"].T
    for n, name in (("h1", "h1"), ("h2", "h2"), ("m3", "w3")):
        t = i[f"L1_ffn_{name}_w"].T
        a[n] = t.reshape(HT, P, -1).transpose(1, 0, 2).reshape(P, -1)

    a["ident"] = np.eye(P, dtype=f)
    a["diag"] = np.repeat(np.eye(KT, dtype=f), P, axis=1)
    sel = np.zeros((CW, EPAIRS + 1, P), f)
    for e in range(EXPERTS):
        rows = [e, LO + e] if e < EXPERTS - 1 else [EXPERTS]
        sel[rows, e // 2, (e % 2) * HD:(e % 2 + 1) * HD] = 1.0
    sel[[EXPERTS - 1, LO + EXPERTS - 1], EPAIRS, :] = 1.0
    a["sel"] = sel.reshape(CW, -1)
    steps = np.exp(np.arange(0, HD, 2, dtype=f) * f(-(np.log(10000.0) / HD)))
    angle = np.arange(LEN, dtype=f)[:, None] * steps
    pos = np.zeros((LEN, HD), f)
    pos[:, 0::2], pos[:, 1::2] = np.sin(angle), np.cos(angle)
    a["pos"] = np.zeros((P, LEN), f)
    a["pos"][0:HD] = pos.T
    tokens = np.arange(P) // HEADS
    a["mask"] = np.where(tokens[:, None] == tokens, 0.0, LOWEST).astype(f)

    nc = bacc.Bacc("TRN2", target_bir_lowering=False, num_devices=1)
    arrays, args = {}, {}
    for n, v in a.items():
        v = np.ascontiguousarray(v)
        arrays[f"in_{n}"] = v
        args[n] = nc.dram_tensor(f"in_{n}", v.shape, mybir.dt.from_np(v.dtype), kind="ExternalInput").ap()
    out = nc.dram_tensor("out", (P, TOKENS), F32, kind="ExternalOutput").ap()
    two_layers(nc, args, out)
    r = run_bass_kernel_spmd(nc, [arrays], core_ids=[0])
    return r.results[0]["out"].T.reshape(SEQS, LEN, P)
```
